# Optimizing a Trainium2 kernel written in Bass

```python
import numpy as np
import jax
import jax.numpy as jnp

def _softmax(x, axis=-1):
    return jax.nn.softmax(x, axis=axis)

def _gelu(x):
    return jax.nn.gelu(x, approximate=True)

def _silu(x):
    return jax.nn.silu(x)

def _sigmoid(x):
    return jax.nn.sigmoid(x)

def _layernorm(x, axis=-1, eps=1e-05):
    m = jnp.mean(x, axis=axis, keepdims=True)
    v = jnp.var(x, axis=axis, keepdims=True)
    return (x - m) / jnp.sqrt(v + eps)

def _scatter_add(tgt, idx, src, axis=0):
    return tgt.at[idx].add(src)

def _segment_sum(src, seg, n):
    return jax.ops.segment_sum(src, seg, n)
kernel_name = 'mk_gnn_resnorm_d4_gnn_r32_5799cf'

def setup_inputs(seed: int=0):
    np.random.seed(seed)
    _w = jnp.asarray

    def _rec_inputs():
        import jax
        import jax.numpy as jnp
        _gk = jax.random.key(seed)
        x = -9.915e-05 + 0.125 * jax.random.normal(jax.random.fold_in(_gk, 1), (3125, 64), jnp.float32)
        src = jax.random.randint(jax.random.fold_in(_gk, 2), (100000,), 0, 3125, jnp.int32)
        dst = jnp.minimum((3125 * jax.random.uniform(jax.random.fold_in(_gk, 3), (100000,)) ** 2.0).astype(jnp.int32), 99999)
        _o = jnp.argsort(dst, stable=True)
        src = src[_o]
        dst = dst[_o]
        edge_type_12 = jax.random.randint(jax.random.fold_in(_gk, 14), (100000,), 0, 12, jnp.int32)
        node_vec1 = jax.random.uniform(jax.random.fold_in(_gk, 15), (3125, 1), jnp.float32, 0.0, 0.999993)
        return (x, src, dst, edge_type_12, node_vec1)
    x, src, dst, edge_type_12, node_vec1 = _rec_inputs()

    def _L0_gnn_setup():
        import jax, jax.numpy as jnp
        import numpy as np
        import math
        NUM_NODES = 30471
        EMBED = 64
        NUM_REL = 12
        NUM_BASES = 30
        NUM_EDGES = 62500
        key = jax.random.key(seed)
        k1, k2, k3, k4, k5, k6, k7 = jax.random.split(key, 7)
        bound = 1.0 / math.sqrt(EMBED)
        feats = jax.random.uniform(k1, (NUM_NODES, EMBED), minval=-bound, maxval=bound, dtype=jnp.float32)
        x = feats / jnp.maximum(jnp.linalg.norm(feats, axis=1, keepdims=True), 1e-12)
        basis = jax.random.normal(k2, (NUM_BASES, EMBED, EMBED), dtype=jnp.float32) * (1.0 / math.sqrt(EMBED))
        comp = jax.random.normal(k3, (NUM_REL, NUM_BASES), dtype=jnp.float32) * (1.0 / math.sqrt(NUM_BASES))
        root = jax.random.normal(k4, (EMBED, EMBED), dtype=jnp.float32) * (1.0 / math.sqrt(EMBED))
        bias = jnp.zeros((EMBED,), dtype=jnp.float32)
        edge_type = jax.random.randint(k5, (NUM_EDGES,), 0, NUM_REL, dtype=jnp.int64)
        edge_index = jax.random.randint(k6, (2, NUM_EDGES), 0, NUM_NODES, dtype=jnp.int64)
        return {'edge_type': edge_type, 'edge_index': edge_index, 'x': x, 'basis': basis, 'comp': comp, 'root': root, 'bias': bias}
    _L0_gnn_all = _L0_gnn_setup()
    _L0_gnn_in = {k: v for k, v in _L0_gnn_all.items() if k in ('basis', 'comp', 'root', 'bias')}
    del _L0_gnn_all

    def _L1_gnn_setup():
        import jax, jax.numpy as jnp
        import numpy as np
        N = 50000
        E = 25000
        C = 64
        H = 64
        EPS = 1e-05

        def _bn(h, gamma, beta):
            m = h.mean(axis=0)
            v = ((h - m) ** 2).mean(axis=0)
            return (h - m) * jax.lax.rsqrt(v + EPS) * gamma + beta
        key = jax.random.key(seed)
        ks = jax.random.split(key, 8)

        def glorot(k, shape):
            return jax.random.normal(k, shape, dtype=jnp.float32) / jnp.sqrt(jnp.float32(shape[0]))
        x = jax.random.normal(ks[0], (N, C), dtype=jnp.float32)
        edge_index = jax.random.randint(ks[1], (2, E), 0, N)
        return {'x': x, 'edge_index': edge_index, 'W_unite': glorot(ks[2], (2 * C, H)), 'b_unite': jnp.zeros((H,), jnp.float32), 'g1': jnp.ones((H,), jnp.float32), 'be1': jnp.zeros((H,), jnp.float32), 'W_gconv': glorot(ks[3], (2 * H, H)), 'b_gconv': jnp.zeros((H,), jnp.float32), 'g2': jnp.ones((H,), jnp.float32), 'be2': jnp.zeros((H,), jnp.float32), 'W_transfer': glorot(ks[4], (2 * H, H)), 'b_transfer': jnp.zeros((H,), jnp.float32), 'W_lin': glorot(ks[5], (H, H)), 'b_lin': jnp.zeros((H,), jnp.float32), 'g3': jnp.ones((H,), jnp.float32), 'be3': jnp.zeros((H,), jnp.float32)}
    _L1_gnn_all = _L1_gnn_setup()
    _L1_gnn_in = {k: v for k, v in _L1_gnn_all.items() if k in ('W_unite', 'b_unite', 'g1', 'be1', 'W_gconv', 'b_gconv', 'g2', 'be2', 'W_transfer', 'b_transfer', 'W_lin', 'b_lin', 'g3', 'be3')}
    del _L1_gnn_all

    def _L2_gnn_setup():
        import jax, jax.numpy as jnp
        import numpy as np
        EPS = 1e-05

        def _bn(x):
            mu = jnp.mean(x, axis=0, keepdims=True)
            var = jnp.var(x, axis=0, keepdims=True)
            return (x - mu) * jax.lax.rsqrt(var + EPS)

        def _conv(x, src, tgt, norm, W):
            n = x.shape[0]
            agg = x + jax.ops.segment_sum(x[src], tgt, num_segments=n)
            return norm * agg @ W

        def _biconv(x, src, tgt, norm, norm_t, W_out, W_back):
            return _conv(x, src, tgt, norm, W_out) + _conv(x, tgt, src, norm_t, W_back)
        key = jax.random.key(seed)
        ks = jax.random.split(key, 9)
        N, E, C = (3125, 1250000, 64)
        x = jax.random.normal(ks[0], (N, C), dtype=jnp.float32)
        sources = jax.random.randint(ks[1], (E,), 0, N)
        targets = jax.random.randint(ks[2], (E,), 0, N)
        norm = jax.random.uniform(ks[3], (N, 1), dtype=jnp.float32)
        norm_t = jax.random.uniform(ks[4], (N, 1), dtype=jnp.float32)
        std = float(np.sqrt(2.0 / (C + C)))
        W1_out = jax.random.normal(ks[5], (C, C), dtype=jnp.float32) * std
        W1_back = jax.random.normal(ks[6], (C, C), dtype=jnp.float32) * std
        W2_out = jax.random.normal(ks[7], (C, C), dtype=jnp.float32) * std
        W2_back = jax.random.normal(ks[8], (C, C), dtype=jnp.float32) * std
        return {'x': x, 'sources': sources, 'targets': targets, 'norm': norm, 'norm_t': norm_t, 'W1_out': W1_out, 'W1_back': W1_back, 'W2_out': W2_out, 'W2_back': W2_back}
    _L2_gnn_all = _L2_gnn_setup()
    _L2_gnn_in = {k: v for k, v in _L2_gnn_all.items() if k in ('W1_out', 'W1_back', 'W2_out', 'W2_back')}
    del _L2_gnn_all

    def _L3_gnn_setup():
        import jax, jax.numpy as jnp
        import numpy as np
        NUM_NODES = 31250
        EMBED_DIM = 64
        HIDDEN_DIM = 128
        key = jax.random.key(seed)
        k_e, k_emb, k_w1, k_b1, k_w2, k_b2 = jax.random.split(key, 6)
        edge_index = jax.random.randint(k_e, (2, 1250000), 0, NUM_NODES, dtype=jnp.int64)
        emb = jax.random.normal(k_emb, (NUM_NODES, EMBED_DIM), dtype=jnp.float32)
        w1 = jax.random.normal(k_w1, (HIDDEN_DIM, EMBED_DIM), dtype=jnp.float32) * (1.0 / np.sqrt(EMBED_DIM))
        b1 = jax.random.normal(k_b1, (HIDDEN_DIM,), dtype=jnp.float32) * 0.01
        w2 = jax.random.normal(k_w2, (EMBED_DIM, HIDDEN_DIM), dtype=jnp.float32) * (1.0 / np.sqrt(HIDDEN_DIM))
        b2 = jax.random.normal(k_b2, (EMBED_DIM,), dtype=jnp.float32) * 0.01
        return {'edge_index': edge_index, 'emb': emb, 'w1': w1, 'b1': b1, 'w2': w2, 'b2': b2}
    _L3_gnn_all = _L3_gnn_setup()
    _L3_gnn_in = {k: v for k, v in _L3_gnn_all.items() if k in ('w1', 'b1', 'w2', 'b2')}
    del _L3_gnn_all
    return {'x': x, 'src': src, 'dst': dst, 'edge_type_12': edge_type_12, 'node_vec1': node_vec1, 'L0_gnn_basis': _L0_gnn_in['basis'], 'L0_gnn_comp': _L0_gnn_in['comp'], 'L0_gnn_root': _L0_gnn_in['root'], 'L0_gnn_bias': _L0_gnn_in['bias'], 'L1_gnn_W_unite': _L1_gnn_in['W_unite'], 'L1_gnn_b_unite': _L1_gnn_in['b_unite'], 'L1_gnn_g1': _L1_gnn_in['g1'], 'L1_gnn_be1': _L1_gnn_in['be1'], 'L1_gnn_W_gconv': _L1_gnn_in['W_gconv'], 'L1_gnn_b_gconv': _L1_gnn_in['b_gconv'], 'L1_gnn_g2': _L1_gnn_in['g2'], 'L1_gnn_be2': _L1_gnn_in['be2'], 'L1_gnn_W_transfer': _L1_gnn_in['W_transfer'], 'L1_gnn_b_transfer': _L1_gnn_in['b_transfer'], 'L1_gnn_W_lin': _L1_gnn_in['W_lin'], 'L1_gnn_b_lin': _L1_gnn_in['b_lin'], 'L1_gnn_g3': _L1_gnn_in['g3'], 'L1_gnn_be3': _L1_gnn_in['be3'], 'L2_gnn_W1_out': _L2_gnn_in['W1_out'], 'L2_gnn_W1_back': _L2_gnn_in['W1_back'], 'L2_gnn_W2_out': _L2_gnn_in['W2_out'], 'L2_gnn_W2_back': _L2_gnn_in['W2_back'], 'L3_gnn_w1': _L3_gnn_in['w1'], 'L3_gnn_b1': _L3_gnn_in['b1'], 'L3_gnn_w2': _L3_gnn_in['w2'], 'L3_gnn_b2': _L3_gnn_in['b2']}

def reference(x, src, dst, edge_type_12, node_vec1, L0_gnn_basis, L0_gnn_comp, L0_gnn_root, L0_gnn_bias, L1_gnn_W_unite, L1_gnn_b_unite, L1_gnn_g1, L1_gnn_be1, L1_gnn_W_gconv, L1_gnn_b_gconv, L1_gnn_g2, L1_gnn_be2, L1_gnn_W_transfer, L1_gnn_b_transfer, L1_gnn_W_lin, L1_gnn_b_lin, L1_gnn_g3, L1_gnn_be3, L2_gnn_W1_out, L2_gnn_W1_back, L2_gnn_W2_out, L2_gnn_W2_back, L3_gnn_w1, L3_gnn_b1, L3_gnn_w2, L3_gnn_b2):
    import jax
    import jax.numpy as jnp

    def _L0_gnn_ref(edge_type, edge_index, x, basis, comp, root, bias):
        import jax, jax.numpy as jnp
        import numpy as np
        import math
        NUM_NODES = 30471
        EMBED = 64
        NUM_REL = 12
        NUM_BASES = 30
        NUM_EDGES = 62500
        N = x.shape[0]
        src, dst = (edge_index[0], edge_index[1])
        xs = x[src]
        W = jnp.einsum('rb,bio->rio', comp, basis)
        out = x @ root + bias
        for r in range(W.shape[0]):
            mask = edge_type == r
            num = jax.ops.segment_sum(jnp.where(mask[:, None], xs, 0.0), dst, num_segments=N)
            cnt = jax.ops.segment_sum(mask.astype(x.dtype), dst, num_segments=N)
            mean = num / jnp.maximum(cnt, 1.0)[:, None]
            out = out + mean @ W[r]
        return jax.nn.relu(out)

    def _L1_gnn_ref(x, edge_index, W_unite, b_unite, g1, be1, W_gconv, b_gconv, g2, be2, W_transfer, b_transfer, W_lin, b_lin, g3, be3):
        import jax, jax.numpy as jnp
        import numpy as np
        N = 50000
        E = 25000
        C = 64
        H = 64
        EPS = 1e-05

        def _bn(h, gamma, beta):
            m = h.mean(axis=0)
            v = ((h - m) ** 2).mean(axis=0)
            return (h - m) * jax.lax.rsqrt(v + EPS) * gamma + beta
        n = x.shape[0]
        src_e = edge_index[0]
        dst_e = edge_index[1]
        self_idx = jnp.arange(n)
        rows_src = jnp.concatenate([self_idx, src_e])
        rows_dom = jnp.concatenate([self_idx, dst_e])
        f = x[rows_src]
        dsum = jax.ops.segment_sum(f, rows_dom, num_segments=n)
        h = jnp.concatenate([f, dsum[rows_dom]], axis=-1) @ W_unite + b_unite
        h = jax.nn.relu(_bn(h, g1, be1))
        s = jax.ops.segment_sum(h, rows_dom, num_segments=n)
        msg = jax.ops.segment_sum(s[src_e], dst_e, num_segments=n)
        h2 = jnp.concatenate([h, msg[rows_dom]], axis=-1) @ W_gconv + b_gconv
        h2 = jax.nn.relu(_bn(h2, g2, be2))
        agg = jax.ops.segment_sum(h2, rows_src, num_segments=n)
        t = jnp.concatenate([h2[:n], agg], axis=-1) @ W_transfer + b_transfer
        t = jax.nn.relu(_bn(t, g2, be2))
        out = jax.nn.relu(t @ W_lin + b_lin)
        out = jax.nn.relu(_bn(out, g3, be3))
        return out

    def _L2_gnn_ref(x, sources, targets, norm, norm_t, W1_out, W1_back, W2_out, W2_back):
        import jax, jax.numpy as jnp
        import numpy as np
        EPS = 1e-05

        def _bn(x):
            mu = jnp.mean(x, axis=0, keepdims=True)
            var = jnp.var(x, axis=0, keepdims=True)
            return (x - mu) * jax.lax.rsqrt(var + EPS)

        def _conv(x, src, tgt, norm, W):
            n = x.shape[0]
            agg = x + jax.ops.segment_sum(x[src], tgt, num_segments=n)
            return norm * agg @ W

        def _biconv(x, src, tgt, norm, norm_t, W_out, W_back):
            return _conv(x, src, tgt, norm, W_out) + _conv(x, tgt, src, norm_t, W_back)
        save = x
        h = _bn(jax.nn.relu(x))
        h = _biconv(h, sources, targets, norm, norm_t, W1_out, W1_back)
        h = _bn(jax.nn.relu(h))
        h = _biconv(h, sources, targets, norm, norm_t, W2_out, W2_back)
        return save + h

    def _L3_gnn_ref(edge_index, emb, w1, b1, w2, b2):
        import jax, jax.numpy as jnp
        import numpy as np
        NUM_NODES = 31250
        EMBED_DIM = 64
        HIDDEN_DIM = 128
        src, dst = (edge_index[0], edge_index[1])
        messages = jnp.zeros_like(emb).at[dst].add(emb[src])
        aggregated = jax.nn.relu(messages @ w1.T + b1)
        updated = jax.nn.relu(aggregated @ w2.T + b2)
        return emb + updated
    edge_index = jnp.stack([src, dst])
    deg = jnp.maximum(jax.ops.segment_sum(jnp.ones(dst.shape, jnp.float32), dst, num_segments=3125), 1.0)
    deg_isqrt = deg ** (-0.5)
    x = _layernorm(x + _L0_gnn_ref(edge_type_12, edge_index, x, L0_gnn_basis, L0_gnn_comp, L0_gnn_root, L0_gnn_bias), axis=-1)
    x = _layernorm(x + _L1_gnn_ref(x, edge_index, L1_gnn_W_unite, L1_gnn_b_unite, L1_gnn_g1, L1_gnn_be1, L1_gnn_W_gconv, L1_gnn_b_gconv, L1_gnn_g2, L1_gnn_be2, L1_gnn_W_transfer, L1_gnn_b_transfer, L1_gnn_W_lin, L1_gnn_b_lin, L1_gnn_g3, L1_gnn_be3), axis=-1)
    x = _layernorm(x + _L2_gnn_ref(x, src, dst, deg_isqrt[:, None], node_vec1, L2_gnn_W1_out, L2_gnn_W1_back, L2_gnn_W2_out, L2_gnn_W2_back), axis=-1)
    x = _layernorm(x + _L3_gnn_ref(edge_index, x, L3_gnn_w1, L3_gnn_b1, L3_gnn_w2, L3_gnn_b2), axis=-1)
    return x

_drawn_inputs = setup_inputs


def setup_inputs(seed=0):
    import zlib

    import numpy as np

    out = dict(_drawn_inputs(seed))
    spreads = {'L0_gnn_bias': (0.0, 0.1),
     'L1_gnn_b_unite': (0.0, 2.0),
     'L1_gnn_g1': (1.0, 0.2),
     'L1_gnn_be1': (0.0, 0.1),
     'L1_gnn_b_gconv': (0.0, 2.0),
     'L1_gnn_g2': (1.0, 0.2),
     'L1_gnn_be2': (0.0, 0.1),
     'L1_gnn_b_transfer': (0.0, 2.0),
     'L1_gnn_b_lin': (0.0, 0.1),
     'L1_gnn_g3': (1.0, 0.2),
     'L1_gnn_be3': (0.0, 0.1)}
    factors = {'L3_gnn_b1': 44.501, 'L3_gnn_b2': 28.438}
    for name, (base, spread) in spreads.items():
        noise = np.random.default_rng([zlib.crc32(name.encode()), seed]).standard_normal(out[name].shape)
        drawn = base * np.exp(spread * noise) if base else spread * noise
        out[name] = jnp.asarray(drawn.astype(out[name].dtype))
    for name, factor in factors.items():
        out[name] = (out[name] * factor).astype(out[name].dtype)
    return out
```

```python
from contextlib import ExitStack

import concourse.bass as bass
from concourse import mybir

N = 3125
D = 64
E = 100000
R = 12
BASES = 30
P = 128
NB = (N + P - 1) // P
NP = NB * P
ET = 125
IT = E // ET
GT = 20
IG = IT // GT
GE = GT * ET
BINS = NB * NB
NT = 1408
TC = NT // P
TRASH = 4
EPS = 1e-5
BANK = 512
CH = [(c * BANK, min(BANK, NP - c * BANK)) for c in range((NP + BANK - 1) // BANK)]

ALU = mybir.AluOpType
ACT = mybir.ActivationFunctionType
AX = mybir.AxisListType
f32, bf16, f16 = mybir.dt.float32, mybir.dt.bfloat16, mybir.dt.float16
i32, i16 = mybir.dt.int32, mybir.dt.int16


H = 4
M = NT // H
HE = H * P
ALL = E + N
A_ROWS = (NB + TRASH) * P
PARAMS = ["L0_gnn_bias", "L1_gnn_b_unite", "L1_gnn_g1", "L1_gnn_be1", "L1_gnn_b_gconv", "L1_gnn_g2",
          "L1_gnn_be2", "L1_gnn_b_transfer", "L1_gnn_b_lin", "L1_gnn_g3", "L1_gnn_be3", "L3_gnn_b2"]
WEIGHTS = ["root", "unite_x", "unite_d", "gconv_h", "gconv_m", "transfer_h", "transfer_a", "lin",
           "W1_out", "W1_back", "W2_out", "W2_back", "gconv_hT"]

STEPS = {
    "tensor": (
        "i0_ps", "o0_ps", "root_ps", "ln0_mean", "ln0_var", "x1N_ps", "P_ps", "Q_ps", "DT_ps", "PN_ps",
        "QN_ps", "hsN_used", "sN_ps", "R_ps", "sW_ps", "GW_ps", "Mc_ps", "wc2_ps", "RN_ps", "h2_ps", "t_ps",
        "lin_ps", "ln1_mean", "ln1_var", "hN0_ps", "y1_ps", "hN1_ps", "y2_ps", "ln2_mean", "ln2_var",
        "x3N_ps", "h128_ps", "up_ps", "ln3_mean", "ln3_var", "outN_ps"),
    "vector": (
        "key", "rowtot", "bins", "based", "scat_seen", "tab_c", "fields", "consts2", "onesb", "xpad", "inv",
        "deg_rep", "i0_sb", "o0_sb", "ln0_in", "ln0_sq", "ln0", "x1", "dsum", "P_sb", "Q_sb", "DT_sb",
        "bn1_var", "PQ", "hsN", "s", "msg", "R_sb", "sW_sb", "gram_sb", "GW_sb", "bn2_var", "diag2", "RT",
        "wc2", "h2", "agg", "bnt_var", "bnt", "bnl_var", "bnl", "ln1_in", "ln1_sq", "ln1", "deg1", "bnh0_var",
        "bnh0", "agg2", "agg3", "bnh1_var", "bnh1", "agg4", "agg5", "ln2_in", "ln2_sq", "ln2", "m3", "h128",
        "ln3_in", "ln3_sq", "ln3"),
    "scalar": (
        "x1N", "PN", "QN", "sN", "RN", "deg_sqrt", "hN0", "hN1", "x3N", "outN"),
}


def wait_count(eng, sem, n):
    if not isinstance(n, int) or n > 0:
        eng.wait_ge(sem, n)


def stage_of(i, b, lag):
    n = 4 * i + b - lag
    if isinstance(n, int) and not 0 <= n < M:
        return None, 0, 0
    return n, (b - lag) % 4, i - (1 if b < lag else 0)


def half_rounds(eng, body, last):
    for b in range(4):
        body(0, b)
    with eng.Fori(1, M // 4) as i:
        for b in range(4):
            body(i, b)
    for b in range(last):
        body(M // 4, b)


class Region:

    def __init__(self, tensor):
        self.tensor, self.at = tensor, 0

    def take(self, parts, cols, dt=f32):
        words = cols if dt in (f32, i32) else (cols + 1) // 2
        ap = self.tensor[0:parts, self.at:self.at + words]
        self.at += words
        assert self.at <= self.tensor.shape[1], (self.at, self.tensor.shape)
        return ap if dt == f32 else ap.bitcast(dt)

    def reset(self):
        self.at = 0


def build(nc, A, out, stage):
    ctx = ExitStack()
    with ctx:
        def sb(name, shape, dt=f32):
            return ctx.enter_context(nc.sbuf_tensor(name, shape, dt))

        def dram(name, shape, dt=f32):
            return nc.dram_tensor(name, shape, dt, kind="Internal").ap()

        named = {}

        def S(name):
            if name not in named:
                named[name] = ctx.enter_context(nc.semaphore(name))
            return named[name]

        passed = {k: 0 for k in STEPS}

        def now(name):
            for eng, names in STEPS.items():
                if name in names:
                    assert names.index(name) == passed[eng], name
                    passed[eng] += 1
                    return S(eng + "_steps"), 1
            return S(name), 1

        def after(eng, name):
            for e, names in STEPS.items():
                if name in names:
                    eng.wait_ge(S(e + "_steps"), names.index(name) + 1)
                    return
            eng.wait_ge(S(name), 1)

        slots = dram("slots", [P * NT, 4], i32)
        keyrow_d = dram("keyrow_d", [IT, ET], f16)
        dbrow_d = dram("dbrow_d", [IT, ET], bf16)
        bins_d = dram("bins_d", [1, BINS])
        tab_d = dram("tab_d", [NT, 4], i16)
        same_d = dram("same_d", [1, NT])
        slrow_d = dram("slrow_d", [NT, P], bf16)
        dlrow_d = dram("dlrow_d", [NT, P], bf16)
        A_sd = dram("A_sd", [A_ROWS, NP])
        A_ds = dram("A_ds", [A_ROWS, NP])
        w_d = dram("w_d", [R, D * D])
        y_d = dram("y_d", [NP, R * D])

        F = sb("F", [P, 6 * NP + 960])
        WK = sb("WK", [P, 8192])
        RW = sb("RW", [P, 6400])
        NR = sb("NR", [P, 4800])
        ident = sb("ident", [P, P])
        iota = sb("iota", [P, P])
        iotab = sb("iotab", [P, P], bf16)
        pcol = sb("pcol", [P, 1])
        tri = sb("tri", [P, P])
        ones = sb("ones", [P, P])
        triT = sb("triT", [P, P])
        slf = sb("slf", [P, NT])
        dlf = sb("dlf", [P, NT])
        tab = sb("tab", [1, NT * 4], i16)
        small = sb("small", [P, 1800])
        gate = sb("gate", [1, 4])
        cnt = sb("cnt", [P, NB * 16])
        inv = sb("inv", [P, NB * 16])
        odeg = sb("odeg", [P, NB])
        onesb = sb("onesb", [P, 1], bf16)
        wts = sb("wts", [D, len(WEIGHTS), D])
        prm = sb("prm", [D, len(PARAMS)])
        w1T = sb("w1T", [D, 2 * D])
        w2T = sb("w2T", [2 * D, D])
        b1c = sb("b1c", [2 * D, 1])
        mean64 = sb("mean64", [D, D])
        cols = sb("cols", [D, 32])
        m64 = sb("m64", [D, 4 * D])
        epsc = sb("epsc", [D, 1])
        xs = sb("xs", [P, 2, D])
        ps = ctx.enter_context(nc.psum_tensor("ps", [P, 8, BANK], f32))

        rn, rr, rw = Region(NR), Region(RW), Region(WK)
        src_c, dst_c, typ_c = (rn.take(ET, IT, i32) for _ in range(3))
        dbf, sbf, key = (rn.take(ET, IT) for _ in range(3))
        C = F[0:NB, 0:(IT + 1) * NB].rearrange("p (t s) -> p t s", s=NB)
        krow = rr.take(ET, 2 * GE, f16).rearrange("p (b n) -> p b n", b=2)
        drow = rr.take(NB, 2 * GE, bf16).rearrange("p (b n) -> p b n", b=2)
        ohS = rr.take(ET, 2 * GT * NB, bf16).rearrange("p (b t s) -> p b t s", b=2, s=NB)
        ohD = rr.take(ET, 2 * GT * NB, bf16).rearrange("p (b t s) -> p b t s", b=2, s=NB)
        ohT = rw.take(NB, 2 * GE).rearrange("p (b n) -> p b n", b=2)
        cg = rw.take(NB, 2 * GT * NB).rearrange("p (b n) -> p b n", b=2)
        sm = Region(small)
        sel3 = sm.take(ET, GT * NB).rearrange("p (t s) -> p t s", s=NB)
        base_e = sm.take(ET, GT)
        rank = sm.take(ET, GT)
        posi = sm.take(ET, 3 * GT, i32).rearrange("p (k n) -> p k n", k=3)
        posf = sm.take(ET, GT)
        idx = sm.take(ET, 2 * GT, i32).rearrange("p (b n) -> p b n", b=2)
        rec = sm.take(ET, 2 * GT * 4, i32).rearrange("p (b n k) -> p b n k", b=2, k=4)
        junk2 = rw.take(ET, 2 * ET).rearrange("p (b e) -> p b e", b=2)
        kk = sm.take(ET, GT)
        zk = sm.take(ET, GT)
        tot = sm.take(NB, NB)
        toti = sm.take(NB, NB, i32)
        toti2 = sm.take(NB, NB, i32)
        tri4 = sm.take(P, TC, i32)
        tri4b = sm.take(P, TC, i32)
        nt_f = sm.take(NB, NB)
        incl = sm.take(NB, NB)
        one25 = sm.take(NB, NB)
        roff = sm.take(NB, 1)
        binrow = WK[:, 0:BINS]
        tcol = sm.take(P, 3 * TC)
        kcol = sm.take(P, 3 * TC)
        tmp24 = sm.take(P, NB)
        dbc = sm.take(P, TC)
        sbc = sm.take(P, TC)
        fin = sm.take(P, TC)
        tr4 = sm.take(P, TC)
        tabc = sm.take(P, TC * 4, i16).rearrange("p (c k) -> p c k", k=4)
        edge25 = sm.take(P, NB)
        samec = sm.take(P, TC)
        binjunk = WK[:, 640:640 + BINS]
        slot_i = F[:, 0:NT * 4].bitcast(i32).rearrange("p (t k) -> p t k", k=4)
        rowst = F[:, NT * 4:NT * 4 + TC * P].bitcast(bf16).rearrange("p (k c e) -> p k c e", k=2, e=P)
        tyf, same, yidx = NR[:, 0:NT], NR[:, NT:2 * NT], NR[:, 2 * NT:3 * NT].bitcast(i32)
        fill = F[:, 0:NT * 4].bitcast(i32)

        keyst = WK[0:IT // 8, 0:8 * ET // 2 + 4].bitcast(f16)[:, 0:8 * ET].rearrange("r (c e) -> r c e", c=8)
        dbst = WK[0:IT // 8, 1024:1024 + 8 * ET // 2 + 4].bitcast(bf16)[:, 0:8 * ET].rearrange("r (c e) -> r c e", c=8)
        rows8 = IT // 8

        posA = F[0:ET, NT * 4:NT * 4 + 2 * IT].bitcast(i32).rearrange("p (k n) -> p k n", k=2)

        ring = Region(WK)
        b_oS = ring.take(P, 4 * P, bf16).rearrange("p (b n) -> p b n", b=4)
        b_oD = ring.take(P, 4 * P, bf16).rearrange("p (b n) -> p b n", b=4)
        b_oT = ring.take(P, 4 * 16, bf16).rearrange("p (b n) -> p b n", b=4)
        b_acc = ring.take(P, 4 * 2 * P).rearrange("p (b n) -> p b n", b=4)
        l_row = ring.take(P, 2 * HE, bf16).rearrange("p (b n) -> p b n", b=2)
        l_oDT = ring.take(P, 2 * HE).rearrange("p (b n) -> p b n", b=2)
        l_oDw = ring.take(P, 2 * HE).rearrange("p (b n) -> p b n", b=2)
        l_y = ring.take(P, 4 * H * D).rearrange("p (b k n) -> p b k n", b=4, k=H)
        l_idx = ring.take(P, 4 * H, i32).rearrange("p (b k) -> p b k", b=4)
        l_w = ring.take(P, 2 * H).rearrange("p (b k) -> p b k", b=2)
        l_j = ring.take(P, 2 * 16).rearrange("p (b k) -> p b k", b=2)
        ring.reset()
        e_srow = ring.take(P, 2 * HE, bf16).rearrange("p (b n) -> p b n", b=2)
        e_drow = ring.take(P, 2 * HE, bf16).rearrange("p (b n) -> p b n", b=2)
        e_oST = ring.take(P, 2 * HE).rearrange("p (b n) -> p b n", b=2)
        e_oDT = ring.take(P, 4 * HE).rearrange("p (b n) -> p b n", b=4)
        e_o = ring.take(P, 4 * HE).rearrange("p (b n) -> p b n", b=4)
        e_h = ring.take(P, 2 * H * D).rearrange("p (b n) -> p b n", b=2)
        e_hT = ring.take(D, 2 * HE).rearrange("p (b n) -> p b n", b=2)
        e_h2 = ring.take(P, 2 * H * D).rearrange("p (b n) -> p b n", b=2)
        arow = WK[:, 0:2 * NP].rearrange("p (b n) -> p b n", b=2)
        FT = [F[0:D, k * NP:(k + 1) * NP] for k in range(6)]
        h128 = F[:, 2 * NP:3 * NP]
        Wsb = F[0:R, 2 * NP:2 * NP + D * D]
        Wall = F[0:D, 4 * NP:4 * NP + R * D].rearrange("p (r o) -> p r o", r=R)
        ystg = F[:, 4 * NP + R * D:4 * NP + 3 * R * D].rearrange("p (b n) -> p b n", b=2)
        compT = F[0:BASES, 3 * NP:3 * NP + R]
        basis = F[0:BASES, 3 * NP + R:3 * NP + R + D * D]
        i0row, o0row = RW[0:D, 0:NP], RW[0:D, NP:2 * NP]
        sm25 = tmp24
        NT_ = [NR[:, k * NB * D:(k + 1) * NB * D] for k in range(3)]
        psF = ps[0:D, 0:7, :].rearrange("p b n -> p (b n)")[:, 0:NP]
        psH = ps[:, 0:7, :].rearrange("p b n -> p (b n)")[:, 0:NP]
        psN = ps[:, 0:4, :].rearrange("p b n -> p (b n)")[:, 0:NB * D]
        wt = {n: wts[:, k, :] for k, n in enumerate(WEIGHTS)}
        pr = {n: prm[:, k:k + 1] for k, n in enumerate(PARAMS)}
        gram_sb, gw_sb, diag2, wc2 = (m64[:, k * D:(k + 1) * D] for k in range(4))
        PAD = slice(N, NP)

        block = ctx.enter_context(nc.Block())

        @block.gpsimd
        def _(pool):
            def link(ins):
                links[0] += 1
                ins.then_inc(S("pool_link"), 1)
                pool.wait_ge(S("pool_link"), links[0])
            links = [0]
            nc.gpsimd.iota(iota[:], pattern=[[1, P]], base=0, channel_multiplier=0,
                           allow_small_or_imprecise_dtypes=True).then_inc(S("const"), 1)
            nc.gpsimd.iota(pcol[:], pattern=[[0, 1]], base=0, channel_multiplier=1,
                           allow_small_or_imprecise_dtypes=True).then_inc(S("const"), 1)
            nc.gpsimd.iota(tcol[:, 0:TC], pattern=[[P, TC]], base=0, channel_multiplier=1,
                           allow_small_or_imprecise_dtypes=True).then_inc(S("const"), 1)
            nc.gpsimd.iota(edge25[:], pattern=[[NB, NB]], base=0, channel_multiplier=0,
                           allow_small_or_imprecise_dtypes=True).then_inc(S("const"), 1)
            nc.gpsimd.memset(ones[:], 1.0).then_inc(S("ones"), 1)
            nc.gpsimd.memset(gate[:], 0.0).then_inc(S("gate"), 1)
            after(pool, "ones")
            nc.gpsimd.affine_select(out=tri[:], in_=ones[:], compare_op=ALU.is_gt, fill=0.0, base=0,
                                    pattern=[[-1, P]], channel_multiplier=1).then_inc(S("tri"), 1)
            nc.gpsimd.affine_select(out=triT[:], in_=ones[:], compare_op=ALU.is_gt, fill=0.0, base=0,
                                    pattern=[[1, P]], channel_multiplier=-1).then_inc(S("tri"), 1)
            nc.gpsimd.affine_select(out=ident[:], in_=ones[:], compare_op=ALU.is_equal, fill=0.0, base=0,
                                    pattern=[[-1, P]], channel_multiplier=1).then_inc(S("ident"), 1)
            pool.wait_ge(S("filled"), 16)
            after(pool, "gate")
            with pool.Fori(0, IG // 2) as i:
                for b in range(2):
                    pool.wait_ge(S("idx_ready"), i * 2 + b + 1)
                    pool.wait_ge(S("gate"), i * 2 + b + 1)
                    nc.gpsimd.tensor_tensor(gate[0:1, 0:1], gate[0:1, 1:2], gate[0:1, 2:3],
                                            ALU.add).then_inc(S("gate"), 1)
                    for k in range(GT):
                        nc.gpsimd.indirect_dma_start(
                            out=slots, out_offset=bass.IndirectOffsetOnAxis(ap=idx[:, b, k:k + 1], axis=0),
                            in_=rec[:, b, k, :], in_offset=None).then_inc(S(f"scattered{b}"), 16)
            if stage == "A":
                return
            pool.wait_ge(S("y_out0"), 16 * 13)
            pool.wait_ge(S("y_out1"), 16 * 12)
            table = y_d.rearrange("n (r o) -> (n r) o", r=R)
            sorted_gates = IG

            def gather(i, b):
                n, slot, _ = stage_of(i, b, 0)
                wait_count(pool, S("l0_sc"), n - 3)
                pool.wait_ge(S("l0_idx"), n + 1)
                pool.wait_ge(S("gate"), sorted_gates + n + 1)
                nc.gpsimd.tensor_tensor(gate[0:1, 0:1], gate[0:1, 1:2], gate[0:1, 2:3],
                                        ALU.add).then_inc(S("gate"), 1)
                for k in range(H):
                    nc.gpsimd.indirect_dma_start(
                        out=l_y[:, slot, k, :], out_offset=None, in_=table,
                        in_offset=bass.IndirectOffsetOnAxis(ap=l_idx[:, slot, k:k + 1], axis=0)).then_inc(S(f"l0_y{slot}"), 16)
            half_rounds(pool, gather, 0)

        @block.sync
        def _(sp):
            sp.dma_start(src_c, A["src_c"]).then_inc(S("ids"), 16)
            for ap, name in ((wts[:], "weights"), (prm[:], "params"), (w1T[:], "w1T"), (w2T[:], "w2T"), (b1c[:], "b1")):
                sp.dma_start(ap, A[name]).then_inc(S("wts_in"), 16)
            sp.dma_start(dst_c, A["dst_c"]).then_inc(S("ids"), 16)
            sp.dma_start(typ_c, A["typ_c"]).then_inc(S("ids"), 16)
            after(sp, "fill_set")
            sp.dma_start(slots.rearrange("(p t) k -> p (t k)", p=P), fill).then_inc(S("filled"), 16)
            sp.wait_ge(S("rows_t"), 2 * 8)
            rows = IT // 8
            sp.dma_start(keyrow_d.rearrange("(c r) e -> r c e", r=rows), keyst).then_inc(S("rows_out"), 16)
            sp.dma_start(dbrow_d.rearrange("(c r) e -> r c e", r=rows), dbst).then_inc(S("rows_out"), 16)
            sp.wait_ge(S("rows_out"), 32)
            kd = keyrow_d.rearrange("t e -> (t e)").rearrange("(o n) -> o n", o=1)
            dd = dbrow_d.rearrange("t e -> (t e)").rearrange("(o n) -> o n", o=1)
            for b in range(2):
                sp.dma_start(krow[:, b, :], kd[:, b * GE:(b + 1) * GE].to_broadcast([ET, GE])).then_inc(S(f"krow{b}"), 16)
                sp.dma_start(drow[:, b, :], dd[:, b * GE:(b + 1) * GE].to_broadcast([NB, GE])).then_inc(S(f"krow{b}"), 16)
            with sp.Fori(1, IG // 2) as i:
                for b in range(2):
                    sp.wait_ge(S("idx_ready"), i * 2 + b - 1)
                    sp.dma_start(krow[:, b, :], kd[:, bass.ds((i * 2 + b) * GE, GE)].to_broadcast([ET, GE])).then_inc(S(f"krow{b}"), 16)
                    sp.dma_start(drow[:, b, :], dd[:, bass.ds((i * 2 + b) * GE, GE)].to_broadcast([NB, GE])).then_inc(S(f"krow{b}"), 16)
            after(sp, "bins")
            sp.dma_start(bins_d.rearrange("o (p s) -> (o p) s", s=NB), incl).then_inc(S("bins_out"), 16)
            sp.wait_ge(S("bins_out"), 16)
            after(sp, "scat_seen")
            sp.dma_start(binrow, bins_d.to_broadcast([P, BINS])).then_inc(S("binrow"), 16)
            sp.dma_start(F[:, 0:NT * 4].bitcast(i32), slots.rearrange("(p t) k -> p (t k)", p=P)).then_inc(S("slots_in"), 16)
            after(sp, "tab_c")
            with nc.allow_non_contiguous_dma(reason="one small table"):
                sp.dma_start(tab_d.rearrange("(c p) k -> p c k", p=P), tabc).then_inc(S("tab_out"), 16)
                sp.dma_start(same_d.rearrange("o (c p) -> p (o c)", p=P), samec).then_inc(S("tab_out"), 16)
            sp.wait_ge(S("tab_out"), 32)
            sp.dma_start(tab[:], tab_d.rearrange("t k -> (t k)").rearrange("(o n) -> o n", o=1)).then_inc(S("tab_in"), 16)
            sp.dma_start(same, same_d.to_broadcast([P, NT])).then_inc(S("tab_in"), 16)
            after(sp, "rows_s")
            sp.dma_start(slrow_d.rearrange("(c p) e -> p c e", p=P), rowst[:, 0]).then_inc(S("slrow_out"), 16)
            sp.dma_start(dlrow_d.rearrange("(c p) e -> p c e", p=P), rowst[:, 1]).then_inc(S("slrow_out"), 16)
            sp.wait_ge(S("slrow_out"), 32)
            after(sp, "fields")
            after(sp, "rows_s")
            sp.dma_start(compT, A["compT"]).then_inc(S("basis_in"), 16)
            sp.dma_start(basis, A["basis"]).then_inc(S("basis_in"), 16)
            sp.dma_start(FT[0][:, 0:N], A["xT"]).then_inc(S("xT_in"), 16)
            sp.wait_ge(S("W_sb"), 2)
            sp.dma_start(w_d, Wsb).then_inc(S("W_out"), 16)
            sp.wait_ge(S("W_out"), 16)
            with nc.allow_non_contiguous_dma(reason="rows of one relation"):
                sp.dma_start(Wall, w_d.rearrange("r (i o) -> i r o", i=D)).then_inc(S("W_in"), 16)
            for k in range(NB):
                sp.wait_ge(S("y_v"), k + 1)
                sp.wait_ge(S("y_a"), k + 1)
                sp.dma_start(y_d[k * P:(k + 1) * P, :], ystg[:, k % 2, :]).then_inc(S(f"y_out{k % 2}"), 16)

            def put(i, b):
                for k in range(H):
                    t = (4 * i + b) * H + k
                    sp.wait_ge(S("bl_acc"), t + 1)
                    row = sp.value_load(tab[0:1, bass.ds(t * 4 + 2, 1)], min_val=0, max_val=NB + TRASH - 1)
                    col = sp.value_load(tab[0:1, bass.ds(t * 4, 1)], min_val=0, max_val=NB - 1)
                    sp.dma_start(A_sd[bass.ds(row * P, P), bass.ds(col * P, P)], b_acc[:, k, 0:P]).then_inc(S(f"bl_out{k}"), 16)
            half_rounds(sp, put, 0)

            srows = slrow_d.rearrange("t e -> (t e)").rearrange("(o n) -> o n", o=1)
            drows = dlrow_d.rearrange("t e -> (t e)").rearrange("(o n) -> o n", o=1)

            def l0_rows(i, b):
                n = 4 * i + b
                wait_count(sp, S("l0_tr"), n - 1)
                sp.dma_start(l_row[:, b % 2, :], drows[:, bass.ds(n * HE, HE)].to_broadcast([P, HE])).then_inc(S(f"l0_row{b % 2}"), 16)
            half_rounds(sp, l0_rows, 0)

            def product_rows(q, adj):
                for b in range(2):
                    wait_count(sp, S("pr_mm"), q * NB)
                    if q < 3:
                        sp.wait_ge(S(("l0_add", "b_add", "d_add")[q]), NT)
                    sp.dma_start(arow[:, b, :], adj[b * P:(b + 1) * P, :]).then_inc(S(f"arow{b}"), 16)
                with sp.Fori(1, NB // 2) as i:
                    for b in range(2):
                        sp.wait_ge(S("pr_mm"), q * NB + i * 2 + b - 1)
                        sp.dma_start(arow[:, b, :], adj[bass.ds((i * 2 + b) * P, P), :]).then_inc(S(f"arow{b}"), 16)
                sp.wait_ge(S("pr_mm"), q * NB + NB - 2)
                sp.dma_start(arow[:, 0, :], adj[(NB - 1) * P:NB * P, :]).then_inc(S("arow0"), 16)

            def edge_rows(p):
                def body(i, b):
                    n = 4 * i + b
                    wait_count(sp, S(p + "_tr"), n - 1)
                    sp.dma_start(e_srow[:, b % 2, :], srows[:, bass.ds(n * HE, HE)].to_broadcast([P, HE])).then_inc(S(f"{p}_row{b % 2}"), 16)
                    sp.dma_start(e_drow[:, b % 2, :], drows[:, bass.ds(n * HE, HE)].to_broadcast([P, HE])).then_inc(S(f"{p}_row{b % 2}"), 16)
                half_rounds(sp, body, 0)
            for k in range(4):
                sp.wait_ge(S(f"bl_out{k}"), M * 32)
            product_rows(0, A_sd)
            sp.wait_ge(S("pr_mm"), NB)
            edge_rows("b")
            product_rows(1, A_sd)
            sp.wait_ge(S("pr_mm"), 2 * NB)
            edge_rows("d")
            product_rows(2, A_sd)
            product_rows(3, A_ds)
            sp.dma_start(o0row[:, 0:N], A["normt"].to_broadcast([D, N])).then_inc(S("normt_in"), 16) if False else None
            product_rows(4, A_sd)
            product_rows(5, A_ds)
            product_rows(6, A_sd)
            after(sp, "outN")
            full = N // P
            on = NT_[1].rearrange("p (b d) -> p b d", d=D)
            sp.dma_start(out[0:full * P, :].rearrange("(b p) d -> p b d", p=P), on[:, 0:full, :]).then_inc(S("out"), 16)
            sp.dma_start(out[full * P:N, :], on[0:N - full * P, full, :]).then_inc(S("out"), 16)
            sp.wait_ge(S("out"), 32)

        @block.vector
        def _(dve):
            links = [0]

            def link(ins):
                links[0] += 1
                ins.then_inc(S("dve_link"), 1)
                dve.wait_ge(S("dve_link"), links[0])

            def mark(ins, name):
                ins.then_inc(*now(name))
                after(dve, name)

            V = nc.vector
            V.memset(fill, -1).then_inc(S("fill_set"), 1)
            dve.wait_ge(S("const"), 4)
            link(V.tensor_copy(iotab[:], iota[:]))
            dve.wait_ge(S("ids"), 48)
            link(V.tensor_single_scalar(posA[:, 0], dst_c, 7, op=ALU.arith_shift_right))
            link(V.tensor_single_scalar(posA[:, 1], src_c, 7, op=ALU.arith_shift_right))
            link(V.tensor_copy(dbf, posA[:, 0]))
            link(V.tensor_copy(sbf, posA[:, 1]))
            mark(V.scalar_tensor_tensor(out=key, in0=dbf, scalar=32.0, in1=sbf, op0=ALU.mult, op1=ALU.add), "key")
            for n, (st, dt) in enumerate(((keyst, f16), (dbst, bf16))):
                for c in range(8):
                    dve.wait_ge(S("row_tr"), n * 8 + c + 1)
                    V.tensor_copy(st[:, c, :], ps[0:rows8, c % 2, 0:ET]).then_inc(S("rows_t"), 1)
            def onehots(b, g):
                gs = bass.ds(g * GT, GT)
                V.tensor_tensor(ohD[:, b], dbf[:, gs].unsqueeze(2).to_broadcast([ET, GT, NB]),
                                iota[0:ET, 0:NB].unsqueeze(1).to_broadcast([ET, GT, NB]), ALU.is_equal)
                return V.tensor_tensor(ohS[:, b], sbf[:, gs].unsqueeze(2).to_broadcast([ET, GT, NB]),
                                       iota[0:ET, 0:NB].unsqueeze(1).to_broadcast([ET, GT, NB]), ALU.is_equal)
            for b in range(2):
                onehots(b, b).then_inc(S("oh"), 1)
            with dve.Fori(1, IG // 2) as i:
                for b in range(2):
                    g = i * 2 + b
                    dve.wait_ge(S("counted"), g - 1)
                    onehots(b, g).then_inc(S("oh"), 1)
            dve.wait_ge(S("C_in"), IG)
            dve.wait_ge(S("filled"), 16)
            link(V.memset(C[:, 0, :], 0.0))
            zero = WK[0:NB, 2000:2000 + IT]
            link(V.memset(zero, 0.0))
            for s in range(NB):
                last = V.tensor_tensor_scan(C[:, 1:IT + 1, s], C[:, 1:IT + 1, s], zero, 0.0, ALU.add, ALU.add)
                link(last)
            link(V.tensor_scalar(toti, C[:, IT, :], float(P - 1), None, ALU.add))
            link(V.tensor_single_scalar(toti2, toti, 7, op=ALU.arith_shift_right))
            link(V.tensor_scalar(nt_f, toti2, 1.0, None, ALU.max))
            link(V.memset(one25, 0.0))
            mark(V.tensor_tensor_scan(incl, nt_f, one25, 0.0, ALU.add, ALU.add), "rowtot")
            after(dve, "roff")
            link(V.tensor_copy(roff, ps[0:NB, 4, 0:1]))
            link(V.tensor_tensor(incl, incl, nt_f, ALU.subtract))
            mark(V.tensor_scalar(incl, incl, roff, None, ALU.add), "bins")
            link(V.tensor_scalar(tot, incl, float(P), None, ALU.mult))
            mark(V.tensor_tensor(C[:, 0:IT, :], C[:, 0:IT, :], tot.unsqueeze(1).to_broadcast([NB, IT, NB]), ALU.add), "based")
            dve.wait_ge(S("tri"), 2)

            def lookup(b, g, first):
                gs = bass.ds(g * GT, GT)
                q = (g - b) // 2 if isinstance(g, int) else None
                n = g + 1
                dve.wait_ge(S(f"krow{b}"), (half(g, b) + 1) * 32)
                if not first:
                    dve.wait_ge(S("looked"), g - 1)
                V.tensor_scalar(ohT[:, b, :], drow[:, b, :], pcol[0:NB, :], None, ALU.is_equal).then_inc(S("ohT"), 1)
                V.tensor_tensor(ohS[:, b], sbf[:, gs].unsqueeze(2).to_broadcast([ET, GT, NB]),
                                iota[0:ET, 0:NB].unsqueeze(1).to_broadcast([ET, GT, NB]), ALU.is_equal)
                V.tensor_tensor(kk, key[:, gs], zk, ALU.add).then_inc(S("kk"), 1)
                dve.wait_ge(S("kk"), n)
                for k in range(GT):
                    last = V.scalar_tensor_tensor(out=junk2[:, k % 2, :], in0=krow[:, b, k * ET:(k + 1) * ET], scalar=kk[:, k:k + 1],
                                                  in1=tri[0:ET, 0:ET], op0=ALU.is_equal, op1=ALU.mult,
                                                  accum_out=rank[:, k:k + 1])
                    last.then_inc(S("ranked"), 1)
                    dve.wait_ge(S("ranked"), g * GT + k + 1)
                dve.wait_ge(S("looked"), n)
                V.tensor_tensor(sel3, ps[0:ET, 5 + b, 0:GT * NB].rearrange("p (t s) -> p t s", s=NB), ohS[:, b], ALU.mult).then_inc(S("selected"), 1)
                dve.wait_ge(S("selected"), n)
                V.tensor_reduce(base_e, sel3, AX.X, ALU.add).then_inc(S("reduced"), 1)
                dve.wait_ge(S("reduced"), n)
                steps = [0]

                def step(ins):
                    steps[0] += 1
                    ins.then_inc(S("pos_step"), 1)
                    dve.wait_ge(S("pos_step"), g * 5 + steps[0])
                step(V.tensor_tensor(posi[:, 0], base_e, rank, ALU.add))
                step(V.tensor_single_scalar(posi[:, 1], posi[:, 0], 7, op=ALU.arith_shift_right))
                step(V.tensor_single_scalar(posi[:, 2], posi[:, 0], P - 1, op=ALU.bitwise_and))
                step(V.tensor_copy(posf, posi[:, 1]))
                if not first:
                    dve.wait_ge(S(f"scattered{b}"), half(g, b) * (16 * GT))
                V.tensor_single_scalar(rec[:, b, :, 1], src_c[:, gs], P - 1, op=ALU.bitwise_and)
                V.tensor_single_scalar(rec[:, b, :, 2], dst_c[:, gs], P - 1, op=ALU.bitwise_and)
                V.tensor_scalar(rec[:, b, :, 3], typ_c[:, gs], 0.0, None, ALU.add)
                step(V.scalar_tensor_tensor(out=rec[:, b, :, 0], in0=src_c[:, gs], scalar=float(R), in1=typ_c[:, gs], op0=ALU.mult, op1=ALU.add))
                V.scalar_tensor_tensor(out=idx[:, b, :], in0=posi[:, 2], scalar=float(NT), in1=posf, op0=ALU.mult, op1=ALU.add).then_inc(S("idx_ready"), 1)
                dve.wait_ge(S("idx_ready"), n)

            def half(g, b):
                return hb[0]
            hb = [0]
            link(V.memset(zk, 0.0))
            for b in range(2):
                lookup(b, b, True)
            with dve.Fori(1, IG // 2) as i:
                for b in range(2):
                    hb[0] = i
                    lookup(b, i * 2 + b, False)
            for b in range(2):
                dve.wait_ge(S(f"scattered{b}"), IG // 2 * 16 * GT)
            mark(V.memset(binjunk[:, 0:1], 0.0), "scat_seen")
            link(V.tensor_scalar(tcol[:, TC:2 * TC], tcol[:, 0:TC], -1.0, None, ALU.add))
            link(V.tensor_scalar(tcol[:, 2 * TC:3 * TC], tcol[:, 0:TC], 1.0, None, ALU.add))
            dve.wait_ge(S("binrow"), 16)
            for c in range(3 * TC):
                link(V.tensor_scalar(binjunk, binrow, tcol[:, c:c + 1], 0.0, ALU.is_le, ALU.add, accum_out=kcol[:, c:c + 1]))
            link(V.tensor_scalar(kcol, kcol, -1.0, None, ALU.add))
            for c in range(TC):
                link(V.tensor_scalar(tmp24, edge25, kcol[:, c:c + 1], 0.0, ALU.is_le, ALU.add, accum_out=dbc[:, c:c + 1]))
            link(V.tensor_scalar(dbc, dbc, -1.0, None, ALU.add))
            link(V.scalar_tensor_tensor(out=sbc, in0=dbc, scalar=-float(NB), in1=kcol[:, 0:TC], op0=ALU.mult, op1=ALU.add))
            link(V.tensor_tensor(samec, kcol[:, 0:TC], kcol[:, TC:2 * TC], ALU.is_equal))
            link(V.tensor_scalar(tmp24[:, 0:TC], tcol[:, 0:TC], float(NT - 1), None, ALU.is_equal))
            link(V.tensor_tensor(kcol[:, 2 * TC:3 * TC], kcol[:, 2 * TC:3 * TC], tmp24[:, 0:TC], ALU.add))
            link(V.tensor_tensor(fin, kcol[:, 0:TC], kcol[:, 2 * TC:3 * TC], ALU.not_equal))
            link(V.tensor_copy(tri4, tcol[:, 0:TC]))
            link(V.tensor_single_scalar(tri4b, tri4, TRASH - 1, op=ALU.bitwise_and))
            link(V.tensor_scalar(tr4, tri4b, float(NB), None, ALU.add))
            link(V.tensor_copy(tabc[:, :, 0], dbc))
            link(V.tensor_copy(tabc[:, :, 1], sbc))
            for k, blk in ((2, sbc), (3, dbc)):
                link(V.tensor_tensor(tmp24[:, 0:TC], blk, tr4, ALU.subtract))
                link(V.tensor_tensor(tmp24[:, 0:TC], tmp24[:, 0:TC], fin, ALU.mult))
                ins = V.tensor_tensor(tabc[:, :, k], tmp24[:, 0:TC], tr4, ALU.add)
                link(ins) if k == 2 else mark(ins, "tab_c")
            dve.wait_ge(S("slots_in"), 16)
            link(V.tensor_copy(slf[:], slot_i[:, :, 1]))
            link(V.tensor_copy(tyf, slot_i[:, :, 3]))
            link(V.tensor_scalar(yidx, slot_i[:, :, 0], 0.0, None, ALU.max))
            mark(V.tensor_copy(dlf[:], slot_i[:, :, 2]), "fields")
            for n in range(2):
                for c in range(TC):
                    dve.wait_ge(S("slot_tr"), n * TC + c + 1)
                    ins = V.tensor_copy(rowst[:, n, c, :], ps[:, (n * TC + c) % 2, 0:P])
                    ins.then_inc(S("slot_cp"), 1)
            dve.wait_ge(S("slot_cp"), 2 * TC)
            V.memset(binjunk[:, 0:1], 0.0).then_inc(S("rows_s"), 1)
            link(V.memset(cnt[:], 0.0))
            link(V.memset(odeg[:], 0.0))
            link(V.memset(epsc[:], EPS))
            dve.wait_ge(S("slrow_out"), 32)
            link(V.memset(FT[1], 0.0))
            mark(V.memset(mean64[:], 1.0 / D), "consts2")
            mark(V.memset(onesb[:], 1.0), "onesb")
            after(dve, "rows_s")
            dve.wait_ge(S("tab_in"), 32)
            mark(V.memset(FT[0][:, PAD], 0.0), "xpad")
            after(dve, "W_ps")
            V.tensor_copy(Wsb[:, 0:4 * BANK], ps[0:R, 0:4, :].rearrange("p b n -> p (b n)")).then_inc(S("W_sb"), 1)
            for k in range(NB):
                dve.wait_ge(S("y_ps"), k + 1)
                if k >= 2:
                    dve.wait_ge(S(f"y_out{k % 2}"), 16 * (k // 2))
                V.tensor_copy(ystg[:, k % 2, 0:R * D // 2], ps[:, 2 * (k % 2), 0:R * D // 2]).then_inc(S("y_v"), 1)

            def build(i, b):
                for k in range(H):
                    t = (4 * i + b) * H + k
                    V.tensor_scalar(b_oS[:, k, :], iotab[:], slf[:, bass.ds(t, 1)], None, ALU.is_equal)
                    V.tensor_scalar(b_oD[:, k, :], iotab[:], dlf[:, bass.ds(t, 1)], None, ALU.is_equal)
                    V.tensor_scalar(b_oT[:, k, 0:R], iotab[:, 0:R], tyf[:, bass.ds(t, 1)], None, ALU.is_equal).then_inc(S("bl_oh"), 1)
                for k in range(H):
                    t = (4 * i + b) * H + k
                    n = 4 * i + b
                    db = dve.value_load(tab[0:1, bass.ds(t * 4, 1)], min_val=0, max_val=NB - 1)
                    sbk = dve.value_load(tab[0:1, bass.ds(t * 4 + 1, 1)], min_val=0, max_val=NB - 1)
                    dve.wait_ge(S("bl_mm"), t + 1)
                    wait_count(dve, S(f"bl_out{k}"), n * 32)
                    V.scalar_tensor_tensor(out=b_acc[:, k, :], in0=b_acc[:, (k - 1) % 4, :], scalar=same[:, bass.ds(t, 1)],
                                           in1=ps[:, k, 0:2 * P], op0=ALU.mult, op1=ALU.add).then_inc(S("bl_acc"), 1)
                    c = cnt[:, bass.ds(db * 16, R)]
                    V.tensor_tensor(c, c, ps[:, k, 2 * P:2 * P + R], ALU.add)
                    o = odeg[:, bass.ds(sbk, 1)]
                    V.tensor_tensor(o, o, ps[:, k, 2 * P + 16:2 * P + 17], ALU.add).then_inc(S("bl_cnt"), 1)
                    dve.wait_ge(S("bl_acc"), t + 1)
                    dve.wait_ge(S("bl_cnt"), t + 1)
            link(V.memset(b_acc[:, 3, :], 0.0))
            half_rounds(dve, build, 0)
            link(V.tensor_scalar(inv[:], cnt[:], 1.0, None, ALU.max))
            mark(V.reciprocal(inv[:], inv[:]), "inv")

            def layer0(i, b):
                n, s4, _ = stage_of(i, b, 0)
                if n is not None:
                    wait_count(dve, S(f"l0_y{s4}"), i * 64)
                    V.tensor_scalar(l_idx[:, s4, :], yidx[:, bass.ds(n * H, H)], 0.0, None, ALU.add).then_inc(S("l0_idx"), 1)
                    dve.wait_ge(S(f"l0_row{b % 2}"), (2 * i + b // 2 + 1) * 16)
                    wait_count(dve, S("l0_g"), n - 1)
                    V.tensor_scalar(l_oDT[:, b % 2, :], l_row[:, b % 2, :], pcol[:], None, ALU.is_equal).then_inc(S("l0_tr"), 1)
                n, s4, _ = stage_of(i, b, 1)
                if n is not None:
                    dve.wait_ge(S("l0_g"), n + 1)
                    wait_count(dve, S("l0_sc"), n - 1)
                    for k in range(H):
                        V.scalar_tensor_tensor(out=l_j[:, k % 2, 0:R], in0=iota[:, 0:R], scalar=tyf[:, bass.ds(n * H + k, 1)],
                                               in1=ps[:, s4 % 2, k * 16:k * 16 + R], op0=ALU.is_equal, op1=ALU.mult,
                                               accum_out=l_w[:, s4 % 2, k:k + 1]).then_inc(S("l0_w"), 1)
                        dve.wait_ge(S("l0_w"), n * H + k + 1)
                    for k in range(H):
                        V.tensor_scalar(l_oDw[:, s4 % 2, k * P:(k + 1) * P], iota[:], dlf[:, bass.ds(n * H + k, 1)],
                                        l_w[:, s4 % 2, k:k + 1], ALU.is_equal, ALU.mult).then_inc(S("l0_oh"), 1)
                accumulate(i, b, "l0", 3, 0, FT[1], 4)

            def accumulate(i, b, p, lag, which, accT, bank):
                n, s4, _ = stage_of(i, b, lag)
                if n is not None:
                    for k in range(H):
                        blk = dve.value_load(tab[0:1, bass.ds((n * H + k) * 4 + which, 1)], min_val=0, max_val=NB - 1)
                        if k == 0:
                            dve.wait_ge(S(p + "_sc"), n + 1)
                        a = accT[:, bass.ds(blk * P, P)]
                        V.tensor_tensor(a, a, ps[0:D, bank + s4 % 2, k * P:(k + 1) * P], ALU.add).then_inc(S(p + "_add"), 1)
                        dve.wait_ge(S(p + "_add"), n * H + k + 1)
            half_rounds(dve, layer0, 3)
            link(V.memset(cols[:], 0.0))

            vl = slice(0, N)

            def col(k):
                return cols[:, k:k + 1]

            def ln(tag, X, o, c, t):
                after(dve, tag + "_mean")
                link(V.tensor_tensor(c, X, psF, ALU.subtract))
                mark(V.tensor_tensor(t, c, c, ALU.mult), tag + "_sq")
                after(dve, tag + "_std")
                link(V.reciprocal(t, t))
                mark(V.tensor_tensor(o, c, t, ALU.mult), tag)

            def affine(tag, m, var, g, be, s_, t_):
                mark(V.tensor_scalar(var, var, 1.0, None, ALU.mult), tag + "_var")
                after(dve, tag + "_std")
                link(V.reciprocal(s_, s_))
                if g is not None:
                    link(V.tensor_tensor(s_, s_, g, ALU.mult))
                link(V.tensor_tensor(t_, m, s_, ALU.mult))
                if be is not None:
                    link(V.tensor_tensor(t_, be, t_, ALU.subtract))
                else:
                    link(V.tensor_scalar(t_, t_, -1.0, None, ALU.mult))

            def bn(tag, X, o, g, be, relu):
                link(V.tensor_reduce(col(0), X[:, vl], AX.X, ALU.add))
                link(V.tensor_scalar(col(0), col(0), 1.0 / N, None, ALU.mult))
                link(V.tensor_scalar(X[:, vl], X[:, vl], col(0), None, ALU.subtract))
                link(V.scalar_tensor_tensor(out=o[:, vl], in0=X[:, vl], scalar=1.0, in1=X[:, vl], op0=ALU.mult, op1=ALU.mult,
                                            accum_out=col(1)))
                link(V.tensor_scalar(col(1), col(1), 1.0 / N, None, ALU.mult))
                link(V.memset(col(2), 0.0))
                affine(tag, col(2), col(1), g, be, col(3), col(4))
                link(V.tensor_scalar(o[:, vl], X[:, vl], col(3), col(4), ALU.mult, ALU.add))
                if relu:
                    link(V.tensor_scalar(o[:, vl], o[:, vl], 0.0, None, ALU.max))
                mark(V.memset(o[:, PAD], 0.0), tag)

            def dot(o, a, op, sc, b_, acc):
                link(V.scalar_tensor_tensor(out=o[:, vl], in0=a[:, vl], scalar=sc, in1=b_[:, vl], op0=op, op1=ALU.mult, accum_out=acc))

            dve.wait_ge(S("wts_in"), 80)
            link(V.tensor_reduce(sm25, cnt[:].rearrange("p (b r) -> p b r", r=16)[:, :, 0:R], AX.X, ALU.add))
            link(V.tensor_copy(NT_[0].rearrange("p (b d) -> p b d", d=D), sm25.unsqueeze(2).to_broadcast([P, NB, D])))
            mark(V.tensor_copy(NT_[1].rearrange("p (b d) -> p b d", d=D), odeg[:].unsqueeze(2).to_broadcast([P, NB, D])), "deg_rep")
            after(dve, "i0_ps")
            mark(V.tensor_copy(i0row, psF), "i0_sb")
            after(dve, "o0_ps")
            mark(V.tensor_copy(o0row, psF), "o0_sb")
            after(dve, "root_ps")
            link(V.tensor_tensor(FT[2], psF, FT[1], ALU.add))
            link(V.tensor_scalar(FT[2], FT[2], pr["L0_gnn_bias"], 0.0, ALU.add, ALU.max))
            mark(V.tensor_tensor(FT[2], FT[2], FT[0], ALU.add), "ln0_in")
            ln("ln0", FT[2], FT[0], FT[3], FT[4])
            mark(V.memset(FT[0][:, PAD], 0.0), "x1")

            dve.wait_ge(S("pr_mm"), 1 * NB)
            mark(V.tensor_tensor(FT[1], psF, FT[0], ALU.add), "dsum")
            after(dve, "P_ps")
            mark(V.tensor_copy(FT[2], psF), "P_sb")
            after(dve, "Q_ps")
            mark(V.tensor_scalar(FT[3], psF, pr["L1_gnn_b_unite"], None, ALU.add), "Q_sb")
            after(dve, "DT_ps")
            mark(V.tensor_copy(FT[4], psF), "DT_sb")
            dot(FT[5], o0row, ALU.add, 1.0, FT[2], col(5))
            dot(FT[1], FT[5], ALU.mult, 1.0, FT[2], col(6))
            dot(FT[5], i0row, ALU.add, 1.0, FT[3], col(7))
            dot(FT[1], FT[5], ALU.mult, 1.0, FT[3], col(8))
            dot(FT[1], FT[4], ALU.mult, 2.0, FT[3], col(9))

            def row_stats(tag, sums, squares, g, be):
                link(V.tensor_tensor(col(0), sums[0], sums[1], ALU.add))
                link(V.tensor_scalar(col(0), col(0), 1.0 / ALL, None, ALU.mult))
                link(V.tensor_tensor(col(1), squares[0], squares[1], ALU.add))
                link(V.tensor_tensor(col(1), col(1), squares[2], ALU.add))
                link(V.tensor_tensor(col(2), col(0), col(0), ALU.mult))
                link(V.scalar_tensor_tensor(out=col(1), in0=col(1), scalar=1.0 / ALL, in1=col(2), op0=ALU.mult, op1=ALU.subtract))
                affine(tag, col(0), col(1), g, be, col(3), col(4))
            row_stats("bn1", (col(5), col(7)), (col(6), col(8), col(9)), pr["L1_gnn_g1"], pr["L1_gnn_be1"])
            link(V.tensor_scalar(FT[2], FT[2], col(3), None, ALU.mult))
            link(V.tensor_scalar(FT[3], FT[3], col(3), col(4), ALU.mult, ALU.add))
            link(V.memset(FT[2][:, PAD], 0.0))
            mark(V.memset(FT[3][:, PAD], 0.0), "PQ")
            link(V.tensor_tensor(FT[4], FT[2], FT[3], ALU.add))
            link(V.tensor_scalar(FT[4], FT[4], 0.0, None, ALU.max))
            link(V.tensor_copy(FT[5], FT[4]))
            after(dve, "PN")
            after(dve, "QN")
            link(V.tensor_tensor(NT_[2], NT_[0], NT_[1], ALU.add))
            mark(V.tensor_scalar(NT_[2], NT_[2], 0.0, None, ALU.max), "hsN")

            def onehot_round(p, which):
                def body(i, b):
                    n, s4, _ = stage_of(i, b, 0)
                    if n is not None:
                        dve.wait_ge(S(f"{p}_row{b % 2}"), (2 * i + b // 2 + 1) * 32)
                        wait_count(dve, S(p + "_z"), n - 1)
                        wait_count(dve, S(p + "_sc"), n - 3)
                        V.tensor_scalar(e_oST[:, b % 2, :], e_srow[:, b % 2, :], pcol[:], None, ALU.is_equal)
                        V.tensor_scalar(e_oDT[:, s4, :], e_drow[:, b % 2, :], pcol[:], None, ALU.is_equal).then_inc(S(p + "_tr"), 1)
                        col_ = (dlf, slf)[which]
                        V.tensor_tensor(e_o[:, s4, :].rearrange("p (k n) -> p k n", k=H),
                                        col_[:, bass.ds(n * H, H)].unsqueeze(2).to_broadcast([P, H, P]),
                                        iota[:].unsqueeze(1).to_broadcast([P, H, P]), ALU.is_equal).then_inc(S(p + "_o"), 1)
                    accumulate(i, b, p, 2 if which == 0 else 4, which, FT[5], 2 if which == 0 else 6)
                return body
            dve.wait_ge(S("pr_mm"), NB)
            half_rounds(dve, onehot_round("b", 0), 2)
            mark(V.memset(cols[:, 20:21], 0.0), "s")
            dve.wait_ge(S("pr_mm"), 2 * NB)
            mark(V.tensor_copy(FT[1], psF), "msg")
            after(dve, "R_ps")
            mark(V.tensor_scalar(FT[2], psF, pr["L1_gnn_b_gconv"], None, ALU.add), "R_sb")
            after(dve, "sW_ps")
            mark(V.tensor_copy(FT[3], psF), "sW_sb")
            mark(V.tensor_copy(gram_sb, ps[0:D, 7, 0:D]), "gram_sb")
            after(dve, "GW_ps")
            mark(V.tensor_tensor(gw_sb, ps[0:D, 7, 0:D], wt["gconv_h"], ALU.mult), "GW_sb")
            after(dve, "Mc_ps")
            link(V.tensor_copy(col(10), ps[0:D, 7, 0:1]))
            link(V.tensor_reduce(col(5), FT[3][:, vl], AX.X, ALU.add))
            dot(FT[1], i0row, ALU.add, 1.0, FT[2], col(7))
            dot(FT[1], FT[1], ALU.mult, 1.0, FT[2], col(8))
            dot(FT[1], FT[3], ALU.mult, 2.0, FT[2], col(9))
            row_stats("bn2", (col(5), col(7)), (col(10), col(8), col(9)), pr["L1_gnn_g2"], pr["L1_gnn_be2"])
            mark(V.tensor_scalar(diag2, ident[0:D, 0:D], col(3), None, ALU.mult), "diag2")
            link(V.tensor_scalar(FT[2], FT[2], col(3), col(4), ALU.mult, ALU.add))
            mark(V.memset(FT[2][:, PAD], 0.0), "RT")
            after(dve, "wc2_ps")
            mark(V.tensor_copy(wc2, ps[0:D, 7, 0:D]), "wc2")
            after(dve, "h2_ps")
            link(V.tensor_tensor(FT[4], psF, FT[2], ALU.add))
            link(V.tensor_scalar(FT[4], FT[4], 0.0, None, ALU.max))
            mark(V.tensor_copy(FT[5], FT[4]), "h2")
            half_rounds(dve, onehot_round("d", 1), 4)
            mark(V.memset(cols[:, 21:22], 0.0), "agg")
            after(dve, "t_ps")
            link(V.tensor_scalar(FT[1], psF, pr["L1_gnn_b_transfer"], None, ALU.add))
            bn("bnt", FT[1], FT[2], pr["L1_gnn_g2"], pr["L1_gnn_be2"], True)
            after(dve, "lin_ps")
            link(V.tensor_scalar(FT[3], psF, pr["L1_gnn_b_lin"], 0.0, ALU.add, ALU.max))
            bn("bnl", FT[3], FT[4], pr["L1_gnn_g3"], pr["L1_gnn_be3"], True)
            mark(V.tensor_tensor(FT[5], FT[0], FT[4], ALU.add), "ln1_in")
            ln("ln1", FT[5], FT[0], FT[1], FT[2])

            link(V.tensor_scalar(i0row, i0row, 1.0, None, ALU.max))
            mark(V.tensor_scalar(cols[:, 22:23], cols[:, 22:23], 0.0, None, ALU.mult), "deg1")
            after(dve, "deg_sqrt")
            link(V.reciprocal(i0row, i0row))
            dve.wait_ge(S("normt_in"), 16)
            link(V.memset(o0row[:, PAD], 0.0))
            link(V.tensor_scalar(FT[1], FT[0], 0.0, None, ALU.max))
            for k, (q, w) in enumerate(((2, "y1"), (4, "y2"))):
                bn(f"bnh{k}", FT[1], FT[2], None, None, False)
                for j, (row, o) in enumerate(((i0row, FT[3]), (o0row, FT[4]))):
                    dve.wait_ge(S("pr_mm"), (q + j + 1) * NB)
                    link(V.tensor_tensor(o, psF, FT[2], ALU.add))
                    mark(V.tensor_tensor(o, o, row, ALU.mult), f"agg{q + j}")
                after(dve, w + "_ps")
                if k == 0:
                    link(V.tensor_scalar(FT[1], psF, 0.0, None, ALU.max))
            mark(V.scalar_tensor_tensor(out=FT[5], in0=FT[0], scalar=2.0, in1=psF, op0=ALU.mult, op1=ALU.add), "ln2_in")
            ln("ln2", FT[5], FT[0], FT[1], FT[2])

            dve.wait_ge(S("pr_mm"), 7 * NB)
            mark(V.tensor_copy(FT[1], psF), "m3")
            after(dve, "h128_ps")
            mark(V.tensor_scalar(h128, psH, b1c[:], 0.0, ALU.add, ALU.max), "h128")
            after(dve, "up_ps")
            link(V.tensor_scalar(FT[3], psF, pr["L3_gnn_b2"], 0.0, ALU.add, ALU.max))
            mark(V.scalar_tensor_tensor(out=FT[5], in0=FT[0], scalar=2.0, in1=FT[3], op0=ALU.mult, op1=ALU.add), "ln3_in")
            ln("ln3", FT[5], FT[1], FT[2], FT[4])

        @block.scalar
        def _(act):
            act.wait_ge(S("filled"), 16)
            after(act, "key")
            with act.Fori(0, IG // 2) as i:
                for b in range(2):
                    g = i * 2 + b
                    act.wait_ge(S("counted"), g + 1)
                    nc.scalar.activation(C[:, bass.ds(g * GT + 1, GT), :], ps[0:NB, 2 + b, 0:GT * NB].rearrange("p (t s) -> p t s", s=NB),
                                         ACT.Copy).then_inc(S("C_in"), 1)
            after(act, "based")
            for b in range(2):
                nc.scalar.activation(cg[:, b, :].rearrange("p (t s) -> p t s", s=NB), C[:, b * GT:(b + 1) * GT, :], ACT.Copy).then_inc(S("cg"), 1)
            with act.Fori(1, IG // 2) as i:
                for b in range(2):
                    g = i * 2 + b
                    act.wait_ge(S("looked"), g - 1)
                    nc.scalar.activation(cg[:, b, :].rearrange("p (t s) -> p t s", s=NB), C[:, bass.ds(g * GT, GT), :], ACT.Copy).then_inc(S("cg"), 1)


            after(act, "W_ps")
            nc.scalar.activation(Wsb[:, 4 * BANK:8 * BANK], ps[0:R, 4:8, :].rearrange("p b n -> p (b n)"), ACT.Copy).then_inc(S("W_sb"), 1)
            for k in range(NB):
                act.wait_ge(S("y_ps"), k + 1)
                if k >= 2:
                    act.wait_ge(S(f"y_out{k % 2}"), 16 * (k // 2))
                nc.scalar.activation(ystg[:, k % 2, R * D // 2:R * D], ps[:, 2 * (k % 2) + 1, 0:R * D // 2], ACT.Copy).then_inc(S("y_a"), 1)

            act.wait_ge(S("tab_in"), 32)

            def put(i, b):
                for k in range(H):
                    t = (4 * i + b) * H + k
                    act.wait_ge(S("bl_acc"), t + 1)
                    row = act.value_load(tab[0:1, bass.ds(t * 4 + 3, 1)], min_val=0, max_val=NB + TRASH - 1)
                    col = act.value_load(tab[0:1, bass.ds(t * 4 + 1, 1)], min_val=0, max_val=NB - 1)
                    act.dma_start(A_ds[bass.ds(row * P, P), bass.ds(col * P, P)], b_acc[:, k, P:2 * P]).then_inc(S(f"bl_out{k}"), 16)
            half_rounds(act, put, 0)

            def std(tag, o, in_, prior):
                after(act, prior)
                nc.scalar.activation(o, in_, ACT.Sqrt, bias=epsc[:]).then_inc(S(tag), 1)

            def to_sb(name, o, in_):
                after(act, name + "_ps")
                nc.scalar.activation(o, in_, ACT.Copy).then_inc(*now(name))

            def stationary(q, src):
                for b in range(2):
                    wait_count(act, S("pr_mm"), q * NB)
                    nc.scalar.activation(xs[:, b, :], src[:, b * D:(b + 1) * D], ACT.Copy).then_inc(S("pr_xs"), 1)
                with act.Fori(1, NB // 2) as i:
                    for b in range(2):
                        act.wait_ge(S("pr_mm"), q * NB + i * 2 + b - 1)
                        nc.scalar.activation(xs[:, b, :], src[:, bass.ds((i * 2 + b) * D, D)], ACT.Copy).then_inc(S("pr_xs"), 1)
                act.wait_ge(S("pr_mm"), q * NB + NB - 2)
                nc.scalar.activation(xs[:, 0, :], src[:, (NB - 1) * D:NB * D], ACT.Copy).then_inc(S("pr_xs"), 1)

            def product_in(q, name, k=0):
                to_sb(name, NT_[k], psN)
                after(act, name)
                stationary(q, NT_[k])
            after(act, "consts2")
            std("ln0_std", FT[4], psF, "ln0_var")
            after(act, "o0_sb")
            product_in(0, "x1N")
            std("bn1_std", cols[:, 3:4], cols[:, 1:2], "bn1_var")
            to_sb("PN", NT_[0], psN)
            to_sb("QN", NT_[1], psN)

            def relu_rounds(p):
                def body(i, b):
                    n, s4, _ = stage_of(i, b, 0)
                    if n is not None:
                        act.wait_ge(S(p + "_z"), n + 1)
                        wait_count(act, S(p + ("_sc" if p == "b" else "_T")), n - 1)
                        nc.scalar.activation(e_h[:, s4 % 2, :], ps[:, s4 % 2, 0:H * D], ACT.Relu).then_inc(S(p + "_h"), 1)
                    if p == "b":
                        return
                    n, s4, _ = stage_of(i, b, 1)
                    if n is not None:
                        act.wait_ge(S("d_T"), n + 1)
                        wait_count(act, S("d_u"), n - 1)
                        nc.scalar.activation(e_hT[:, s4 % 2, :], ps[0:D, 2 + s4 % 2, 0:HE], ACT.Copy).then_inc(S("d_hT"), 1)
                    n, s4, _ = stage_of(i, b, 2)
                    if n is not None:
                        act.wait_ge(S("d_u"), n + 1)
                        wait_count(act, S("d_sc"), n - 1)
                        nc.scalar.activation(e_h2[:, s4 % 2, :], ps[:, 4 + s4 % 2, 0:H * D], ACT.Relu).then_inc(S("d_h2"), 1)
                half_rounds(act, body, 0 if p == "b" else 2)
            relu_rounds("b")
            after(act, "hsN_used")
            product_in(1, "sN", 2)
            std("bn2_std", cols[:, 3:4], cols[:, 1:2], "bn2_var")
            act.wait_ge(S("pr_mm"), 2 * NB)
            to_sb("RN", NT_[2], psN)
            after(act, "RN")
            relu_rounds("d")
            std("bnt_std", cols[:, 3:4], cols[:, 1:2], "bnt_var")
            std("bnl_std", cols[:, 3:4], cols[:, 1:2], "bnl_var")
            std("ln1_std", FT[2], psF, "ln1_var")
            act.dma_start(o0row[:, 0:N], A["normt"].to_broadcast([D, N])).then_inc(S("normt_in"), 16)
            after(act, "deg1")
            nc.scalar.activation(i0row, i0row, ACT.Sqrt).then_inc(*now("deg_sqrt"))
            for k, q in enumerate((2, 4)):
                std(f"bnh{k}_std", cols[:, 3:4], cols[:, 1:2], f"bnh{k}_var")
                product_in(q, f"hN{k}")
                stationary(q + 1, NT_[0])
            std("ln2_std", FT[2], psF, "ln2_var")
            product_in(6, "x3N")
            std("ln3_std", FT[4], psF, "ln3_var")
            act.wait_ge(S("pr_mm"), 7 * NB)
            to_sb("outN", NT_[1], psN)

        @block.tensor
        def _(pe):
            after(pe, "ident")
            after(pe, "key")
            for n, col in enumerate((key, dbf)):
                for c in range(8):
                    m = n * 8 + c
                    if m >= 2:
                        pe.wait_ge(S("rows_t"), m - 1)
                    nc.tensor.transpose(ps[0:rows8, c % 2, 0:ET], col[:, c * rows8:(c + 1) * rows8],
                                        ident[0:ET, 0:ET]).then_inc(S("row_tr"), 1)
            def count(b, g, first):
                pe.wait_ge(S("oh"), g + 1)
                if not first:
                    pe.wait_ge(S("C_in"), g - 1)
                for k in range(GT):
                    last = nc.tensor.matmul(ps[0:NB, 2 + b, k * NB:(k + 1) * NB], ohD[:, b, k, :], ohS[:, b, k, :], start=True, stop=True)
                last.then_inc(S("counted"), 1)
            for b in range(2):
                count(b, b, True)
            with pe.Fori(1, IG // 2) as i:
                for b in range(2):
                    count(b, i * 2 + b, False)
            after(pe, "rowtot")
            pe.wait_ge(S("tri"), 2)
            nc.tensor.matmul(ps[0:NB, 4, 0:1], triT[0:NB, 0:NB], incl[:, NB - 1:NB], start=True, stop=True).then_inc(S("roff"), 1)

            def look(b, g, first):
                pe.wait_ge(S("ohT"), g + 1)
                pe.wait_ge(S("cg"), g + 1)
                if not first:
                    pe.wait_ge(S("selected"), g - 1)
                for k in range(GT):
                    last = nc.tensor.matmul(ps[0:ET, 5 + b, k * NB:(k + 1) * NB], ohT[:, b, k * ET:(k + 1) * ET],
                                            cg[:, b, k * NB:(k + 1) * NB], start=True, stop=True)
                last.then_inc(S("looked"), 1)
            for b in range(2):
                look(b, b, True)
            with pe.Fori(1, IG // 2) as i:
                for b in range(2):
                    look(b, i * 2 + b, False)
            after(pe, "fields")
            for n, col in enumerate((slf, dlf)):
                for c in range(TC):
                    m = n * TC + c
                    if m >= 2:
                        pe.wait_ge(S("slot_cp"), m - 1)
                    nc.tensor.transpose(ps[:, m % 2, 0:P], col[:, c * P:(c + 1) * P], ident[:]).then_inc(S("slot_tr"), 1)

            pe.wait_ge(S("basis_in"), 32)
            pe.wait_ge(S("slot_cp"), 2 * TC)
            for c in range(8):
                last = nc.tensor.matmul(ps[0:R, c, :], compT, basis[:, c * BANK:(c + 1) * BANK], start=True, stop=True)
            last.then_inc(S("W_ps"), 1)
            pe.wait_ge(S("W_in"), 16)
            pe.wait_ge(S("W_sb"), 2)
            pe.wait_ge(S("xT_in"), 16)
            after(pe, "xpad")
            wall = Wall.rearrange("p r o -> p (r o)")
            for k in range(NB):
                if k >= 2:
                    pe.wait_ge(S("y_v"), k - 1)
                    pe.wait_ge(S("y_a"), k - 1)
                for j in range(2):
                    last = nc.tensor.matmul(ps[:, 2 * (k % 2) + j, 0:R * D // 2], FT[0][:, k * P:(k + 1) * P],
                                            wall[:, j * R * D // 2:(j + 1) * R * D // 2], start=True, stop=True)
                last.then_inc(S("y_ps"), 1)
            pe.wait_ge(S("y_v"), NB)
            pe.wait_ge(S("y_a"), NB)
            after(pe, "onesb")

            def build(i, b):
                for k in range(H):
                    t = (4 * i + b) * H + k
                    pe.wait_ge(S("bl_oh"), t + 1)
                    wait_count(pe, S("bl_cnt"), t - 3)
                    nc.tensor.matmul(ps[:, k, 0:P], b_oS[:, k, :], b_oD[:, k, :], start=True, stop=True)
                    nc.tensor.matmul(ps[:, k, 2 * P + 16:2 * P + 17], b_oS[:, k, :], onesb[:], start=True, stop=True)
                    nc.tensor.matmul(ps[:, k, P:2 * P], b_oD[:, k, :], b_oS[:, k, :], start=True, stop=True)
                    nc.tensor.matmul(ps[:, k, 2 * P:2 * P + R], b_oD[:, k, :], b_oT[:, k, 0:R], start=True, stop=True).then_inc(S("bl_mm"), 1)
            half_rounds(pe, build, 0)

            def blocks_of(n, which):
                return [pe.value_load(tab[0:1, bass.ds((n * H + k) * 4 + which, 1)], min_val=0, max_val=NB - 1) for k in range(H)]

            after(pe, "inv")

            def layer0(i, b):
                n, s4, _ = stage_of(i, b, 0)
                if n is not None:
                    dbs = blocks_of(n, 0)
                    pe.wait_ge(S("l0_tr"), n + 1)
                    wait_count(pe, S("l0_w"), (n - 1) * H if not isinstance(n, int) or n > 1 else 0)
                    for k in range(H):
                        last = nc.tensor.matmul(ps[:, s4 % 2, k * 16:k * 16 + R], l_oDT[:, s4 % 2, k * P:(k + 1) * P],
                                                inv[:, bass.ds(dbs[k] * 16, R)], start=True, stop=True)
                    last.then_inc(S("l0_g"), 1)
                n, s4, i4 = stage_of(i, b, 2)
                if n is not None:
                    pe.wait_ge(S("l0_oh"), n * H + H)
                    pe.wait_ge(S(f"l0_y{s4}"), (i4 + 1) * 64)
                    wait_count(pe, S("l0_add"), (n - 1) * H if not isinstance(n, int) or n > 1 else 0)
                    for k in range(H):
                        last = nc.tensor.matmul(ps[0:D, 4 + s4 % 2, k * P:(k + 1) * P], l_y[:, s4, k, :],
                                                l_oDw[:, s4 % 2, k * P:(k + 1) * P], start=True, stop=True)
                    last.then_inc(S("l0_sc"), 1)
            half_rounds(pe, layer0, 2)

            def mm(name, terms, rows=D):
                for c, (at, w) in enumerate(CH):
                    for k, (lhs, rhs) in enumerate(terms):
                        last = nc.tensor.matmul(ps[0:rows, c, 0:w], lhs, rhs[:, at:at + w], start=k == 0, stop=k == len(terms) - 1)
                last.then_inc(*now(name))

            def to_T(name, src):
                for k in range(NB):
                    last = nc.tensor.transpose(psT(k), src[:, k * D:(k + 1) * D], ident[:])
                last.then_inc(*now(name))

            def psT(k):
                return ps[0:D, k // 4, (k % 4) * P:(k % 4 + 1) * P]

            def to_N(name, src):
                for k in range(NB):
                    last = nc.tensor.transpose(ps[:, k // 8, (k % 8) * D:(k % 8 + 1) * D], src[:, k * P:(k + 1) * P], ident[0:D, 0:D])
                last.then_inc(*now(name + "_ps"))

            def product(q):
                def one(k, b, uses, first, lst):
                    pe.wait_ge(S(f"arow{b}"), 16 * uses)
                    pe.wait_ge(S("pr_xs"), q * NB + k + 1)
                    for c, (at, w) in enumerate(CH):
                        last = nc.tensor.matmul(ps[0:D, c, 0:w], xs[:, b, :], arow[:, b, at:at + w], start=first, stop=lst)
                    last.then_inc(S("pr_mm"), 1)
                one(0, 0, 13 * q + 1, True, False)
                one(1, 1, 12 * q + 1, False, False)
                with pe.Fori(1, NB // 2) as i:
                    one(i * 2, 0, 13 * q + i + 1, False, False)
                    one(i * 2 + 1, 1, 12 * q + i + 1, False, False)
                one(NB - 1, 0, 13 * (q + 1), False, True)

            def ln(tag, X, t):
                after(pe, tag + "_in")
                mm(tag + "_mean", [(mean64[:], X)])
                after(pe, tag + "_sq")
                mm(tag + "_var", [(mean64[:], t)])

            after(pe, "deg_rep")
            pe.wait_ge(S("l0_add"), NT)
            to_T("i0_ps", NT_[0])
            after(pe, "i0_sb")
            to_T("o0_ps", NT_[1])
            after(pe, "o0_sb")
            pe.wait_ge(S("wts_in"), 80)
            mm("root_ps", [(wt["root"], FT[0])])
            ln("ln0", FT[2], FT[4])
            after(pe, "x1")
            to_N("x1N", FT[0])
            after(pe, "x1N")
            product(0)
            after(pe, "dsum")
            mm("P_ps", [(wt["unite_x"], FT[0])])
            after(pe, "P_sb")
            mm("Q_ps", [(wt["unite_d"], FT[1])])
            after(pe, "Q_sb")
            mm("DT_ps", [(wt["unite_x"], FT[1])])
            after(pe, "DT_sb")
            after(pe, "PQ")
            to_N("PN", FT[2])
            after(pe, "PN")
            to_N("QN", FT[3])
            after(pe, "hsN")
            for k in range(NB - 1):
                nc.tensor.matmul(ps[0:D, 7, 0:D], NT_[2][:, k * D:(k + 1) * D], NT_[2][:, k * D:(k + 1) * D],
                                 start=k == 0, stop=False)

            def gather_rows(p, n, s4):
                sls, dls = blocks_of(n, 1), blocks_of(n, 0)
                pe.wait_ge(S(p + "_tr"), n + 1)
                wait_count(pe, S(p + "_h"), n - 1)
                for k in range(H):
                    e = slice(k * P, (k + 1) * P)
                    o = ps[:, s4 % 2, k * D:(k + 1) * D]
                    nc.tensor.matmul(o, e_oST[:, s4 % 2, e], NT_[0][:, bass.ds(sls[k] * D, D)], start=True, stop=False)
                    last = nc.tensor.matmul(o, e_oDT[:, s4, e], NT_[1][:, bass.ds(dls[k] * D, D)], start=False, stop=True)
                last.then_inc(S(p + "_z"), 1)

            def sums(p, n, s4, h, ready, bank):
                pe.wait_ge(S(ready), n + 1)
                pe.wait_ge(S(p + "_o"), n + 1)
                wait_count(pe, S(p + "_add"), (n - 1) * H if not isinstance(n, int) or n > 1 else 0)
                for k in range(H):
                    hk = h[:, s4 % 2, k * D:(k + 1) * D]
                    last = nc.tensor.matmul(ps[0:D, bank + s4 % 2, k * P:(k + 1) * P], hk, e_o[:, s4, k * P:(k + 1) * P], start=True, stop=True)
                    if p == "b":
                        last = nc.tensor.matmul(ps[0:D, 7, 0:D], hk, hk, start=False, stop=False)
                last.then_inc(S(p + "_sc"), 1)

            def round_b(i, b):
                n, s4, _ = stage_of(i, b, 0)
                if n is not None:
                    gather_rows("b", n, s4)
                n, s4, _ = stage_of(i, b, 1)
                if n is not None:
                    sums("b", n, s4, e_h, "b_h", 2)
            half_rounds(pe, round_b, 1)
            nc.tensor.matmul(ps[0:D, 7, 0:D], NT_[2][:, (NB - 1) * D:NB * D], NT_[2][:, (NB - 1) * D:NB * D],
                             start=False, stop=True).then_inc(*now("hsN_used"))
            after(pe, "s")
            to_N("sN", FT[5])
            after(pe, "sN")
            product(1)
            after(pe, "msg")
            mm("R_ps", [(wt["gconv_m"], FT[1])])
            after(pe, "R_sb")
            mm("sW_ps", [(wt["gconv_h"], FT[5])])
            after(pe, "gram_sb")
            nc.tensor.matmul(ps[0:D, 7, 0:D], gram_sb, wt["gconv_h"], start=True, stop=True).then_inc(*now("GW_ps"))
            after(pe, "GW_sb")
            nc.tensor.matmul(ps[0:D, 7, 0:1], gw_sb, ones[0:D, 0:1], start=True, stop=True).then_inc(*now("Mc_ps"))
            after(pe, "diag2")
            nc.tensor.matmul(ps[0:D, 7, 0:D], wt["gconv_hT"], diag2, start=True, stop=True).then_inc(*now("wc2_ps"))
            after(pe, "RT")
            to_N("RN", FT[2])
            after(pe, "RN")
            after(pe, "wc2")
            mm("h2_ps", [(wc2, FT[4])])
            after(pe, "h2")

            def round_d(i, b):
                n, s4, _ = stage_of(i, b, 0)
                if n is not None:
                    gather_rows("d", n, s4)
                n, s4, _ = stage_of(i, b, 1)
                if n is not None:
                    pe.wait_ge(S("d_h"), n + 1)
                    wait_count(pe, S("d_hT"), n - 1)
                    for k in range(H):
                        last = nc.tensor.matmul(ps[0:D, 2 + s4 % 2, k * P:(k + 1) * P], e_h[:, s4 % 2, k * D:(k + 1) * D], ident[:], start=True, stop=True)
                    last.then_inc(S("d_T"), 1)
                n, s4, _ = stage_of(i, b, 2)
                if n is not None:
                    dls = blocks_of(n, 0)
                    pe.wait_ge(S("d_hT"), n + 1)
                    wait_count(pe, S("d_h2"), n - 1)
                    for k in range(H):
                        e = slice(k * P, (k + 1) * P)
                        o = ps[:, 4 + s4 % 2, k * D:(k + 1) * D]
                        nc.tensor.matmul(o, e_hT[:, s4 % 2, e], wc2, start=True, stop=False)
                        last = nc.tensor.matmul(o, e_oDT[:, s4, e], NT_[2][:, bass.ds(dls[k] * D, D)], start=False, stop=True)
                    last.then_inc(S("d_u"), 1)
                n, s4, _ = stage_of(i, b, 3)
                if n is not None:
                    sums("d", n, s4, e_h2, "d_h2", 6)
            half_rounds(pe, round_d, 3)
            after(pe, "agg")
            mm("t_ps", [(wt["transfer_h"], FT[4]), (wt["transfer_a"], FT[5])])
            after(pe, "bnt")
            mm("lin_ps", [(wt["lin"], FT[2])])
            ln("ln1", FT[5], FT[2])
            for k, (q, w) in enumerate(((2, "1"), (4, "2"))):
                after(pe, f"bnh{k}")
                to_N(f"hN{k}", FT[2])
                after(pe, f"hN{k}")
                product(q)
                after(pe, f"agg{q}")
                product(q + 1)
                after(pe, f"agg{q + 1}")
                mm(f"y{k + 1}_ps", [(wt[f"W{w}_out"], FT[3]), (wt[f"W{w}_back"], FT[4])])
            ln("ln2", FT[5], FT[2])
            after(pe, "ln2")
            to_N("x3N", FT[0])
            after(pe, "x3N")
            product(6)
            after(pe, "m3")
            mm("h128_ps", [(w1T[:], FT[1])], 2 * D)
            after(pe, "h128")
            mm("up_ps", [(w2T[:], h128)])
            ln("ln3", FT[5], FT[4])
            after(pe, "ln3")
            to_N("outN", FT[1])


def kernel(**inputs):
    import numpy as np
    import concourse.bacc as bacc
    from concourse.bass_utils import run_bass_kernel_spmd

    a = {k: np.asarray(v) for k, v in inputs.items()}
    arrays = {
        "xT": np.ascontiguousarray(a["x"].T),
        "src_c": np.ascontiguousarray(a["src"].reshape(IT, ET).T),
        "dst_c": np.ascontiguousarray(a["dst"].reshape(IT, ET).T),
        "typ_c": np.ascontiguousarray(a["edge_type_12"].reshape(IT, ET).T),
    }
    g = a["L1_gnn_W_gconv"]
    weights = [a["L0_gnn_root"], a["L1_gnn_W_unite"][:D], a["L1_gnn_W_unite"][D:], g[:D], g[D:],
               a["L1_gnn_W_transfer"][:D], a["L1_gnn_W_transfer"][D:], a["L1_gnn_W_lin"], a["L2_gnn_W1_out"],
               a["L2_gnn_W1_back"], a["L2_gnn_W2_out"], a["L2_gnn_W2_back"], g[:D].T]
    arrays.update({
        "weights": np.ascontiguousarray(np.stack(weights, 1)),
        "params": np.ascontiguousarray(np.stack([a[n] for n in PARAMS], 1)),
        "w1T": np.ascontiguousarray(a["L3_gnn_w1"].T), "w2T": np.ascontiguousarray(a["L3_gnn_w2"].T),
        "b1": a["L3_gnn_b1"].reshape(2 * D, 1), "compT": np.ascontiguousarray(a["L0_gnn_comp"].T),
        "basis": a["L0_gnn_basis"].reshape(BASES, D * D), "normt": a["node_vec1"].reshape(1, N),
    })
    nc = bacc.Bacc("TRN2", target_bir_lowering=False, num_devices=1)
    handles = {n: nc.dram_tensor("in_" + n, v.shape, mybir.dt.from_np(v.dtype), kind="ExternalInput").ap()
               for n, v in arrays.items()}
    out = nc.dram_tensor("out", (N, D), f32, kind="ExternalOutput").ap()
    build(nc, handles, out, "all")
    r = run_bass_kernel_spmd(nc, [{"in_" + n: v for n, v in arrays.items()}], core_ids=[0])
    return r.results[0]["out"]
```

```python
from contextlib import ExitStack

import concourse.bass as bass
from concourse import mybir

N = 3125
D = 64
E = 100000
R = 12
BASES = 30
P = 128
NB = (N + P - 1) // P
NP = NB * P
ET = 125
IT = E // ET
GT = 20
IG = IT // GT
GE = GT * ET
BINS = NB * NB
NT = 1408
TC = NT // P
TRASH = 4
EPS = 1e-5
BANK = 512
CH = [(c * BANK, min(BANK, NP - c * BANK)) for c in range((NP + BANK - 1) // BANK)]

ALU = mybir.AluOpType
ACT = mybir.ActivationFunctionType
AX = mybir.AxisListType
f32, bf16, f16 = mybir.dt.float32, mybir.dt.bfloat16, mybir.dt.float16
i32, i16 = mybir.dt.int32, mybir.dt.int16


H = 4
M = NT // H
HE = H * P
ALL = E + N
A_ROWS = (NB + TRASH) * P
PARAMS = ["L0_gnn_bias", "L1_gnn_b_unite", "L1_gnn_g1", "L1_gnn_be1", "L1_gnn_b_gconv", "L1_gnn_g2",
          "L1_gnn_be2", "L1_gnn_b_transfer", "L1_gnn_b_lin", "L1_gnn_g3", "L1_gnn_be3", "L3_gnn_b2"]
WEIGHTS = ["root", "unite_x", "unite_d", "gconv_h", "gconv_m", "transfer_h", "transfer_a", "lin",
           "W1_out", "W1_back", "W2_out", "W2_back", "gconv_hT"]

STEPS = {
    "vector": (
        "key", "rowtot", "bins", "based", "scat_seen", "tab_c", "fields", "consts2", "zerob", "xpad", "inv",
        "acc0N", "i0_sb", "acc0T", "ln0_in", "ln0_sq", "ln0", "x1", "dsum", "odeg_rep", "o0_sb", "P_sb",
        "Q_sb", "DT_sb", "bn1_var", "PQ", "hsN", "s", "sT", "msg", "R_sb", "sW_sb", "gram_sb", "GW_sb",
        "bn2_var", "diag2", "RT", "wc2", "h2", "accdN", "agg", "bnt_var", "bnt", "bnl_var", "bnl", "ln1_in",
        "ln1_sq", "ln1", "deg1", "bnh0_var", "bnh0", "agg2", "agg3", "bnh1_var", "bnh1", "agg4", "agg5",
        "ln2_in", "ln2_sq", "ln2", "m3", "h128", "ln3_in", "ln3_sq", "ln3",),
    "scalar": (
        "x1N", "PN", "QN", "RN", "deg_sqrt", "hN0", "hN1", "x3N", "outN",),
    "tensor": (
        "cnt", "acc0", "i0_ps", "acc0_ps", "root_ps", "ln0_mean", "ln0_var", "x1N_ps", "o0_ps", "P_ps",
        "Q_ps", "DT_ps", "PN_ps", "QN_ps", "accb", "s_ps", "R_ps", "sW_ps", "GW_ps", "Mc_ps", "wc2_ps",
        "RN_ps", "h2_ps", "accd", "accd_ps", "t_ps", "lin_ps", "ln1_mean", "ln1_var", "hN0_ps", "y1_ps",
        "hN1_ps", "y2_ps", "ln2_mean", "ln2_var", "x3N_ps", "h128_ps", "up_ps", "ln3_mean", "ln3_var",
        "outN_ps",),
}


def wait_count(eng, sem, n):
    if not isinstance(n, int) or n > 0:
        eng.wait_ge(sem, n)


def stage_of(i, b, lag):
    n = 4 * i + b - lag
    if isinstance(n, int) and not 0 <= n < M:
        return None, 0, 0
    return n, (b - lag) % 4, i - (1 if b < lag else 0)


def half_rounds(eng, body, last):
    for b in range(4):
        body(0, b)
    with eng.Fori(1, M // 4) as i:
        for b in range(4):
            body(i, b)
    for b in range(last):
        body(M // 4, b)


class Region:

    def __init__(self, tensor):
        self.tensor, self.at = tensor, 0

    def take(self, parts, cols, dt=f32):
        words = cols if dt in (f32, i32) else (cols + 1) // 2
        ap = self.tensor[0:parts, self.at:self.at + words]
        self.at += words
        assert self.at <= self.tensor.shape[1], (self.at, self.tensor.shape)
        return ap if dt == f32 else ap.bitcast(dt)

    def reset(self):
        self.at = 0


def build(nc, A, out, stage):
    ctx = ExitStack()
    with ctx:
        def sb(name, shape, dt=f32):
            return ctx.enter_context(nc.sbuf_tensor(name, shape, dt))

        def dram(name, shape, dt=f32):
            return nc.dram_tensor(name, shape, dt, kind="Internal").ap()

        named = {}

        def S(name):
            if name not in named:
                named[name] = ctx.enter_context(nc.semaphore(name))
            return named[name]

        passed = {k: 0 for k in STEPS}

        def now(name):
            for eng, names in STEPS.items():
                if name in names:
                    assert names.index(name) == passed[eng], name
                    passed[eng] += 1
                    return S(eng + "_steps"), 1
            return S(name), 1

        def after(eng, name):
            for e, names in STEPS.items():
                if name in names:
                    eng.wait_ge(S(e + "_steps"), names.index(name) + 1)
                    return
            eng.wait_ge(S(name), 1)

        slots = dram("slots", [P * NT, 4], i32)
        keyrow_d = dram("keyrow_d", [IT, ET], f16)
        dbrow_d = dram("dbrow_d", [IT, ET], bf16)
        bins_d = dram("bins_d", [1, BINS])
        tab_d = dram("tab_d", [4, NT], i16)
        same_d = dram("same_d", [1, NT])
        slrow_d = dram("slrow_d", [NT, P], bf16)
        dlrow_d = dram("dlrow_d", [NT, P], bf16)
        A_sd = dram("A_sd", [A_ROWS, NP])
        A_ds = dram("A_ds", [A_ROWS, NP])
        w_d = dram("w_d", [R, D * D])
        h_d = dram("h_d", [M * P, H * D])
        y_d = dram("y_d", [NP, R * D])

        F = sb("F", [P, 6 * NP + 960])
        WK = sb("WK", [P, 8192])
        RW = sb("RW", [P, 6400])
        NR = sb("NR", [P, 4800])
        ident = sb("ident", [P, P])
        iota = sb("iota", [P, P])
        iotab = sb("iotab", [P, P], bf16)
        pcol = sb("pcol", [P, 1])
        tri = sb("tri", [P, P])
        ones = sb("ones", [P, P])
        triT = sb("triT", [P, P])
        slf = sb("slf", [P, NT])
        dlf = sb("dlf", [P, NT])
        tab = sb("tab", [1, NT * 4], i16)
        small = sb("small", [P, 1800])
        gate = sb("gate", [1, 4])
        cnt = sb("cnt", [P, NB * 16])
        inv = sb("inv", [P, NB * 16])
        odeg = sb("odeg", [P, NB])
        zerob = sb("zerob", [P, BANK], bf16)
        wts = sb("wts", [D, len(WEIGHTS), D])
        prm = sb("prm", [D, len(PARAMS)])
        w1T = sb("w1T", [D, 2 * D])
        w2T = sb("w2T", [2 * D, D])
        b1c = sb("b1c", [2 * D, 1])
        mean64 = sb("mean64", [D, D])
        cols = sb("cols", [D, 32])
        m64 = sb("m64", [D, 4 * D])
        epsc = sb("epsc", [D, 1])
        xs = sb("xs", [P, 2, D])
        ps = ctx.enter_context(nc.psum_tensor("ps", [P, 8, BANK], f32))

        rn, rr, rw = Region(NR), Region(RW), Region(WK)
        src_c, dst_c, typ_c = (rn.take(ET, IT, i32) for _ in range(3))
        dbf, sbf, key = (rn.take(ET, IT) for _ in range(3))
        C = F[0:NB, 0:(IT + 1) * NB].rearrange("p (t s) -> p t s", s=NB)
        krow = rr.take(ET, 2 * GE, f16).rearrange("p (b n) -> p b n", b=2)
        drow = rr.take(NB, 2 * GE, bf16).rearrange("p (b n) -> p b n", b=2)
        ohS = rr.take(ET, 2 * GT * NB, bf16).rearrange("p (b t s) -> p b t s", b=2, s=NB)
        ohD = rr.take(ET, 2 * GT * NB, bf16).rearrange("p (b t s) -> p b t s", b=2, s=NB)
        ohT = rw.take(NB, 2 * GE).rearrange("p (b n) -> p b n", b=2)
        cg = rw.take(NB, 2 * GT * NB).rearrange("p (b n) -> p b n", b=2)
        sm = Region(small)
        sel3 = sm.take(ET, GT * NB).rearrange("p (t s) -> p t s", s=NB)
        base_e = sm.take(ET, GT)
        rank = sm.take(ET, GT)
        posi = sm.take(ET, 3 * GT, i32).rearrange("p (k n) -> p k n", k=3)
        posf = sm.take(ET, GT)
        idx = sm.take(ET, 2 * GT, i32).rearrange("p (b n) -> p b n", b=2)
        rec = sm.take(ET, 2 * GT * 4, i32).rearrange("p (b n k) -> p b n k", b=2, k=4)
        junk2 = rw.take(ET, 2 * ET).rearrange("p (b e) -> p b e", b=2)
        kk = sm.take(ET, GT)
        zk = sm.take(ET, GT)
        tot = sm.take(NB, NB)
        toti = sm.take(NB, NB, i32)
        toti2 = sm.take(NB, NB, i32)
        tri4 = sm.take(P, TC, i32)
        tri4b = sm.take(P, TC, i32)
        nt_f = sm.take(NB, NB)
        incl = sm.take(NB, NB)
        one25 = sm.take(NB, NB)
        roff = sm.take(NB, 1)
        binrow = WK[:, 0:BINS]
        tcol = sm.take(P, 3 * TC)
        kcol = sm.take(P, 3 * TC)
        tmp24 = sm.take(P, NB)
        dbc = sm.take(P, TC)
        sbc = sm.take(P, TC)
        fin = sm.take(P, TC)
        tr4 = sm.take(P, TC)
        tabc = sm.take(P, TC * 4, i16).rearrange("p (k c) -> p k c", k=4)
        edge25 = sm.take(P, NB)
        samec = sm.take(P, TC)
        binjunk = WK[:, 640:640 + BINS]
        slot_i = F[:, 0:NT * 4].bitcast(i32).rearrange("p (t k) -> p t k", k=4)
        rowst = F[:, NT * 4:NT * 4 + TC * P].bitcast(bf16).rearrange("p (k c e) -> p k c e", k=2, e=P)
        tyf, same, yidx = NR[:, 0:NT], NR[:, NT:2 * NT], NR[:, 2 * NT:3 * NT].bitcast(i32)
        fill = F[:, 0:NT * 4].bitcast(i32)

        keyst = WK[0:IT // 8, 0:8 * ET // 2 + 4].bitcast(f16)[:, 0:8 * ET].rearrange("r (c e) -> r c e", c=8)
        dbst = WK[0:IT // 8, 1024:1024 + 8 * ET // 2 + 4].bitcast(bf16)[:, 0:8 * ET].rearrange("r (c e) -> r c e", c=8)
        rows8 = IT // 8

        posA = F[0:ET, NT * 4:NT * 4 + 2 * IT].bitcast(i32).rearrange("p (k n) -> p k n", k=2)

        ring = Region(WK)
        b_oS = ring.take(P, 2 * HE).rearrange("p (b n) -> p b n", b=2)
        b_oD = ring.take(P, 4 * HE).rearrange("p (b n) -> p b n", b=4)
        b_acc = ring.take(P, 4 * 2 * P).rearrange("p (b n) -> p b n", b=4)
        b_same = ring.take(P, 2 * H).rearrange("p (b k) -> p b k", b=2)
        l_row = ring.take(P, 2 * HE, bf16).rearrange("p (b n) -> p b n", b=2)
        l_oDT = ring.take(P, 2 * HE).rearrange("p (b n) -> p b n", b=2)
        l_y = ring.take(P, 4 * H * D).rearrange("p (b k n) -> p b k n", b=4, k=H)
        l_ys = ring.take(P, 2 * H * D).rearrange("p (b k n) -> p b k n", b=2, k=H)
        l_idx = ring.take(P, 4 * H, i32).rearrange("p (b k) -> p b k", b=4)
        l_w = ring.take(P, 2 * H).rearrange("p (b k) -> p b k", b=2)
        l_oT = ring.take(P, 2 * H * R).rearrange("p (b k r) -> p b k r", b=2, k=H)
        l_g = ring.take(P, H * R).rearrange("p (k r) -> p k r", k=H)
        c_oD = b_oS[:, :, :].bitcast(bf16)
        c_oT = b_oD[:, 0:2, 0:H * R].bitcast(bf16)
        ring.reset()
        e_drow = ring.take(P, 2 * HE, bf16).rearrange("p (b n) -> p b n", b=2)
        e_oDT = ring.take(P, 4 * HE).rearrange("p (b n) -> p b n", b=4)
        e_o = ring.take(P, 4 * HE).rearrange("p (b n) -> p b n", b=4)
        e_h = ring.take(P, 4 * H * D).rearrange("p (b n) -> p b n", b=4)
        both = ring.at
        e_srow = ring.take(P, 2 * HE, bf16).rearrange("p (b n) -> p b n", b=2)
        e_oST = ring.take(P, 2 * HE).rearrange("p (b n) -> p b n", b=2)
        ring.at = both
        e_h2 = ring.take(P, 2 * H * D).rearrange("p (b n) -> p b n", b=2)
        e_hT = ring.take(D, 2 * HE).rearrange("p (b n) -> p b n", b=2)
        arow = WK[:, 0:2 * NP].rearrange("p (b n) -> p b n", b=2)
        FT = [F[0:D, k * NP:(k + 1) * NP] for k in range(6)]
        h128 = F[:, 2 * NP:3 * NP]
        Wsb = F[0:R, 2 * NP:2 * NP + D * D]
        Wall = F[0:D, 4 * NP:4 * NP + R * D].rearrange("p (r o) -> p r o", r=R)
        ystg = F[:, 4 * NP + R * D:4 * NP + 3 * R * D].rearrange("p (b n) -> p b n", b=2)
        compT = F[0:BASES, 3 * NP:3 * NP + R]
        basis = F[0:BASES, 3 * NP + R:3 * NP + R + D * D]
        i0row, o0row = RW[0:D, 0:NP], RW[0:D, NP:2 * NP]
        sm25 = tmp24
        NT_ = [NR[:, k * NB * D:(k + 1) * NB * D] for k in range(3)]
        psF = ps[0:D, 0:7, :].rearrange("p b n -> p (b n)")[:, 0:NP]
        psH = ps[:, 0:7, :].rearrange("p b n -> p (b n)")[:, 0:NP]
        psN = ps[:, 0:4, :].rearrange("p b n -> p (b n)")[:, 0:NB * D]
        wt = {n: wts[:, k, :] for k, n in enumerate(WEIGHTS)}
        pr = {n: prm[:, k:k + 1] for k, n in enumerate(PARAMS)}
        gram_sb, gw_sb, diag2, wc2 = (m64[:, k * D:(k + 1) * D] for k in range(4))
        PAD = slice(N, NP)

        def blocks_of(eng, n, which, most=NB - 1):
            return nc.values_load_multi_w_load_instructions(
                tab[0:1, bass.ds(n * H + which * NT, H)], engines=[eng.engine], min_val=0, max_val=most,
                skip_runtime_bounds_check_because="the kernel worked the table out itself")[1]

        block = ctx.enter_context(nc.Block())

        @block.gpsimd
        def _(pool):
            def link(ins):
                links[0] += 1
                ins.then_inc(S("pool_link"), 1)
                pool.wait_ge(S("pool_link"), links[0])
            links = [0]
            nc.gpsimd.iota(iota[:], pattern=[[1, P]], base=0, channel_multiplier=0,
                           allow_small_or_imprecise_dtypes=True).then_inc(S("const"), 1)
            nc.gpsimd.iota(pcol[:], pattern=[[0, 1]], base=0, channel_multiplier=1,
                           allow_small_or_imprecise_dtypes=True).then_inc(S("const"), 1)
            nc.gpsimd.iota(tcol[:, 0:TC], pattern=[[P, TC]], base=0, channel_multiplier=1,
                           allow_small_or_imprecise_dtypes=True).then_inc(S("const"), 1)
            nc.gpsimd.iota(edge25[:], pattern=[[NB, NB]], base=0, channel_multiplier=0,
                           allow_small_or_imprecise_dtypes=True).then_inc(S("const"), 1)
            nc.gpsimd.memset(ones[:], 1.0).then_inc(S("ones"), 1)
            nc.gpsimd.memset(gate[:], 0.0).then_inc(S("gate"), 1)
            after(pool, "ones")
            nc.gpsimd.affine_select(out=tri[:], in_=ones[:], compare_op=ALU.is_gt, fill=0.0, base=0,
                                    pattern=[[-1, P]], channel_multiplier=1).then_inc(S("tri"), 1)
            nc.gpsimd.affine_select(out=triT[:], in_=ones[:], compare_op=ALU.is_gt, fill=0.0, base=0,
                                    pattern=[[1, P]], channel_multiplier=-1).then_inc(S("tri"), 1)
            nc.gpsimd.affine_select(out=ident[:], in_=ones[:], compare_op=ALU.is_equal, fill=0.0, base=0,
                                    pattern=[[-1, P]], channel_multiplier=1).then_inc(S("ident"), 1)
            pool.wait_ge(S("filled"), 16)
            after(pool, "gate")
            with pool.Fori(0, IG // 2) as i:
                for b in range(2):
                    pool.wait_ge(S("idx_ready"), i * 2 + b + 1)
                    pool.wait_ge(S("gate"), i * 2 + b + 1)
                    nc.gpsimd.tensor_tensor(gate[0:1, 0:1], gate[0:1, 1:2], gate[0:1, 2:3],
                                            ALU.add).then_inc(S("gate"), 1)
                    for k in range(GT):
                        nc.gpsimd.indirect_dma_start(
                            out=slots, out_offset=bass.IndirectOffsetOnAxis(ap=idx[:, b, k:k + 1], axis=0),
                            in_=rec[:, b, k, :], in_offset=None).then_inc(S(f"scattered{b}"), 16)
            if stage == "A":
                return
            pool.wait_ge(S("y_out0"), 16 * 13)
            pool.wait_ge(S("y_out1"), 16 * 12)
            table = y_d.rearrange("n (r o) -> (n r) o", r=R)
            sorted_gates = IG

            def gather(i, b):
                n, slot, _ = stage_of(i, b, 0)
                wait_count(pool, S("l0_ys"), n - 3)
                pool.wait_ge(S("l0_idx"), n + 1)
                pool.wait_ge(S("gate"), sorted_gates + n + 1)
                nc.gpsimd.tensor_tensor(gate[0:1, 0:1], gate[0:1, 1:2], gate[0:1, 2:3],
                                        ALU.add).then_inc(S("gate"), 1)
                for k in range(H):
                    nc.gpsimd.indirect_dma_start(
                        out=l_y[:, slot, k, :], out_offset=None, in_=table,
                        in_offset=bass.IndirectOffsetOnAxis(ap=l_idx[:, slot, k:k + 1], axis=0)).then_inc(S(f"l0_y{slot}"), 16)
            half_rounds(pool, gather, 0)

        @block.sync
        def _(sp):
            sp.dma_start(src_c, A["src_c"]).then_inc(S("ids"), 16)
            for ap, name in ((wts[:], "weights"), (prm[:], "params"), (w1T[:], "w1T"), (w2T[:], "w2T"), (b1c[:], "b1")):
                sp.dma_start(ap, A[name]).then_inc(S("wts_in"), 16)
            sp.dma_start(dst_c, A["dst_c"]).then_inc(S("ids"), 16)
            sp.dma_start(typ_c, A["typ_c"]).then_inc(S("ids"), 16)
            after(sp, "fill_set")
            sp.dma_start(slots.rearrange("(p t) k -> p (t k)", p=P), fill).then_inc(S("filled"), 16)
            sp.wait_ge(S("rows_t"), 2 * 8)
            rows = IT // 8
            sp.dma_start(keyrow_d.rearrange("(c r) e -> r c e", r=rows), keyst).then_inc(S("rows_out"), 16)
            sp.dma_start(dbrow_d.rearrange("(c r) e -> r c e", r=rows), dbst).then_inc(S("rows_out"), 16)
            sp.wait_ge(S("rows_out"), 32)
            kd = keyrow_d.rearrange("t e -> (t e)").rearrange("(o n) -> o n", o=1)
            dd = dbrow_d.rearrange("t e -> (t e)").rearrange("(o n) -> o n", o=1)
            for b in range(2):
                sp.dma_start(krow[:, b, :], kd[:, b * GE:(b + 1) * GE].to_broadcast([ET, GE])).then_inc(S(f"krow{b}"), 16)
                sp.dma_start(drow[:, b, :], dd[:, b * GE:(b + 1) * GE].to_broadcast([NB, GE])).then_inc(S(f"krow{b}"), 16)
            with sp.Fori(1, IG // 2) as i:
                for b in range(2):
                    sp.wait_ge(S("idx_ready"), i * 2 + b - 1)
                    sp.dma_start(krow[:, b, :], kd[:, bass.ds((i * 2 + b) * GE, GE)].to_broadcast([ET, GE])).then_inc(S(f"krow{b}"), 16)
                    sp.dma_start(drow[:, b, :], dd[:, bass.ds((i * 2 + b) * GE, GE)].to_broadcast([NB, GE])).then_inc(S(f"krow{b}"), 16)
            after(sp, "bins")
            sp.dma_start(bins_d.rearrange("o (p s) -> (o p) s", s=NB), incl).then_inc(S("bins_out"), 16)
            sp.wait_ge(S("bins_out"), 16)
            after(sp, "scat_seen")
            sp.dma_start(binrow, bins_d.to_broadcast([P, BINS])).then_inc(S("binrow"), 16)
            sp.dma_start(F[:, 0:NT * 4].bitcast(i32), slots.rearrange("(p t) k -> p (t k)", p=P)).then_inc(S("slots_in"), 16)
            after(sp, "tab_c")
            with nc.allow_non_contiguous_dma(reason="one small table"):
                sp.dma_start(tab_d.rearrange("k (c p) -> p k c", p=P), tabc).then_inc(S("tab_out"), 16)
                sp.dma_start(same_d.rearrange("o (c p) -> p (o c)", p=P), samec).then_inc(S("tab_out"), 16)
            sp.wait_ge(S("tab_out"), 32)
            sp.dma_start(tab[:], tab_d.rearrange("k t -> (k t)").rearrange("(o n) -> o n", o=1)).then_inc(S("tab_in"), 16)
            sp.dma_start(same, same_d.to_broadcast([P, NT])).then_inc(S("tab_in"), 16)
            after(sp, "rows_s")
            sp.dma_start(slrow_d.rearrange("(c p) e -> p c e", p=P), rowst[:, 0]).then_inc(S("slrow_out"), 16)
            sp.dma_start(dlrow_d.rearrange("(c p) e -> p c e", p=P), rowst[:, 1]).then_inc(S("slrow_out"), 16)
            sp.wait_ge(S("slrow_out"), 32)
            after(sp, "fields")
            after(sp, "rows_s")
            sp.dma_start(compT, A["compT"]).then_inc(S("basis_in"), 16)
            sp.dma_start(basis, A["basis"]).then_inc(S("basis_in"), 16)
            sp.dma_start(FT[0][:, 0:N], A["xT"]).then_inc(S("xT_in"), 16)
            sp.wait_ge(S("W_sb"), 2)
            sp.dma_start(w_d, Wsb).then_inc(S("W_out"), 16)
            sp.wait_ge(S("W_out"), 16)
            with nc.allow_non_contiguous_dma(reason="rows of one relation"):
                sp.dma_start(Wall, w_d.rearrange("r (i o) -> i r o", i=D)).then_inc(S("W_in"), 16)
            for k in range(NB):
                sp.wait_ge(S("y_v"), k + 1)
                sp.wait_ge(S("y_a"), k + 1)
                sp.dma_start(y_d[k * P:(k + 1) * P, :], ystg[:, k % 2, :]).then_inc(S(f"y_out{k % 2}"), 16)

            srows = slrow_d.rearrange("t e -> (t e)").rearrange("(o n) -> o n", o=1)
            drows = dlrow_d.rearrange("t e -> (t e)").rearrange("(o n) -> o n", o=1)

            def put(i, b):
                n = 4 * i + b
                if stage_of(i, b, 0)[0] is not None:
                    wait_count(sp, S("l0_tr"), n - 1)
                    sp.dma_start(l_row[:, b % 2, :], drows[:, bass.ds(n * HE, HE)].to_broadcast([P, HE])).then_inc(S(f"l0_row{b % 2}"), 16)
                n, _, _ = stage_of(i, b, 1)
                if n is None:
                    return
                rows, cols_ = blocks_of(sp, n, 2, NB + TRASH - 1), blocks_of(sp, n, 0)
                for k in range(H):
                    sp.wait_ge(S("bl_acc"), n * H + k + 1)
                    sp.dma_start(A_sd[bass.ds(rows[k] * P, P), bass.ds(cols_[k] * P, P)], b_acc[:, k, 0:P]).then_inc(S(f"bl_out{k}"), 16)
            half_rounds(sp, put, 1)


            def product_rows(q, adj):
                for b in range(2):
                    wait_count(sp, S("pr_mm"), q * NB)
                    if q < 3:
                        sp.wait_ge(S(("l0_sc", "b_sc", "d_sc")[q]), M)
                    sp.dma_start(arow[:, b, :], adj[b * P:(b + 1) * P, :]).then_inc(S(f"arow{b}"), 16)
                with sp.Fori(1, NB // 2) as i:
                    for b in range(2):
                        sp.wait_ge(S("pr_mm"), q * NB + i * 2 + b - 1)
                        if q == 0:
                            sp.wait_ge(S("odeg"), i * 2 + b - 1)
                        sp.dma_start(arow[:, b, :], adj[bass.ds((i * 2 + b) * P, P), :]).then_inc(S(f"arow{b}"), 16)
                sp.wait_ge(S("pr_mm"), q * NB + NB - 2)
                if q == 0:
                    sp.wait_ge(S("odeg"), NB - 2)
                sp.dma_start(arow[:, 0, :], adj[(NB - 1) * P:NB * P, :]).then_inc(S("arow0"), 16)

            def edge_rows(p):
                def body(i, b):
                    n = 4 * i + b
                    wait_count(sp, S(p + "_tr"), n - 1)
                    sp.dma_start(e_drow[:, b % 2, :], drows[:, bass.ds(n * HE, HE)].to_broadcast([P, HE])).then_inc(S(f"{p}_row{b % 2}"), 16)
                    if p == "b":
                        sp.dma_start(e_srow[:, b % 2, :], srows[:, bass.ds(n * HE, HE)].to_broadcast([P, HE])).then_inc(S(f"{p}_row{b % 2}"), 16)
                    else:
                        wait_count(sp, S("d_T"), n - 3)
                        sp.dma_start(e_h[:, b, :], h_d[bass.ds(n * P, P), :]).then_inc(S(f"d_in{b}"), 16)
                half_rounds(sp, body, 0)
            for k in range(4):
                sp.wait_ge(S(f"bl_out{k}"), M * 32)
            product_rows(0, A_sd)
            sp.wait_ge(S("pr_mm"), NB)
            sp.wait_ge(S("odeg"), NB)
            edge_rows("b")
            for b in range(4):
                sp.wait_ge(S(f"b_out{b}"), M // 4 * 16)
            product_rows(1, A_sd)
            sp.wait_ge(S("pr_mm"), 2 * NB)
            edge_rows("d")
            product_rows(2, A_sd)
            product_rows(3, A_ds)
            sp.dma_start(o0row[:, 0:N], A["normt"].to_broadcast([D, N])).then_inc(S("normt_in"), 16) if False else None
            product_rows(4, A_sd)
            product_rows(5, A_ds)
            product_rows(6, A_sd)
            after(sp, "outN")
            full = N // P
            on = NT_[1].rearrange("p (b d) -> p b d", d=D)
            sp.dma_start(out[0:full * P, :].rearrange("(b p) d -> p b d", p=P), on[:, 0:full, :]).then_inc(S("out"), 16)
            sp.dma_start(out[full * P:N, :], on[0:N - full * P, full, :]).then_inc(S("out"), 16)
            sp.wait_ge(S("out"), 32)

        @block.vector
        def _(dve):
            links = [0]

            def link(ins):
                links[0] += 1
                ins.then_inc(S("dve_link"), 1)
                dve.wait_ge(S("dve_link"), links[0])

            def mark(ins, name):
                ins.then_inc(*now(name))
                after(dve, name)

            V = nc.vector
            V.memset(fill, -1).then_inc(S("fill_set"), 1)
            dve.wait_ge(S("const"), 4)
            link(V.tensor_copy(iotab[:], iota[:]))
            dve.wait_ge(S("ids"), 48)
            link(V.tensor_single_scalar(posA[:, 0], dst_c, 7, op=ALU.arith_shift_right))
            link(V.tensor_single_scalar(posA[:, 1], src_c, 7, op=ALU.arith_shift_right))
            link(V.tensor_copy(dbf, posA[:, 0]))
            link(V.tensor_copy(sbf, posA[:, 1]))
            mark(V.scalar_tensor_tensor(out=key, in0=dbf, scalar=32.0, in1=sbf, op0=ALU.mult, op1=ALU.add), "key")
            for n, (st, dt) in enumerate(((keyst, f16), (dbst, bf16))):
                for c in range(8):
                    dve.wait_ge(S("row_tr"), n * 8 + c + 1)
                    V.tensor_copy(st[:, c, :], ps[0:rows8, c % 2, 0:ET]).then_inc(S("rows_t"), 1)
            def onehots(b, g):
                gs = bass.ds(g * GT, GT)
                V.tensor_tensor(ohD[:, b], dbf[:, gs].unsqueeze(2).to_broadcast([ET, GT, NB]),
                                iota[0:ET, 0:NB].unsqueeze(1).to_broadcast([ET, GT, NB]), ALU.is_equal)
                return V.tensor_tensor(ohS[:, b], sbf[:, gs].unsqueeze(2).to_broadcast([ET, GT, NB]),
                                       iota[0:ET, 0:NB].unsqueeze(1).to_broadcast([ET, GT, NB]), ALU.is_equal)
            for b in range(2):
                onehots(b, b).then_inc(S("oh"), 1)
            with dve.Fori(1, IG // 2) as i:
                for b in range(2):
                    g = i * 2 + b
                    dve.wait_ge(S("counted"), g - 1)
                    onehots(b, g).then_inc(S("oh"), 1)
            dve.wait_ge(S("C_in"), IG)
            dve.wait_ge(S("filled"), 16)
            link(V.memset(C[:, 0, :], 0.0))
            zero = WK[0:NB, 2000:2000 + IT]
            link(V.memset(zero, 0.0))
            for s in range(NB):
                last = V.tensor_tensor_scan(C[:, 1:IT + 1, s], C[:, 1:IT + 1, s], zero, 0.0, ALU.add, ALU.add)
                link(last)
            link(V.tensor_scalar(toti, C[:, IT, :], float(P - 1), None, ALU.add))
            link(V.tensor_single_scalar(toti2, toti, 7, op=ALU.arith_shift_right))
            link(V.tensor_scalar(nt_f, toti2, 1.0, None, ALU.max))
            link(V.memset(one25, 0.0))
            mark(V.tensor_tensor_scan(incl, nt_f, one25, 0.0, ALU.add, ALU.add), "rowtot")
            after(dve, "roff")
            link(V.tensor_copy(roff, ps[0:NB, 4, 0:1]))
            link(V.tensor_tensor(incl, incl, nt_f, ALU.subtract))
            mark(V.tensor_scalar(incl, incl, roff, None, ALU.add), "bins")
            link(V.tensor_scalar(tot, incl, float(P), None, ALU.mult))
            mark(V.tensor_tensor(C[:, 0:IT, :], C[:, 0:IT, :], tot.unsqueeze(1).to_broadcast([NB, IT, NB]), ALU.add), "based")
            dve.wait_ge(S("tri"), 2)

            def lookup(b, g, first):
                gs = bass.ds(g * GT, GT)
                q = (g - b) // 2 if isinstance(g, int) else None
                n = g + 1
                dve.wait_ge(S(f"krow{b}"), (half(g, b) + 1) * 32)
                if not first:
                    dve.wait_ge(S("looked"), g - 1)
                V.tensor_scalar(ohT[:, b, :], drow[:, b, :], pcol[0:NB, :], None, ALU.is_equal).then_inc(S("ohT"), 1)
                V.tensor_tensor(ohS[:, b], sbf[:, gs].unsqueeze(2).to_broadcast([ET, GT, NB]),
                                iota[0:ET, 0:NB].unsqueeze(1).to_broadcast([ET, GT, NB]), ALU.is_equal)
                V.tensor_tensor(kk, key[:, gs], zk, ALU.add).then_inc(S("kk"), 1)
                dve.wait_ge(S("kk"), n)
                for k in range(GT):
                    last = V.scalar_tensor_tensor(out=junk2[:, k % 2, :], in0=krow[:, b, k * ET:(k + 1) * ET], scalar=kk[:, k:k + 1],
                                                  in1=tri[0:ET, 0:ET], op0=ALU.is_equal, op1=ALU.mult,
                                                  accum_out=rank[:, k:k + 1])
                    last.then_inc(S("ranked"), 1)
                    dve.wait_ge(S("ranked"), g * GT + k + 1)
                dve.wait_ge(S("looked"), n)
                V.tensor_tensor(sel3, ps[0:ET, 5 + b, 0:GT * NB].rearrange("p (t s) -> p t s", s=NB), ohS[:, b], ALU.mult).then_inc(S("selected"), 1)
                dve.wait_ge(S("selected"), n)
                V.tensor_reduce(base_e, sel3, AX.X, ALU.add).then_inc(S("reduced"), 1)
                dve.wait_ge(S("reduced"), n)
                steps = [0]

                def step(ins):
                    steps[0] += 1
                    ins.then_inc(S("pos_step"), 1)
                    dve.wait_ge(S("pos_step"), g * 5 + steps[0])
                step(V.tensor_tensor(posi[:, 0], base_e, rank, ALU.add))
                step(V.tensor_single_scalar(posi[:, 1], posi[:, 0], 7, op=ALU.arith_shift_right))
                step(V.tensor_single_scalar(posi[:, 2], posi[:, 0], P - 1, op=ALU.bitwise_and))
                step(V.tensor_copy(posf, posi[:, 1]))
                if not first:
                    dve.wait_ge(S(f"scattered{b}"), half(g, b) * (16 * GT))
                V.tensor_single_scalar(rec[:, b, :, 1], src_c[:, gs], P - 1, op=ALU.bitwise_and)
                V.tensor_single_scalar(rec[:, b, :, 2], dst_c[:, gs], P - 1, op=ALU.bitwise_and)
                V.tensor_scalar(rec[:, b, :, 3], typ_c[:, gs], 0.0, None, ALU.add)
                step(V.scalar_tensor_tensor(out=rec[:, b, :, 0], in0=src_c[:, gs], scalar=float(R), in1=typ_c[:, gs], op0=ALU.mult, op1=ALU.add))
                V.scalar_tensor_tensor(out=idx[:, b, :], in0=posi[:, 2], scalar=float(NT), in1=posf, op0=ALU.mult, op1=ALU.add).then_inc(S("idx_ready"), 1)
                dve.wait_ge(S("idx_ready"), n)

            def half(g, b):
                return hb[0]
            hb = [0]
            link(V.memset(zk, 0.0))
            for b in range(2):
                lookup(b, b, True)
            with dve.Fori(1, IG // 2) as i:
                for b in range(2):
                    hb[0] = i
                    lookup(b, i * 2 + b, False)
            for b in range(2):
                dve.wait_ge(S(f"scattered{b}"), IG // 2 * 16 * GT)
            mark(V.memset(binjunk[:, 0:1], 0.0), "scat_seen")
            link(V.tensor_scalar(tcol[:, TC:2 * TC], tcol[:, 0:TC], -1.0, None, ALU.add))
            link(V.tensor_scalar(tcol[:, 2 * TC:3 * TC], tcol[:, 0:TC], 1.0, None, ALU.add))
            dve.wait_ge(S("binrow"), 16)
            for c in range(3 * TC):
                link(V.tensor_scalar(binjunk, binrow, tcol[:, c:c + 1], 0.0, ALU.is_le, ALU.add, accum_out=kcol[:, c:c + 1]))
            link(V.tensor_scalar(kcol, kcol, -1.0, None, ALU.add))
            for c in range(TC):
                link(V.tensor_scalar(tmp24, edge25, kcol[:, c:c + 1], 0.0, ALU.is_le, ALU.add, accum_out=dbc[:, c:c + 1]))
            link(V.tensor_scalar(dbc, dbc, -1.0, None, ALU.add))
            link(V.scalar_tensor_tensor(out=sbc, in0=dbc, scalar=-float(NB), in1=kcol[:, 0:TC], op0=ALU.mult, op1=ALU.add))
            link(V.tensor_tensor(samec, kcol[:, 0:TC], kcol[:, TC:2 * TC], ALU.is_equal))
            link(V.tensor_scalar(tmp24[:, 0:TC], tcol[:, 0:TC], float(NT - 1), None, ALU.is_equal))
            link(V.tensor_tensor(kcol[:, 2 * TC:3 * TC], kcol[:, 2 * TC:3 * TC], tmp24[:, 0:TC], ALU.add))
            link(V.tensor_tensor(fin, kcol[:, 0:TC], kcol[:, 2 * TC:3 * TC], ALU.not_equal))
            link(V.tensor_copy(tri4, tcol[:, 0:TC]))
            link(V.tensor_single_scalar(tri4b, tri4, TRASH - 1, op=ALU.bitwise_and))
            link(V.tensor_scalar(tr4, tri4b, float(NB), None, ALU.add))
            link(V.tensor_copy(tabc[:, 0], dbc))
            link(V.tensor_copy(tabc[:, 1], sbc))
            for k, blk in ((2, sbc), (3, dbc)):
                link(V.tensor_tensor(tmp24[:, 0:TC], blk, tr4, ALU.subtract))
                link(V.tensor_tensor(tmp24[:, 0:TC], tmp24[:, 0:TC], fin, ALU.mult))
                ins = V.tensor_tensor(tabc[:, k], tmp24[:, 0:TC], tr4, ALU.add)
                link(ins) if k == 2 else mark(ins, "tab_c")
            dve.wait_ge(S("slots_in"), 16)
            link(V.tensor_copy(slf[:], slot_i[:, :, 1]))
            link(V.tensor_copy(tyf, slot_i[:, :, 3]))
            link(V.tensor_scalar(yidx, slot_i[:, :, 0], 0.0, None, ALU.max))
            mark(V.tensor_copy(dlf[:], slot_i[:, :, 2]), "fields")
            for n in range(2):
                for c in range(TC):
                    dve.wait_ge(S("slot_tr"), n * TC + c + 1)
                    ins = V.tensor_copy(rowst[:, n, c, :], ps[:, (n * TC + c) % 2, 0:P])
                    ins.then_inc(S("slot_cp"), 1)
            dve.wait_ge(S("slot_cp"), 2 * TC)
            V.memset(binjunk[:, 0:1], 0.0).then_inc(S("rows_s"), 1)
            link(V.memset(epsc[:], EPS))
            dve.wait_ge(S("slrow_out"), 32)
            mark(V.memset(mean64[:], 1.0 / D), "consts2")
            mark(V.memset(zerob[:], 0.0), "zerob")
            after(dve, "rows_s")
            dve.wait_ge(S("tab_in"), 32)
            mark(V.memset(FT[0][:, PAD], 0.0), "xpad")
            after(dve, "W_ps")
            V.tensor_copy(Wsb[:, 0:4 * BANK], ps[0:R, 0:4, :].rearrange("p b n -> p (b n)")).then_inc(S("W_sb"), 1)
            for k in range(NB):
                dve.wait_ge(S("y_ps"), k + 1)
                if k >= 2:
                    dve.wait_ge(S(f"y_out{k % 2}"), 16 * (k // 2))
                V.tensor_copy(ystg[:, k % 2, 0:R * D // 2], ps[:, 2 * (k % 2), 0:R * D // 2]).then_inc(S("y_v"), 1)

            def onehot(o, column, n, width=P):
                return V.tensor_tensor(o.rearrange("p (k n) -> p k n", k=H), column[:, bass.ds(n * H, H)].unsqueeze(2).to_broadcast([P, H, width]),
                                       iota[:, 0:width].unsqueeze(1).to_broadcast([P, H, width]), ALU.is_equal)

            def counts(i, b):
                n, _, _ = stage_of(i, b, 0)
                wait_count(dve, S("c_mm"), n - 1)
                onehot(c_oD[:, b % 2, 0:HE], dlf, n)
                onehot(c_oT[:, b % 2, 0:H * R], tyf, n, R).then_inc(S("c_oh"), 1)
            half_rounds(dve, counts, 0)
            after(dve, "cnt")
            link(V.tensor_copy(cnt[:], ps[:, 7, 0:NB * 16]))
            link(V.tensor_scalar(inv[:], cnt[:], 1.0, None, ALU.max))
            mark(V.reciprocal(inv[:], inv[:]), "inv")

            def build(i, b):
                n, s4, _ = stage_of(i, b, 0)
                u, u4, _ = stage_of(i, b, 1)

                def running(k):
                    if u is None:
                        return
                    if k % 2 == 0:
                        dve.wait_ge(S("bl_mm"), u * 2 + k // 2 + 1)
                    wait_count(dve, S(f"bl_out{k}"), u * 32)
                    wait_count(dve, S("bl_acc"), u * H + k)
                    V.scalar_tensor_tensor(out=b_acc[:, k, :], in0=b_acc[:, (k - 1) % 4, :], scalar=b_same[:, u4 % 2, k:k + 1],
                                           in1=ps[:, 5 + k // 2, (k % 2) * 2 * P:(k % 2 + 1) * 2 * P],
                                           op0=ALU.mult, op1=ALU.add).then_inc(S("bl_acc"), 1)
                running(0)
                if n is not None:
                    wait_count(dve, S("bl_mm"), (n - 1) * 2 if not isinstance(n, int) or n > 1 else 0)
                    wait_count(dve, S("l0_sc"), n - 3)
                    onehot(b_oS[:, b % 2, :], slf, n)
                running(1)
                if n is not None:
                    onehot(b_oD[:, s4, :], dlf, n).then_inc(S("bl_oh"), 1)
                running(2)
                if n is not None:
                    wait_count(dve, S(f"l0_y{s4}"), i * 64)
                    V.tensor_scalar(l_idx[:, s4, :], yidx[:, bass.ds(n * H, H)], 0.0, None, ALU.add).then_inc(S("l0_idx"), 1)
                    dve.wait_ge(S(f"l0_row{b % 2}"), (2 * i + b // 2 + 1) * 16)
                    wait_count(dve, S("l0_g"), n - 1)
                    V.tensor_scalar(l_oDT[:, b % 2, :], l_row[:, b % 2, :], pcol[:], None, ALU.is_equal).then_inc(S("l0_tr"), 1)
                running(3)
                if u is not None:
                    dve.wait_ge(S("l0_g"), u + 1)
                    V.tensor_tensor(l_g, ps[:, (4, 7)[u4 % 2], 0:H * 16].rearrange("p (k r) -> p k r", r=16)[:, :, 0:R],
                                    l_oT[:, u4 % 2], ALU.mult).then_inc(S("l0_sel"), 1)
                    dve.wait_ge(S("l0_sel"), u + 1)
                    wait_count(dve, S("l0_ys"), u - 1)
                    V.tensor_reduce(l_w[:, u4 % 2, :], l_g, AX.X, ALU.add).then_inc(S("l0_w"), 1)
                    dve.wait_ge(S("l0_w"), u + 1)
                if n is not None:
                    V.tensor_scalar(b_same[:, b % 2, :], same[:, bass.ds(n * H, H)], 0.0, None, ALU.add)
                    onehot(l_oT[:, b % 2].rearrange("p k r -> p (k r)"), tyf, n, R).then_inc(S("l0_oT"), 1)
                    dve.wait_ge(S("l0_oT"), n + 1)
            link(V.memset(b_acc[:, 3, :], 0.0))
            half_rounds(dve, build, 1)
            link(V.memset(cols[:], 0.0))

            vl = slice(0, N)

            def col(k):
                return cols[:, k:k + 1]

            def ln(tag, X, o, c, t):
                after(dve, tag + "_mean")
                link(V.tensor_tensor(c, X, psF, ALU.subtract))
                mark(V.tensor_tensor(t, c, c, ALU.mult), tag + "_sq")
                after(dve, tag + "_std")
                link(V.reciprocal(t, t))
                mark(V.tensor_tensor(o, c, t, ALU.mult), tag)

            def affine(tag, m, var, g, be, s_, t_):
                mark(V.tensor_scalar(var, var, 1.0, None, ALU.mult), tag + "_var")
                after(dve, tag + "_std")
                link(V.reciprocal(s_, s_))
                if g is not None:
                    link(V.tensor_tensor(s_, s_, g, ALU.mult))
                link(V.tensor_tensor(t_, m, s_, ALU.mult))
                if be is not None:
                    link(V.tensor_tensor(t_, be, t_, ALU.subtract))
                else:
                    link(V.tensor_scalar(t_, t_, -1.0, None, ALU.mult))

            def bn(tag, X, o, g, be, relu):
                link(V.tensor_reduce(col(0), X[:, vl], AX.X, ALU.add))
                link(V.tensor_scalar(col(0), col(0), 1.0 / N, None, ALU.mult))
                link(V.tensor_scalar(X[:, vl], X[:, vl], col(0), None, ALU.subtract))
                link(V.scalar_tensor_tensor(out=o[:, vl], in0=X[:, vl], scalar=1.0, in1=X[:, vl], op0=ALU.mult, op1=ALU.mult,
                                            accum_out=col(1)))
                link(V.tensor_scalar(col(1), col(1), 1.0 / N, None, ALU.mult))
                link(V.memset(col(2), 0.0))
                affine(tag, col(2), col(1), g, be, col(3), col(4))
                link(V.tensor_scalar(o[:, vl], X[:, vl], col(3), col(4), ALU.mult, ALU.add))
                if relu:
                    link(V.tensor_scalar(o[:, vl], o[:, vl], 0.0, None, ALU.max))
                mark(V.memset(o[:, PAD], 0.0), tag)

            def dot(o, a, op, sc, b_, acc):
                link(V.scalar_tensor_tensor(out=o[:, vl], in0=a[:, vl], scalar=sc, in1=b_[:, vl], op0=op, op1=ALU.mult, accum_out=acc))

            dve.wait_ge(S("wts_in"), 80)
            link(V.tensor_reduce(sm25, cnt[:].rearrange("p (b r) -> p b r", r=16)[:, :, 0:R], AX.X, ALU.add))
            link(V.tensor_copy(NT_[0].rearrange("p (b d) -> p b d", d=D), sm25.unsqueeze(2).to_broadcast([P, NB, D])))
            after(dve, "acc0")
            mark(V.tensor_copy(NT_[1], psN), "acc0N")
            after(dve, "i0_ps")
            mark(V.tensor_copy(i0row, psF), "i0_sb")
            after(dve, "acc0_ps")
            mark(V.tensor_copy(FT[1], psF), "acc0T")
            after(dve, "root_ps")
            link(V.tensor_tensor(FT[2], psF, FT[1], ALU.add))
            link(V.tensor_scalar(FT[2], FT[2], pr["L0_gnn_bias"], 0.0, ALU.add, ALU.max))
            mark(V.tensor_tensor(FT[2], FT[2], FT[0], ALU.add), "ln0_in")
            ln("ln0", FT[2], FT[0], FT[3], FT[4])
            mark(V.memset(FT[0][:, PAD], 0.0), "x1")

            for k in range(NB):
                dve.wait_ge(S(f"arow{k % 2}"), 16 * (k // 2 + 1))
                V.tensor_reduce(odeg[:, k:k + 1], arow[:, k % 2, :], AX.X, ALU.add).then_inc(S("odeg"), 1)
            dve.wait_ge(S("odeg"), NB)
            dve.wait_ge(S("pr_mm"), NB)
            mark(V.tensor_tensor(FT[1], psF, FT[0], ALU.add), "dsum")
            mark(V.tensor_copy(NT_[1].rearrange("p (b d) -> p b d", d=D), odeg[:].unsqueeze(2).to_broadcast([P, NB, D])), "odeg_rep")
            after(dve, "o0_ps")
            mark(V.tensor_copy(o0row, psF), "o0_sb")
            after(dve, "P_ps")
            mark(V.tensor_copy(FT[2], psF), "P_sb")
            after(dve, "Q_ps")
            mark(V.tensor_scalar(FT[3], psF, pr["L1_gnn_b_unite"], None, ALU.add), "Q_sb")
            after(dve, "DT_ps")
            mark(V.tensor_copy(FT[4], psF), "DT_sb")
            dot(FT[5], o0row, ALU.add, 1.0, FT[2], col(5))
            dot(FT[1], FT[5], ALU.mult, 1.0, FT[2], col(6))
            dot(FT[5], i0row, ALU.add, 1.0, FT[3], col(7))
            dot(FT[1], FT[5], ALU.mult, 1.0, FT[3], col(8))
            dot(FT[1], FT[4], ALU.mult, 2.0, FT[3], col(9))

            def row_stats(tag, sums, squares, g, be):
                link(V.tensor_tensor(col(0), sums[0], sums[1], ALU.add))
                link(V.tensor_scalar(col(0), col(0), 1.0 / ALL, None, ALU.mult))
                link(V.tensor_tensor(col(1), squares[0], squares[1], ALU.add))
                link(V.tensor_tensor(col(1), col(1), squares[2], ALU.add))
                link(V.tensor_tensor(col(2), col(0), col(0), ALU.mult))
                link(V.scalar_tensor_tensor(out=col(1), in0=col(1), scalar=1.0 / ALL, in1=col(2), op0=ALU.mult, op1=ALU.subtract))
                affine(tag, col(0), col(1), g, be, col(3), col(4))
            row_stats("bn1", (col(5), col(7)), (col(6), col(8), col(9)), pr["L1_gnn_g1"], pr["L1_gnn_be1"])
            link(V.tensor_scalar(FT[2], FT[2], col(3), None, ALU.mult))
            link(V.tensor_scalar(FT[3], FT[3], col(3), col(4), ALU.mult, ALU.add))
            link(V.memset(FT[2][:, PAD], 0.0))
            mark(V.memset(FT[3][:, PAD], 0.0), "PQ")
            link(V.tensor_tensor(FT[4], FT[2], FT[3], ALU.add))
            link(V.tensor_scalar(FT[4], FT[4], 0.0, None, ALU.max))
            after(dve, "PN")
            after(dve, "QN")
            link(V.tensor_tensor(NT_[2], NT_[0], NT_[1], ALU.add))
            mark(V.tensor_scalar(NT_[2], NT_[2], 0.0, None, ALU.max), "hsN")

            def onehot_round(p, which):
                def body(i, b):
                    n, s4, _ = stage_of(i, b, 0)
                    if n is not None:
                        dve.wait_ge(S(f"{p}_row{b % 2}"), (2 * i + b // 2 + 1) * (32 if p == "b" else 16))
                        wait_count(dve, S(p + "_sc"), n - 3)
                        if p == "b":
                            wait_count(dve, S("b_z"), n - 1)
                            V.tensor_scalar(e_oST[:, b % 2, :], e_srow[:, b % 2, :], pcol[:], None, ALU.is_equal)
                        V.tensor_scalar(e_oDT[:, s4, :], e_drow[:, b % 2, :], pcol[:], None, ALU.is_equal).then_inc(S(p + "_tr"), 1)
                        onehot(e_o[:, s4, :], (dlf, slf)[which], n).then_inc(S(p + "_o"), 1)
                return body
            dve.wait_ge(S("pr_mm"), NB)
            half_rounds(dve, onehot_round("b", 0), 0)
            after(dve, "accb")
            mark(V.tensor_tensor(NT_[2], NT_[2], psN, ALU.add), "s")
            after(dve, "s_ps")
            mark(V.tensor_copy(FT[5], psF), "sT")
            dve.wait_ge(S("pr_mm"), 2 * NB)
            mark(V.tensor_copy(FT[1], psF), "msg")
            after(dve, "R_ps")
            mark(V.tensor_scalar(FT[2], psF, pr["L1_gnn_b_gconv"], None, ALU.add), "R_sb")
            after(dve, "sW_ps")
            mark(V.tensor_copy(FT[3], psF), "sW_sb")
            mark(V.tensor_copy(gram_sb, ps[0:D, 7, 0:D]), "gram_sb")
            after(dve, "GW_ps")
            mark(V.tensor_tensor(gw_sb, ps[0:D, 7, 0:D], wt["gconv_h"], ALU.mult), "GW_sb")
            after(dve, "Mc_ps")
            link(V.tensor_copy(col(10), ps[0:D, 7, 0:1]))
            link(V.tensor_reduce(col(5), FT[3][:, vl], AX.X, ALU.add))
            dot(FT[1], i0row, ALU.add, 1.0, FT[2], col(7))
            dot(FT[1], FT[1], ALU.mult, 1.0, FT[2], col(8))
            dot(FT[1], FT[3], ALU.mult, 2.0, FT[2], col(9))
            row_stats("bn2", (col(5), col(7)), (col(10), col(8), col(9)), pr["L1_gnn_g2"], pr["L1_gnn_be2"])
            mark(V.tensor_scalar(diag2, ident[0:D, 0:D], col(3), None, ALU.mult), "diag2")
            link(V.tensor_scalar(FT[2], FT[2], col(3), col(4), ALU.mult, ALU.add))
            mark(V.memset(FT[2][:, PAD], 0.0), "RT")
            after(dve, "wc2_ps")
            mark(V.tensor_copy(wc2, ps[0:D, 7, 0:D]), "wc2")
            after(dve, "h2_ps")
            link(V.tensor_tensor(FT[4], psF, FT[2], ALU.add))
            link(V.tensor_scalar(FT[4], FT[4], 0.0, None, ALU.max))
            mark(V.memset(cols[:, 20:21], 0.0), "h2")
            half_rounds(dve, onehot_round("d", 1), 0)
            after(dve, "accd")
            mark(V.tensor_copy(NT_[2], psN), "accdN")
            after(dve, "accd_ps")
            mark(V.tensor_tensor(FT[5], psF, FT[4], ALU.add), "agg")
            after(dve, "t_ps")
            link(V.tensor_scalar(FT[1], psF, pr["L1_gnn_b_transfer"], None, ALU.add))
            bn("bnt", FT[1], FT[2], pr["L1_gnn_g2"], pr["L1_gnn_be2"], True)
            after(dve, "lin_ps")
            link(V.tensor_scalar(FT[3], psF, pr["L1_gnn_b_lin"], 0.0, ALU.add, ALU.max))
            bn("bnl", FT[3], FT[4], pr["L1_gnn_g3"], pr["L1_gnn_be3"], True)
            mark(V.tensor_tensor(FT[5], FT[0], FT[4], ALU.add), "ln1_in")
            ln("ln1", FT[5], FT[0], FT[1], FT[2])

            link(V.tensor_scalar(i0row, i0row, 1.0, None, ALU.max))
            mark(V.tensor_scalar(cols[:, 22:23], cols[:, 22:23], 0.0, None, ALU.mult), "deg1")
            after(dve, "deg_sqrt")
            link(V.reciprocal(i0row, i0row))
            dve.wait_ge(S("normt_in"), 16)
            link(V.memset(o0row[:, PAD], 0.0))
            link(V.tensor_scalar(FT[1], FT[0], 0.0, None, ALU.max))
            for k, (q, w) in enumerate(((2, "y1"), (4, "y2"))):
                bn(f"bnh{k}", FT[1], FT[2], None, None, False)
                for j, (row, o) in enumerate(((i0row, FT[3]), (o0row, FT[4]))):
                    dve.wait_ge(S("pr_mm"), (q + j + 1) * NB)
                    link(V.tensor_tensor(o, psF, FT[2], ALU.add))
                    mark(V.tensor_tensor(o, o, row, ALU.mult), f"agg{q + j}")
                after(dve, w + "_ps")
                if k == 0:
                    link(V.tensor_scalar(FT[1], psF, 0.0, None, ALU.max))
            mark(V.scalar_tensor_tensor(out=FT[5], in0=FT[0], scalar=2.0, in1=psF, op0=ALU.mult, op1=ALU.add), "ln2_in")
            ln("ln2", FT[5], FT[0], FT[1], FT[2])

            dve.wait_ge(S("pr_mm"), 7 * NB)
            mark(V.tensor_copy(FT[1], psF), "m3")
            after(dve, "h128_ps")
            mark(V.tensor_scalar(h128, psH, b1c[:], 0.0, ALU.add, ALU.max), "h128")
            after(dve, "up_ps")
            link(V.tensor_scalar(FT[3], psF, pr["L3_gnn_b2"], 0.0, ALU.add, ALU.max))
            mark(V.scalar_tensor_tensor(out=FT[5], in0=FT[0], scalar=2.0, in1=FT[3], op0=ALU.mult, op1=ALU.add), "ln3_in")
            ln("ln3", FT[5], FT[1], FT[2], FT[4])

        @block.scalar
        def _(act):
            act.wait_ge(S("filled"), 16)
            after(act, "key")
            with act.Fori(0, IG // 2) as i:
                for b in range(2):
                    g = i * 2 + b
                    act.wait_ge(S("counted"), g + 1)
                    nc.scalar.activation(C[:, bass.ds(g * GT + 1, GT), :], ps[0:NB, 2 + b, 0:GT * NB].rearrange("p (t s) -> p t s", s=NB),
                                         ACT.Copy).then_inc(S("C_in"), 1)
            after(act, "based")
            for b in range(2):
                nc.scalar.activation(cg[:, b, :].rearrange("p (t s) -> p t s", s=NB), C[:, b * GT:(b + 1) * GT, :], ACT.Copy).then_inc(S("cg"), 1)
            with act.Fori(1, IG // 2) as i:
                for b in range(2):
                    g = i * 2 + b
                    act.wait_ge(S("looked"), g - 1)
                    nc.scalar.activation(cg[:, b, :].rearrange("p (t s) -> p t s", s=NB), C[:, bass.ds(g * GT, GT), :], ACT.Copy).then_inc(S("cg"), 1)


            after(act, "W_ps")
            nc.scalar.activation(Wsb[:, 4 * BANK:8 * BANK], ps[0:R, 4:8, :].rearrange("p b n -> p (b n)"), ACT.Copy).then_inc(S("W_sb"), 1)
            for k in range(NB):
                act.wait_ge(S("y_ps"), k + 1)
                if k >= 2:
                    act.wait_ge(S(f"y_out{k % 2}"), 16 * (k // 2))
                nc.scalar.activation(ystg[:, k % 2, R * D // 2:R * D], ps[:, 2 * (k % 2) + 1, 0:R * D // 2], ACT.Copy).then_inc(S("y_a"), 1)

            act.wait_ge(S("tab_in"), 32)

            def put(i, b):
                n, s4, i4 = stage_of(i, b, 1)
                if n is None:
                    return
                rows, cols_ = blocks_of(act, n, 3, NB + TRASH - 1), blocks_of(act, n, 1)
                for k in range(H):
                    act.wait_ge(S("bl_acc"), n * H + k + 1)
                    act.dma_start(A_ds[bass.ds(rows[k] * P, P), bass.ds(cols_[k] * P, P)], b_acc[:, k, P:2 * P]).then_inc(S(f"bl_out{k}"), 16)
                act.wait_ge(S("l0_w"), n + 1)
                act.wait_ge(S(f"l0_y{s4}"), (i4 + 1) * 64)
                wait_count(act, S("l0_sc"), n - 1)
                for k in range(H):
                    last = nc.scalar.activation(l_ys[:, s4 % 2, k, :], l_y[:, s4, k, :], ACT.Copy, scale=l_w[:, s4 % 2, k:k + 1])
                last.then_inc(S("l0_ys"), 1)
            half_rounds(act, put, 1)

            def std(tag, o, in_, prior):
                after(act, prior)
                nc.scalar.activation(o, in_, ACT.Sqrt, bias=epsc[:]).then_inc(S(tag), 1)

            def to_sb(name, o, in_):
                after(act, name + "_ps")
                nc.scalar.activation(o, in_, ACT.Copy).then_inc(*now(name))

            def stationary(q, src):
                for b in range(2):
                    wait_count(act, S("pr_mm"), q * NB)
                    nc.scalar.activation(xs[:, b, :], src[:, b * D:(b + 1) * D], ACT.Copy).then_inc(S("pr_xs"), 1)
                with act.Fori(1, NB // 2) as i:
                    for b in range(2):
                        act.wait_ge(S("pr_mm"), q * NB + i * 2 + b - 1)
                        nc.scalar.activation(xs[:, b, :], src[:, bass.ds((i * 2 + b) * D, D)], ACT.Copy).then_inc(S("pr_xs"), 1)
                act.wait_ge(S("pr_mm"), q * NB + NB - 2)
                nc.scalar.activation(xs[:, 0, :], src[:, (NB - 1) * D:NB * D], ACT.Copy).then_inc(S("pr_xs"), 1)

            def product_in(q, name, k=0):
                to_sb(name, NT_[k], psN)
                after(act, name)
                stationary(q, NT_[k])
            after(act, "consts2")
            std("ln0_std", FT[4], psF, "ln0_var")
            product_in(0, "x1N")
            std("bn1_std", cols[:, 3:4], cols[:, 1:2], "bn1_var")
            to_sb("PN", NT_[0], psN)
            to_sb("QN", NT_[1], psN)

            def relu_rounds(p):
                def body(i, b):
                    if p == "d":
                        n, s4, _ = stage_of(i, b, 1)
                        if n is not None:
                            act.wait_ge(S("d_u"), n + 1)
                            wait_count(act, S("d_sc"), n - 1)
                            nc.scalar.activation(e_h2[:, s4 % 2, :], ps[:, (4, 7)[s4 % 2], 0:H * D], ACT.Relu).then_inc(S("d_h2"), 1)
                        n, s4, _ = stage_of(i, b, 0)
                        if n is not None:
                            act.wait_ge(S("d_T"), n + 1)
                            wait_count(act, S("d_u"), n - 1)
                            nc.scalar.activation(e_hT[:, s4 % 2, :], ps[0:D, 5 + s4 % 2, 0:HE], ACT.Copy).then_inc(S("d_hT"), 1)
                    else:
                        n, _, _ = stage_of(i, b, 0)
                        if n is not None:
                            act.wait_ge(S("b_z"), n + 1)
                            wait_count(act, S("b_sc"), n - 3)
                            wait_count(act, S(f"b_out{b}"), i * 16)
                            nc.scalar.activation(e_h[:, b, :], ps[:, 4 + b % 2, 0:H * D], ACT.Relu).then_inc(S("b_h"), 1)
                        n, s4, _ = stage_of(i, b, 1)
                        if n is not None:
                            act.wait_ge(S("b_h"), n + 1)
                            act.dma_start(h_d[bass.ds(n * P, P), :], e_h[:, s4, :]).then_inc(S(f"b_out{s4}"), 16)
                half_rounds(act, body, 1)
            relu_rounds("b")
            after(act, "s")
            stationary(1, NT_[2])
            std("bn2_std", cols[:, 3:4], cols[:, 1:2], "bn2_var")
            act.wait_ge(S("pr_mm"), 2 * NB)
            to_sb("RN", NT_[2], psN)
            after(act, "RN")
            relu_rounds("d")
            std("bnt_std", cols[:, 3:4], cols[:, 1:2], "bnt_var")
            std("bnl_std", cols[:, 3:4], cols[:, 1:2], "bnl_var")
            std("ln1_std", FT[2], psF, "ln1_var")
            act.dma_start(o0row[:, 0:N], A["normt"].to_broadcast([D, N])).then_inc(S("normt_in"), 16)
            after(act, "deg1")
            nc.scalar.activation(i0row, i0row, ACT.Sqrt).then_inc(*now("deg_sqrt"))
            for k, q in enumerate((2, 4)):
                std(f"bnh{k}_std", cols[:, 3:4], cols[:, 1:2], f"bnh{k}_var")
                product_in(q, f"hN{k}")
                stationary(q + 1, NT_[0])
            std("ln2_std", FT[2], psF, "ln2_var")
            product_in(6, "x3N")
            std("ln3_std", FT[4], psF, "ln3_var")
            act.wait_ge(S("pr_mm"), 7 * NB)
            to_sb("outN", NT_[1], psN)

        @block.tensor
        def _(pe):
            after(pe, "ident")
            after(pe, "key")
            for n, col in enumerate((key, dbf)):
                for c in range(8):
                    m = n * 8 + c
                    if m >= 2:
                        pe.wait_ge(S("rows_t"), m - 1)
                    nc.tensor.transpose(ps[0:rows8, c % 2, 0:ET], col[:, c * rows8:(c + 1) * rows8],
                                        ident[0:ET, 0:ET]).then_inc(S("row_tr"), 1)
            def count(b, g, first):
                pe.wait_ge(S("oh"), g + 1)
                if not first:
                    pe.wait_ge(S("C_in"), g - 1)
                for k in range(GT):
                    last = nc.tensor.matmul(ps[0:NB, 2 + b, k * NB:(k + 1) * NB], ohD[:, b, k, :], ohS[:, b, k, :], start=True, stop=True)
                last.then_inc(S("counted"), 1)
            for b in range(2):
                count(b, b, True)
            with pe.Fori(1, IG // 2) as i:
                for b in range(2):
                    count(b, i * 2 + b, False)
            after(pe, "rowtot")
            pe.wait_ge(S("tri"), 2)
            nc.tensor.matmul(ps[0:NB, 4, 0:1], triT[0:NB, 0:NB], incl[:, NB - 1:NB], start=True, stop=True).then_inc(S("roff"), 1)

            def look(b, g, first):
                pe.wait_ge(S("ohT"), g + 1)
                pe.wait_ge(S("cg"), g + 1)
                if not first:
                    pe.wait_ge(S("selected"), g - 1)
                for k in range(GT):
                    last = nc.tensor.matmul(ps[0:ET, 5 + b, k * NB:(k + 1) * NB], ohT[:, b, k * ET:(k + 1) * ET],
                                            cg[:, b, k * NB:(k + 1) * NB], start=True, stop=True)
                last.then_inc(S("looked"), 1)
            for b in range(2):
                look(b, b, True)
            with pe.Fori(1, IG // 2) as i:
                for b in range(2):
                    look(b, i * 2 + b, False)
            after(pe, "fields")
            for n, col in enumerate((slf, dlf)):
                for c in range(TC):
                    m = n * TC + c
                    if m >= 2:
                        pe.wait_ge(S("slot_cp"), m - 1)
                    nc.tensor.transpose(ps[:, m % 2, 0:P], col[:, c * P:(c + 1) * P], ident[:]).then_inc(S("slot_tr"), 1)

            pe.wait_ge(S("basis_in"), 32)
            pe.wait_ge(S("slot_cp"), 2 * TC)
            for c in range(8):
                last = nc.tensor.matmul(ps[0:R, c, :], compT, basis[:, c * BANK:(c + 1) * BANK], start=True, stop=True)
            last.then_inc(S("W_ps"), 1)
            pe.wait_ge(S("W_in"), 16)
            pe.wait_ge(S("W_sb"), 2)
            pe.wait_ge(S("xT_in"), 16)
            after(pe, "xpad")
            wall = Wall.rearrange("p r o -> p (r o)")
            for k in range(NB):
                if k >= 2:
                    pe.wait_ge(S("y_v"), k - 1)
                    pe.wait_ge(S("y_a"), k - 1)
                for j in range(2):
                    last = nc.tensor.matmul(ps[:, 2 * (k % 2) + j, 0:R * D // 2], FT[0][:, k * P:(k + 1) * P],
                                            wall[:, j * R * D // 2:(j + 1) * R * D // 2], start=True, stop=True)
                last.then_inc(S("y_ps"), 1)
            pe.wait_ge(S("y_v"), NB)
            pe.wait_ge(S("y_a"), NB)
            after(pe, "zerob")

            def clear(bank, stop=False):
                return nc.tensor.matmul(ps[:, bank, :], zerob[:, 0:P], zerob[:], start=not stop, stop=stop)

            def warm_up(times, bank=7):
                for _ in range(times):
                    nc.tensor.matmul(ps[:, bank, :], zerob[:, 0:P], zerob[:], start=True, stop=True)

            clear(7)

            def counts(i, b):
                n, _, _ = stage_of(i, b, 0)
                dbs = blocks_of(pe, n, 0)
                pe.wait_ge(S("c_oh"), n + 1)
                for k in range(H):
                    last = nc.tensor.matmul(ps[:, 7, bass.ds(dbs[k] * 16, R)], c_oD[:, b % 2, k * P:(k + 1) * P],
                                            c_oT[:, b % 2, k * R:(k + 1) * R], start=False, stop=False)
                last.then_inc(S("c_mm"), 1)
            half_rounds(pe, counts, 0)
            clear(7, True).then_inc(*now("cnt"))

            for k in range(4):
                clear(k)
            after(pe, "inv")

            def build(i, b):
                n, s4, _ = stage_of(i, b, 0)
                if n is not None:
                    dbs = blocks_of(pe, n, 0)
                    pe.wait_ge(S("bl_oh"), n + 1)
                    for j in range(2):
                        wait_count(pe, S("bl_acc"), n * H + 2 * j - 2 if not isinstance(n, int) or n else 0)
                        for k in (2 * j, 2 * j + 1):
                            e, at = slice(k * P, (k + 1) * P), (k % 2) * 2 * P
                            nc.tensor.matmul(ps[:, 5 + j, at:at + P], b_oS[:, b % 2, e], b_oD[:, s4, e], start=True, stop=True)
                            last = nc.tensor.matmul(ps[:, 5 + j, at + P:at + 2 * P], b_oD[:, s4, e], b_oS[:, b % 2, e], start=True, stop=True)
                        last.then_inc(S("bl_mm"), 1)
                    pe.wait_ge(S("l0_tr"), n + 1)
                    wait_count(pe, S("l0_w"), n - 1)
                    warm_up(1, (4, 7)[b % 2])
                    for k in range(H):
                        last = nc.tensor.matmul(ps[:, (4, 7)[b % 2], k * 16:k * 16 + R], l_oDT[:, b % 2, k * P:(k + 1) * P],
                                                inv[:, bass.ds(dbs[k] * 16, R)], start=True, stop=True)
                    last.then_inc(S("l0_g"), 1)
                n, s4, _ = stage_of(i, b, 2)
                if n is not None:
                    dbs = blocks_of(pe, n, 0)
                    pe.wait_ge(S("l0_ys"), n + 1)
                    for k in range(H):
                        last = nc.tensor.matmul(psN[:, bass.ds(dbs[k] * D, D)], b_oD[:, s4, k * P:(k + 1) * P],
                                                l_ys[:, s4 % 2, k, :], start=False, stop=False)
                    last.then_inc(S("l0_sc"), 1)
            half_rounds(pe, build, 2)

            def end_sums(name):
                for k in range(4):
                    last = clear(k, True)
                last.then_inc(*now(name))
            end_sums("acc0")

            def mm(name, terms, rows=D):
                for c, (at, w) in enumerate(CH):
                    for k, (lhs, rhs) in enumerate(terms):
                        last = nc.tensor.matmul(ps[0:rows, c, 0:w], lhs, rhs[:, at:at + w], start=k == 0, stop=k == len(terms) - 1)
                last.then_inc(*now(name))

            def to_T(name, src):
                for k in range(NB):
                    last = nc.tensor.transpose(psT(k), src[:, k * D:(k + 1) * D], ident[:])
                last.then_inc(*now(name))

            def psT(k):
                return ps[0:D, k // 4, (k % 4) * P:(k % 4 + 1) * P]

            def to_N(name, src):
                for k in range(NB):
                    last = nc.tensor.transpose(ps[:, k // 8, (k % 8) * D:(k % 8 + 1) * D], src[:, k * P:(k + 1) * P], ident[0:D, 0:D])
                last.then_inc(*now(name + "_ps"))

            def product(q):
                def one(k, b, uses, first, lst):
                    pe.wait_ge(S(f"arow{b}"), 16 * uses)
                    pe.wait_ge(S("pr_xs"), q * NB + k + 1)
                    for c, (at, w) in enumerate(CH):
                        last = nc.tensor.matmul(ps[0:D, c, 0:w], xs[:, b, :], arow[:, b, at:at + w], start=first, stop=lst)
                    last.then_inc(S("pr_mm"), 1)
                one(0, 0, 13 * q + 1, True, False)
                one(1, 1, 12 * q + 1, False, False)
                with pe.Fori(1, NB // 2) as i:
                    one(i * 2, 0, 13 * q + i + 1, False, False)
                    one(i * 2 + 1, 1, 12 * q + i + 1, False, False)
                one(NB - 1, 0, 13 * (q + 1), False, True)

            def ln(tag, X, t):
                after(pe, tag + "_in")
                mm(tag + "_mean", [(mean64[:], X)])
                after(pe, tag + "_sq")
                mm(tag + "_var", [(mean64[:], t)])

            after(pe, "acc0N")
            to_T("i0_ps", NT_[0])
            after(pe, "i0_sb")
            to_T("acc0_ps", NT_[1])
            after(pe, "acc0T")
            pe.wait_ge(S("wts_in"), 80)
            mm("root_ps", [(wt["root"], FT[0])])
            ln("ln0", FT[2], FT[4])
            after(pe, "x1")
            to_N("x1N", FT[0])
            after(pe, "x1N")
            product(0)
            after(pe, "odeg_rep")
            to_T("o0_ps", NT_[1])
            after(pe, "o0_sb")
            mm("P_ps", [(wt["unite_x"], FT[0])])
            after(pe, "P_sb")
            mm("Q_ps", [(wt["unite_d"], FT[1])])
            after(pe, "Q_sb")
            mm("DT_ps", [(wt["unite_x"], FT[1])])
            after(pe, "DT_sb")
            after(pe, "PQ")
            to_N("PN", FT[2])
            after(pe, "PN")
            to_N("QN", FT[3])
            after(pe, "hsN")
            for k in range(4):
                clear(k)
            for k in range(NB - 1):
                nc.tensor.matmul(ps[0:D, 7, 0:D], NT_[2][:, k * D:(k + 1) * D], NT_[2][:, k * D:(k + 1) * D],
                                 start=k == 0, stop=False)

            def gather_rows(n, s4):
                sls, dls = blocks_of(pe, n, 1), blocks_of(pe, n, 0)
                pe.wait_ge(S("b_tr"), n + 1)
                wait_count(pe, S("b_h"), n - 1)
                for k in range(H):
                    e = slice(k * P, (k + 1) * P)
                    o = ps[:, 4 + s4 % 2, k * D:(k + 1) * D]
                    nc.tensor.matmul(o, e_oST[:, s4 % 2, e], NT_[0][:, bass.ds(sls[k] * D, D)], start=True, stop=False)
                    last = nc.tensor.matmul(o, e_oDT[:, s4, e], NT_[1][:, bass.ds(dls[k] * D, D)], start=False, stop=True)
                last.then_inc(S("b_z"), 1)

            def sums(p, n, s4, h, ready, which):
                blks = blocks_of(pe, n, which)
                pe.wait_ge(S(ready), n + 1)
                pe.wait_ge(S(p + "_o"), n + 1)
                for k in range(H):
                    hk = h[:, s4 % h.shape[1], k * D:(k + 1) * D]
                    last = nc.tensor.matmul(psN[:, bass.ds(blks[k] * D, D)], e_o[:, s4, k * P:(k + 1) * P], hk, start=False, stop=False)
                    if p == "b":
                        last = nc.tensor.matmul(ps[0:D, 7, 0:D], hk, hk, start=False, stop=False)
                last.then_inc(S(p + "_sc"), 1)

            def round_b(i, b):
                n, s4, _ = stage_of(i, b, 2)
                if n is not None:
                    sums("b", n, s4, e_h, "b_h", 0)
                n, s4, _ = stage_of(i, b, 0)
                if n is not None:
                    gather_rows(n, s4)
            half_rounds(pe, round_b, 2)
            nc.tensor.matmul(ps[0:D, 7, 0:D], NT_[2][:, (NB - 1) * D:NB * D], NT_[2][:, (NB - 1) * D:NB * D],
                             start=False, stop=True)
            end_sums("accb")
            after(pe, "s")
            to_T("s_ps", NT_[2])
            after(pe, "sT")
            product(1)
            after(pe, "msg")
            mm("R_ps", [(wt["gconv_m"], FT[1])])
            after(pe, "R_sb")
            mm("sW_ps", [(wt["gconv_h"], FT[5])])
            after(pe, "gram_sb")
            nc.tensor.matmul(ps[0:D, 7, 0:D], gram_sb, wt["gconv_h"], start=True, stop=True).then_inc(*now("GW_ps"))
            after(pe, "GW_sb")
            nc.tensor.matmul(ps[0:D, 7, 0:1], gw_sb, ones[0:D, 0:1], start=True, stop=True).then_inc(*now("Mc_ps"))
            after(pe, "diag2")
            nc.tensor.matmul(ps[0:D, 7, 0:D], wt["gconv_hT"], diag2, start=True, stop=True).then_inc(*now("wc2_ps"))
            after(pe, "RT")
            to_N("RN", FT[2])
            after(pe, "RN")
            after(pe, "wc2")
            mm("h2_ps", [(wc2, FT[4])])
            after(pe, "h2")
            warm_up(16)
            for k in range(4):
                clear(k)

            def round_d(i, b):
                n, s4, _ = stage_of(i, b, 2)
                if n is not None:
                    sums("d", n, s4, e_h2, "d_h2", 1)
                n, s4, _ = stage_of(i, b, 1)
                m, m4, mi = stage_of(i, b, 0)
                dls = None if n is None else blocks_of(pe, n, 0)
                if m is not None:
                    pe.wait_ge(S(f"d_in{m4}"), (mi + 1) * 16)
                    wait_count(pe, S("d_hT"), m - 1)
                if n is not None:
                    pe.wait_ge(S("d_tr"), n + 1)
                    pe.wait_ge(S("d_hT"), n + 1)
                    wait_count(pe, S("d_h2"), n - 1)
                    warm_up(10 if isinstance(n, int) else 2, (4, 7)[s4 % 2])
                    for k in range(H):
                        e = slice(k * P, (k + 1) * P)
                        o = ps[:, (4, 7)[s4 % 2], k * D:(k + 1) * D]
                        nc.tensor.matmul(o, e_hT[:, s4 % 2, e], wc2, start=True, stop=False)
                        last = nc.tensor.matmul(o, e_oDT[:, s4, e], NT_[2][:, bass.ds(dls[k] * D, D)], start=False, stop=True)
                    last.then_inc(S("d_u"), 1)
                if m is not None:
                    for k in range(H):
                        last = nc.tensor.transpose(ps[0:D, 5 + m4 % 2, k * P:(k + 1) * P], e_h[:, m4, k * D:(k + 1) * D], ident[:])
                    last.then_inc(S("d_T"), 1)
            half_rounds(pe, round_d, 2)
            end_sums("accd")
            after(pe, "accdN")
            to_T("accd_ps", NT_[2])
            after(pe, "agg")
            mm("t_ps", [(wt["transfer_h"], FT[4]), (wt["transfer_a"], FT[5])])
            after(pe, "bnt")
            mm("lin_ps", [(wt["lin"], FT[2])])
            ln("ln1", FT[5], FT[2])
            for k, (q, w) in enumerate(((2, "1"), (4, "2"))):
                after(pe, f"bnh{k}")
                to_N(f"hN{k}", FT[2])
                after(pe, f"hN{k}")
                product(q)
                after(pe, f"agg{q}")
                product(q + 1)
                after(pe, f"agg{q + 1}")
                mm(f"y{k + 1}_ps", [(wt[f"W{w}_out"], FT[3]), (wt[f"W{w}_back"], FT[4])])
            ln("ln2", FT[5], FT[2])
            after(pe, "ln2")
            to_N("x3N", FT[0])
            after(pe, "x3N")
            product(6)
            after(pe, "m3")
            mm("h128_ps", [(w1T[:], FT[1])], 2 * D)
            after(pe, "h128")
            mm("up_ps", [(w2T[:], h128)])
            ln("ln3", FT[5], FT[4])
            after(pe, "ln3")
            to_N("outN", FT[1])


def kernel(**inputs):
    import numpy as np
    import concourse.bacc as bacc
    from concourse.bass_utils import run_bass_kernel_spmd

    a = {k: np.asarray(v) for k, v in inputs.items()}
    arrays = {
        "xT": np.ascontiguousarray(a["x"].T),
        "src_c": np.ascontiguousarray(a["src"].reshape(IT, ET).T),
        "dst_c": np.ascontiguousarray(a["dst"].reshape(IT, ET).T),
        "typ_c": np.ascontiguousarray(a["edge_type_12"].reshape(IT, ET).T),
    }
    g = a["L1_gnn_W_gconv"]
    weights = [a["L0_gnn_root"], a["L1_gnn_W_unite"][:D], a["L1_gnn_W_unite"][D:], g[:D], g[D:],
               a["L1_gnn_W_transfer"][:D], a["L1_gnn_W_transfer"][D:], a["L1_gnn_W_lin"], a["L2_gnn_W1_out"],
               a["L2_gnn_W1_back"], a["L2_gnn_W2_out"], a["L2_gnn_W2_back"], g[:D].T]
    arrays.update({
        "weights": np.ascontiguousarray(np.stack(weights, 1)),
        "params": np.ascontiguousarray(np.stack([a[n] for n in PARAMS], 1)),
        "w1T": np.ascontiguousarray(a["L3_gnn_w1"].T), "w2T": np.ascontiguousarray(a["L3_gnn_w2"].T),
        "b1": a["L3_gnn_b1"].reshape(2 * D, 1), "compT": np.ascontiguousarray(a["L0_gnn_comp"].T),
        "basis": a["L0_gnn_basis"].reshape(BASES, D * D), "normt": a["node_vec1"].reshape(1, N),
    })
    nc = bacc.Bacc("TRN2", target_bir_lowering=False, num_devices=1)
    handles = {n: nc.dram_tensor("in_" + n, v.shape, mybir.dt.from_np(v.dtype), kind="ExternalInput").ap()
               for n, v in arrays.items()}
    out = nc.dram_tensor("out", (N, D), f32, kind="ExternalOutput").ap()
    build(nc, handles, out, "all")
    r = run_bass_kernel_spmd(nc, [{"in_" + n: v for n, v in arrays.items()}], core_ids=[0])
    return r.results[0]["out"]
```

```python
from contextlib import ExitStack

import concourse.bass as bass
from concourse import mybir

N = 3125
D = 64
E = 100000
R = 12
BASES = 30
P = 128
NB = (N + P - 1) // P
NP = NB * P
ET = 125
IT = E // ET
GT = 20
IG = IT // GT
GE = GT * ET
BINS = NB * NB
NT = 1408
TC = NT // P
TRASH = 4
EPS = 1e-5
BANK = 512
PB = 5
HALF = [(0, 3 * BANK), (3 * BANK, NP - 3 * BANK)]
PH = 2 * NB
CH = [(c * BANK, min(BANK, NP - c * BANK)) for c in range((NP + BANK - 1) // BANK)]

ALU = mybir.AluOpType
ACT = mybir.ActivationFunctionType
AX = mybir.AxisListType
f32, bf16, f16 = mybir.dt.float32, mybir.dt.bfloat16, mybir.dt.float16
i32, i16 = mybir.dt.int32, mybir.dt.int16


H = 4
M = NT // H
HE = H * P
ALL = E + N
A_ROWS = (NB + TRASH) * P
PARAMS = ["L0_gnn_bias", "L1_gnn_b_unite", "L1_gnn_g1", "L1_gnn_be1", "L1_gnn_b_gconv", "L1_gnn_g2",
          "L1_gnn_be2", "L1_gnn_b_transfer", "L1_gnn_b_lin", "L1_gnn_g3", "L1_gnn_be3", "L3_gnn_b2"]
WEIGHTS = ["root", "unite_x", "unite_d", "gconv_h", "gconv_m", "transfer_h", "transfer_a", "lin",
           "W1_out", "W1_back", "W2_out", "W2_back", "gconv_hT"]

STEPS = {
    "vector": (
        "key", "rowtot", "bins", "based", "scat_seen", "tab_c", "fields", "consts2", "zerob", "xpad", "inv",
        "acc0N", "i0_sb", "acc0T", "ln0_in", "ln0_var", "ln0", "ln0T", "large", "flag", "dsum", "odeg_rep",
        "o0_sb", "P_sb", "Q_sb", "DT_sb", "bn1_var", "PQ", "hsN", "s", "sT", "msg", "R_sb", "sW_sb",
        "gram_sb", "GW_sb", "bn2_var", "diag2", "RT", "wc2", "h2", "accdN", "agg", "bnt_var", "bnt",
        "bnl_var", "bnl", "ln1_in", "ln1_var", "ln1", "ln1T", "deg1", "norm_rep", "bnh0_var", "bnh0", "agg2",
        "agg3", "bnh1_var", "bnh1", "agg4", "agg5", "ln2_in", "ln2_var", "ln2", "ln2T", "m3", "h128",
        "ln3_in", "ln3_var", "ln3",),
    "scalar": (
        "PN", "QN", "gram_up", "RN", "deg_sqrt", "hN0", "hN1",),
    "tensor": (
        "cnt", "acc0", "i0_ps", "acc0_ps", "root_ps", "ln0_ps", "ln0T_ps", "large_ps", "o0_ps", "P_ps",
        "Q_ps", "DT_ps", "PN_ps", "QN_ps", "accb", "s_ps", "R_ps", "sW_ps", "GW_ps", "Mc_ps", "wc2_ps",
        "RN_ps", "h2_ps", "accd", "accd_ps", "t_ps", "lin_ps", "ln1_ps", "ln1T_ps", "norm_ps", "hN0_ps",
        "y1_ps", "hN1_ps", "y2_ps", "ln2_ps", "ln2T_ps", "h128_ps", "up_ps", "ln3_ps",),
}


def wait_count(eng, sem, n):
    if not isinstance(n, int) or n > 0:
        eng.wait_ge(sem, n)


def stage_of(i, b, lag):
    n = 4 * i + b - lag
    if isinstance(n, int) and not 0 <= n < M:
        return None, 0, 0
    return n, (b - lag) % 4, i - (1 if b < lag else 0)


def half_rounds(eng, body, last):
    for b in range(4):
        body(0, b)
    with eng.Fori(1, M // 4) as i:
        for b in range(4):
            body(i, b)
    for b in range(last):
        body(M // 4, b)


def counting_rounds(eng, body):
    for b in range(2):
        body(0, b, b)
    with eng.Fori(1, M // 4) as i:
        for b in range(2):
            body(i, b, i * 2 + b)


class Region:

    def __init__(self, tensor):
        self.tensor, self.at = tensor, 0

    def take(self, parts, cols, dt=f32):
        words = cols if dt in (f32, i32) else (cols + 1) // 2
        ap = self.tensor[0:parts, self.at:self.at + words]
        self.at += words
        assert self.at <= self.tensor.shape[1], (self.at, self.tensor.shape)
        return ap if dt == f32 else ap.bitcast(dt)

    def reset(self):
        self.at = 0


def build(nc, A, out):
    ctx = ExitStack()
    with ctx:
        def sb(name, shape, dt=f32):
            return ctx.enter_context(nc.sbuf_tensor(name, shape, dt))

        def dram(name, shape, dt=f32):
            return nc.dram_tensor(name, shape, dt, kind="Internal").ap()

        named = {}

        def S(name):
            if name not in named:
                named[name] = ctx.enter_context(nc.semaphore(name))
            return named[name]

        passed = {k: 0 for k in STEPS}

        def now(name):
            for eng, names in STEPS.items():
                if name in names:
                    assert names.index(name) == passed[eng], name
                    passed[eng] += 1
                    return S(eng + "_steps"), 1
            return S(name), 1

        def after(eng, name):
            for e, names in STEPS.items():
                if name in names:
                    eng.wait_ge(S(e + "_steps"), names.index(name) + 1)
                    return
            eng.wait_ge(S(name), 1)

        slots = dram("slots", [P * NT, 4], i32)
        keyrow_d = dram("keyrow_d", [IT, ET], f16)
        dbrow_d = dram("dbrow_d", [IT, ET], bf16)
        bins_d = dram("bins_d", [1, BINS])
        tab_d = dram("tab_d", [4, NT], i16)
        same_d = dram("same_d", [1, NT])
        slrow_d = dram("slrow_d", [NT, P], bf16)
        dlrow_d = dram("dlrow_d", [NT, P], bf16)
        A_sd = dram("A_sd", [A_ROWS, NP])
        A_ds = dram("A_ds", [A_ROWS, NP])
        w_d = dram("w_d", [R, D * D])
        h_d = dram("h_d", [M * P, H * D])
        y_d = dram("y_d", [NP, R * D])

        F = sb("F", [P, 6 * NP + 960])
        WK = sb("WK", [P, 5 * HALF[1][1]])
        RW = sb("RW", [P, 6400])
        NR = sb("NR", [P, 4800])
        ident = sb("ident", [P, P])
        iota = sb("iota", [P, P])
        iotab = sb("iotab", [P, P], bf16)
        pcol = sb("pcol", [P, 1])
        tri = sb("tri", [P, P])
        ones = sb("ones", [P, P])
        triT = sb("triT", [P, P])
        slf = sb("slf", [P, NT])
        dlf = sb("dlf", [P, NT])
        tab = sb("tab", [1, NT * 4], i16)
        small = sb("small", [P, 1800])
        gate = sb("gate", [1, 4])
        cnt = sb("cnt", [P, NB * 16])
        inv = sb("inv", [P, NB * 16])
        odeg = sb("odeg", [P, NB])
        oparts = sb("oparts", [P, NB, 2])
        zerob = sb("zerob", [P, BANK], bf16)
        wts = sb("wts", [D, len(WEIGHTS), D])
        prm = sb("prm", [D, len(PARAMS)])
        w1T = sb("w1T", [D, 2 * D])
        w2T = sb("w2T", [2 * D, D])
        b1c = sb("b1c", [2 * D, 1])
        stat = sb("stat", [P, 2, NB])
        cols = sb("cols", [D, 32])
        m64 = sb("m64", [D, 4 * D])
        wc2s = sb("wc2s", [P, 2 * D])
        epsc = sb("epsc", [P, 1])
        xs = sb("xs", [P, PB, 2 * D])
        xb = sb("xb", [P, PB, 3 * D], bf16)
        rest = sb("rest", [P, PB, D])
        large = sb("large", [P, 1])
        flag = sb("flag", [1, 1], i32)
        ps = ctx.enter_context(nc.psum_tensor("ps", [P, 8, BANK], f32))

        rn, rr, rw = Region(NR), Region(RW), Region(WK)
        src_c, dst_c, typ_c = (rn.take(ET, IT, i32) for _ in range(3))
        dbf, sbf, key = (rn.take(ET, IT) for _ in range(3))
        C = F[0:NB, 0:(IT + 1) * NB].rearrange("p (t s) -> p t s", s=NB)
        krow = rr.take(ET, 2 * GE, f16).rearrange("p (b n) -> p b n", b=2)
        drow = rr.take(NB, 2 * GE, bf16).rearrange("p (b n) -> p b n", b=2)
        ohS = rr.take(ET, 2 * GT * NB, bf16).rearrange("p (b t s) -> p b t s", b=2, s=NB)
        ohD = rr.take(ET, 2 * GT * NB, bf16).rearrange("p (b t s) -> p b t s", b=2, s=NB)
        ohT = rw.take(NB, 2 * GE).rearrange("p (b n) -> p b n", b=2)
        cg = rw.take(NB, 2 * GT * NB).rearrange("p (b n) -> p b n", b=2)
        sm = Region(small)
        sel3 = sm.take(ET, GT * NB).rearrange("p (t s) -> p t s", s=NB)
        base_e = sm.take(ET, GT)
        rank = sm.take(ET, GT)
        posi = sm.take(ET, 3 * GT, i32).rearrange("p (k n) -> p k n", k=3)
        posf = sm.take(ET, GT)
        idx = sm.take(ET, 2 * GT, i32).rearrange("p (b n) -> p b n", b=2)
        rec = sm.take(ET, 2 * GT * 4, i32).rearrange("p (b n k) -> p b n k", b=2, k=4)
        junk2 = rw.take(ET, 2 * ET).rearrange("p (b e) -> p b e", b=2)
        kk = sm.take(ET, GT)
        zk = sm.take(ET, GT)
        tot = sm.take(NB, NB)
        toti = sm.take(NB, NB, i32)
        toti2 = sm.take(NB, NB, i32)
        tri4 = sm.take(P, TC, i32)
        tri4b = sm.take(P, TC, i32)
        nt_f = sm.take(NB, NB)
        incl = sm.take(NB, NB)
        one25 = sm.take(NB, NB)
        roff = sm.take(NB, 1)
        binrow = WK[:, 0:BINS]
        tcol = sm.take(P, 3 * TC)
        kcol = sm.take(P, 3 * TC)
        tmp24 = sm.take(P, NB)
        dbc = sm.take(P, TC)
        sbc = sm.take(P, TC)
        fin = sm.take(P, TC)
        tr4 = sm.take(P, TC)
        tabc = sm.take(P, TC * 4, i16).rearrange("p (k c) -> p k c", k=4)
        edge25 = sm.take(P, NB)
        samec = sm.take(P, TC)
        binjunk = WK[:, 640:640 + BINS]
        slot_i = F[:, 0:NT * 4].bitcast(i32).rearrange("p (t k) -> p t k", k=4)
        rowst = F[:, NT * 4:NT * 4 + TC * P].bitcast(bf16).rearrange("p (k c e) -> p k c e", k=2, e=P)
        tyf, same, yidx = NR[:, 0:NT], NR[:, NT:2 * NT], NR[:, 2 * NT:3 * NT].bitcast(i32)
        fill = F[:, 0:NT * 4].bitcast(i32)

        keyst = WK[0:IT // 8, 0:8 * ET // 2 + 4].bitcast(f16)[:, 0:8 * ET].rearrange("r (c e) -> r c e", c=8)
        dbst = WK[0:IT // 8, 1024:1024 + 8 * ET // 2 + 4].bitcast(bf16)[:, 0:8 * ET].rearrange("r (c e) -> r c e", c=8)
        rows8 = IT // 8

        posA = F[0:ET, NT * 4:NT * 4 + 2 * IT].bitcast(i32).rearrange("p (k n) -> p k n", k=2)

        ring = Region(WK)
        b_oS = ring.take(P, 2 * HE).rearrange("p (b n) -> p b n", b=2)
        b_oD = ring.take(P, 4 * HE).rearrange("p (b n) -> p b n", b=4)
        b_acc = ring.take(P, 4 * 2 * P).rearrange("p (b n) -> p b n", b=4)
        b_same = ring.take(P, 2 * H).rearrange("p (b k) -> p b k", b=2)
        l_row = ring.take(P, 2 * HE, bf16).rearrange("p (b n) -> p b n", b=2)
        l_oDT = ring.take(P, 2 * HE).rearrange("p (b n) -> p b n", b=2)
        l_y = ring.take(P, 4 * H * D).rearrange("p (b k n) -> p b k n", b=4, k=H)
        l_ys = ring.take(P, 2 * H * D).rearrange("p (b k n) -> p b k n", b=2, k=H)
        l_idx = ring.take(P, 4 * H, i32).rearrange("p (b k) -> p b k", b=4)
        l_w = ring.take(P, 2 * H).rearrange("p (b k) -> p b k", b=2)
        l_oT = ring.take(P, 2 * H * R).rearrange("p (b k r) -> p b k r", b=2, k=H)
        l_g = ring.take(P, H * R).rearrange("p (k r) -> p k r", k=H)
        c_oD = b_oS[:, :, :].bitcast(bf16)
        c_oT = b_oD[:, 0:2, 0:H * R].bitcast(bf16)
        ring.reset()
        e_drow = ring.take(P, 2 * HE, bf16).rearrange("p (b n) -> p b n", b=2)
        e_oDT = ring.take(P, 4 * HE).rearrange("p (b n) -> p b n", b=4)
        e_o = ring.take(P, 4 * HE).rearrange("p (b n) -> p b n", b=4)
        e_h = ring.take(P, 4 * H * D).rearrange("p (b n) -> p b n", b=4)
        both = ring.at
        e_srow = ring.take(P, 2 * HE, bf16).rearrange("p (b n) -> p b n", b=2)
        e_oST = ring.take(P, 2 * HE).rearrange("p (b n) -> p b n", b=2)
        ring.at = both
        e_h2 = ring.take(P, 2 * H * D).rearrange("p (b n) -> p b n", b=2)
        e_hT = ring.take(P, HE).rearrange("p (b n) -> p b n", b=2)
        arow = WK[:].rearrange("p (b n) -> p b n", b=5)
        arow_top = WK[:].bitcast(bf16).rearrange("p (b n two) -> p b n two", b=5, two=2)[:, :, :, 1]
        FT = [F[0:D, k * NP:(k + 1) * NP] for k in range(6)]
        h128 = F[:, 2 * NP:3 * NP]
        Wsb = F[0:R, 2 * NP:2 * NP + D * D]
        Wall = F[0:D, 4 * NP:4 * NP + R * D].rearrange("p (r o) -> p r o", r=R)
        ystg = F[:, 4 * NP + R * D:4 * NP + 3 * R * D].rearrange("p (b n) -> p b n", b=2)
        compT = F[0:BASES, 3 * NP:3 * NP + R]
        basis = F[0:BASES, 3 * NP + R:3 * NP + R + D * D]
        i0row, o0row = RW[0:D, 0:NP], RW[0:D, NP:2 * NP]
        sm25 = tmp24
        NT_ = [NR[:, k * NB * D:(k + 1) * NB * D] for k in range(3)]
        psF = ps[0:D, 0:7, :].rearrange("p b n -> p (b n)")[:, 0:NP]
        psU = ps[D:P, 0:7, :].rearrange("p b n -> p (b n)")[:, 0:NP]
        psH = ps[:, 0:7, :].rearrange("p b n -> p (b n)")[:, 0:NP]
        psN = ps[:, 0:4, :].rearrange("p b n -> p (b n)")[:, 0:NB * D]
        wt = {n: wts[:, k, :] for k, n in enumerate(WEIGHTS)}
        pr = {n: prm[:, k:k + 1] for k, n in enumerate(PARAMS)}
        gram_sb, gw_sb, diag2, wc2 = (m64[:, k * D:(k + 1) * D] for k in range(4))
        PAD = slice(N, NP)

        def blocks_of(eng, n, which, most=NB - 1):
            return nc.values_load_multi_w_load_instructions(
                tab[0:1, bass.ds(n * H + which * NT, H)], engines=[eng.engine], min_val=0, max_val=most,
                skip_runtime_bounds_check_because="the kernel worked the table out itself")[1]

        block = ctx.enter_context(nc.Block())

        @block.gpsimd
        def _(pool):
            def link(ins):
                links[0] += 1
                ins.then_inc(S("pool_link"), 1)
                pool.wait_ge(S("pool_link"), links[0])
            links = [0]
            nc.gpsimd.iota(iota[:], pattern=[[1, P]], base=0, channel_multiplier=0,
                           allow_small_or_imprecise_dtypes=True).then_inc(S("const"), 1)
            nc.gpsimd.iota(pcol[:], pattern=[[0, 1]], base=0, channel_multiplier=1,
                           allow_small_or_imprecise_dtypes=True).then_inc(S("const"), 1)
            nc.gpsimd.iota(tcol[:, 0:TC], pattern=[[P, TC]], base=0, channel_multiplier=1,
                           allow_small_or_imprecise_dtypes=True).then_inc(S("const"), 1)
            nc.gpsimd.iota(edge25[:], pattern=[[NB, NB]], base=0, channel_multiplier=0,
                           allow_small_or_imprecise_dtypes=True).then_inc(S("const"), 1)
            nc.gpsimd.memset(ones[:], 1.0).then_inc(S("ones"), 1)
            nc.gpsimd.memset(gate[:], 0.0).then_inc(S("gate"), 1)
            after(pool, "ones")
            nc.gpsimd.affine_select(out=tri[:], in_=ones[:], compare_op=ALU.is_gt, fill=0.0, base=0,
                                    pattern=[[-1, P]], channel_multiplier=1).then_inc(S("tri"), 1)
            nc.gpsimd.affine_select(out=triT[:], in_=ones[:], compare_op=ALU.is_gt, fill=0.0, base=0,
                                    pattern=[[1, P]], channel_multiplier=-1).then_inc(S("tri"), 1)
            nc.gpsimd.affine_select(out=ident[:], in_=ones[:], compare_op=ALU.is_equal, fill=0.0, base=0,
                                    pattern=[[-1, P]], channel_multiplier=1).then_inc(S("ident"), 1)
            pool.wait_ge(S("filled"), 16)
            after(pool, "gate")
            with pool.Fori(0, IG // 2) as i:
                for b in range(2):
                    pool.wait_ge(S("idx_ready"), i * 2 + b + 1)
                    pool.wait_ge(S("gate"), i * 2 + b + 1)
                    nc.gpsimd.tensor_tensor(gate[0:1, 0:1], gate[0:1, 1:2], gate[0:1, 2:3],
                                            ALU.add).then_inc(S("gate"), 1)
                    for k in range(GT):
                        nc.gpsimd.indirect_dma_start(
                            out=slots, out_offset=bass.IndirectOffsetOnAxis(ap=idx[:, b, k:k + 1], axis=0),
                            in_=rec[:, b, k, :], in_offset=None).then_inc(S(f"scattered{b}"), 16)
            pool.wait_ge(S("y_out0"), 16 * 13)
            pool.wait_ge(S("y_out1"), 16 * 12)
            table = y_d.rearrange("n (r o) -> (n r) o", r=R)
            sorted_gates = IG

            def gather(i, b):
                n, slot, _ = stage_of(i, b, 0)
                wait_count(pool, S("l0_ys"), n - 3)
                pool.wait_ge(S("l0_idx"), n + 1)
                pool.wait_ge(S("gate"), sorted_gates + n + 1)
                nc.gpsimd.tensor_tensor(gate[0:1, 0:1], gate[0:1, 1:2], gate[0:1, 2:3],
                                        ALU.add).then_inc(S("gate"), 1)
                for k in range(H):
                    nc.gpsimd.indirect_dma_start(
                        out=l_y[:, slot, k, :], out_offset=None, in_=table,
                        in_offset=bass.IndirectOffsetOnAxis(ap=l_idx[:, slot, k:k + 1], axis=0)).then_inc(S(f"l0_y{slot}"), 16)
            half_rounds(pool, gather, 0)

        @block.sync
        def _(sp):
            sp.dma_start(src_c, A["src_c"]).then_inc(S("ids"), 16)
            for ap, name in ((wts[:], "weights"), (prm[:], "params"), (w1T[:], "w1T"), (w2T[:], "w2T"), (b1c[:], "b1")):
                sp.dma_start(ap, A[name]).then_inc(S("wts_in"), 16)
            sp.dma_start(dst_c, A["dst_c"]).then_inc(S("ids"), 16)
            sp.dma_start(typ_c, A["typ_c"]).then_inc(S("ids"), 16)
            after(sp, "fill_set")
            sp.dma_start(slots.rearrange("(p t) k -> p (t k)", p=P), fill).then_inc(S("filled"), 16)
            sp.wait_ge(S("rows_t"), 2 * 8)
            rows = IT // 8
            sp.dma_start(keyrow_d.rearrange("(c r) e -> r c e", r=rows), keyst).then_inc(S("rows_out"), 16)
            sp.dma_start(dbrow_d.rearrange("(c r) e -> r c e", r=rows), dbst).then_inc(S("rows_out"), 16)
            sp.wait_ge(S("rows_out"), 32)
            kd = keyrow_d.rearrange("t e -> (t e)").rearrange("(o n) -> o n", o=1)
            dd = dbrow_d.rearrange("t e -> (t e)").rearrange("(o n) -> o n", o=1)
            for b in range(2):
                sp.dma_start(krow[:, b, :], kd[:, b * GE:(b + 1) * GE].to_broadcast([ET, GE])).then_inc(S(f"krow{b}"), 16)
                sp.dma_start(drow[:, b, :], dd[:, b * GE:(b + 1) * GE].to_broadcast([NB, GE])).then_inc(S(f"krow{b}"), 16)
            with sp.Fori(1, IG // 2) as i:
                for b in range(2):
                    sp.wait_ge(S("idx_ready"), i * 2 + b - 1)
                    sp.dma_start(krow[:, b, :], kd[:, bass.ds((i * 2 + b) * GE, GE)].to_broadcast([ET, GE])).then_inc(S(f"krow{b}"), 16)
                    sp.dma_start(drow[:, b, :], dd[:, bass.ds((i * 2 + b) * GE, GE)].to_broadcast([NB, GE])).then_inc(S(f"krow{b}"), 16)
            after(sp, "bins")
            sp.dma_start(bins_d.rearrange("o (p s) -> (o p) s", s=NB), incl).then_inc(S("bins_out"), 16)
            sp.wait_ge(S("bins_out"), 16)
            after(sp, "scat_seen")
            sp.dma_start(binrow, bins_d.to_broadcast([P, BINS])).then_inc(S("binrow"), 16)
            sp.dma_start(F[:, 0:NT * 4].bitcast(i32), slots.rearrange("(p t) k -> p (t k)", p=P)).then_inc(S("slots_in"), 16)
            after(sp, "tab_c")
            with nc.allow_non_contiguous_dma(reason="one small table"):
                sp.dma_start(tab_d.rearrange("k (c p) -> p k c", p=P), tabc).then_inc(S("tab_out"), 16)
                sp.dma_start(same_d.rearrange("o (c p) -> p (o c)", p=P), samec).then_inc(S("tab_out"), 16)
            sp.wait_ge(S("tab_out"), 32)
            sp.dma_start(tab[:], tab_d.rearrange("k t -> (k t)").rearrange("(o n) -> o n", o=1)).then_inc(S("tab_in"), 16)
            sp.dma_start(same, same_d.to_broadcast([P, NT])).then_inc(S("tab_in"), 16)
            after(sp, "rows_s")
            sp.dma_start(slrow_d.rearrange("(c p) e -> p c e", p=P), rowst[:, 0]).then_inc(S("slrow_out"), 16)
            sp.dma_start(dlrow_d.rearrange("(c p) e -> p c e", p=P), rowst[:, 1]).then_inc(S("slrow_out"), 16)
            sp.wait_ge(S("slrow_out"), 32)
            after(sp, "fields")
            after(sp, "rows_s")
            sp.dma_start(compT, A["compT"]).then_inc(S("basis_in"), 16)
            sp.dma_start(basis, A["basis"]).then_inc(S("basis_in"), 16)
            sp.dma_start(FT[0][:, 0:N], A["xT"]).then_inc(S("xT_in"), 16)
            sp.wait_ge(S("W_sb"), 2)
            sp.dma_start(w_d, Wsb).then_inc(S("W_out"), 16)
            sp.wait_ge(S("W_out"), 16)
            with nc.allow_non_contiguous_dma(reason="rows of one relation"):
                sp.dma_start(Wall, w_d.rearrange("r (i o) -> i r o", i=D)).then_inc(S("W_in"), 16)
            for k in range(NB):
                sp.wait_ge(S("y_v"), k + 1)
                sp.wait_ge(S("y_a"), k + 1)
                sp.dma_start(y_d[k * P:(k + 1) * P, :], ystg[:, k % 2, :]).then_inc(S(f"y_out{k % 2}"), 16)

            srows = slrow_d.rearrange("t e -> (t e)").rearrange("(o n) -> o n", o=1)
            drows = dlrow_d.rearrange("t e -> (t e)").rearrange("(o n) -> o n", o=1)

            def put(i, b):
                n = 4 * i + b
                if stage_of(i, b, 0)[0] is not None:
                    wait_count(sp, S("l0_tr"), n - 1)
                    sp.dma_start(l_row[:, b % 2, :], drows[:, bass.ds(n * HE, HE)].to_broadcast([P, HE])).then_inc(S(f"l0_row{b % 2}"), 16)
                n, _, _ = stage_of(i, b, 1)
                if n is None:
                    return
                rows, cols_ = blocks_of(sp, n, 2, NB + TRASH - 1), blocks_of(sp, n, 0)
                for k in range(H):
                    sp.wait_ge(S("bl_acc"), n * H + k + 1)
                    sp.dma_start(A_sd[bass.ds(rows[k] * P, P), bass.ds(cols_[k] * P, P)], b_acc[:, k, 0:P]).then_inc(S(f"bl_out{k}"), 16)
            half_rounds(sp, put, 1)


            def product_rows(q, adj):
                def rounds(i):
                    for j in range(2 * PB):
                        n, (at, w) = i * 2 * PB + j, HALF[j % 2]
                        wait_count(sp, S("pr_mm"), n + q * PH - 4)
                        if q == 0:
                            wait_count(sp, S("odeg"), n - 4)
                        sp.dma_start(arow[:, j % 5, 0:w], adj[bass.ds((i * PB + j // 2) * P, P), at:at + w]).then_inc(S(f"arow{j % 5}"), 16)
                if q < 3:
                    sp.wait_ge(S(("l0_sc", "b_sc", "d_sc")[q]), M)
                rounds(0)
                with sp.Fori(1, NB // PB) as i:
                    rounds(i)

            def edge_rows(p):
                def body(i, b):
                    n = 4 * i + b
                    wait_count(sp, S(p + "_tr"), n - 1)
                    sp.dma_start(e_drow[:, b % 2, :], drows[:, bass.ds(n * HE, HE)].to_broadcast([P, HE])).then_inc(S(f"{p}_row{b % 2}"), 16)
                    if p == "b":
                        sp.dma_start(e_srow[:, b % 2, :], srows[:, bass.ds(n * HE, HE)].to_broadcast([P, HE])).then_inc(S(f"{p}_row{b % 2}"), 16)
                    else:
                        wait_count(sp, S("d_T"), n - 3)
                        sp.dma_start(e_h[:, b, :], h_d[bass.ds(n * P, P), :]).then_inc(S(f"d_in{b}"), 16)
                half_rounds(sp, body, 0)
            for k in range(4):
                sp.wait_ge(S(f"bl_out{k}"), M * 32)
            product_rows(0, A_sd)
            sp.wait_ge(S("pr_mm"), PH)
            sp.wait_ge(S("odeg"), PH)
            edge_rows("b")
            for b in range(4):
                sp.wait_ge(S(f"b_out{b}"), M // 4 * 16)
            product_rows(1, A_sd)
            sp.wait_ge(S("pr_mm"), 2 * PH)
            edge_rows("d")
            product_rows(2, A_sd)
            product_rows(3, A_ds)
            product_rows(4, A_sd)
            product_rows(5, A_ds)
            product_rows(6, A_sd)
            after(sp, "ln3")
            full = N // P
            on = NT_[1].rearrange("p (b d) -> p b d", d=D)
            sp.dma_start(out[0:full * P, :].rearrange("(b p) d -> p b d", p=P), on[:, 0:full, :]).then_inc(S("out"), 16)
            sp.dma_start(out[full * P:N, :], on[0:N - full * P, full, :]).then_inc(S("out"), 16)
            sp.wait_ge(S("out"), 32)

        @block.vector
        def _(dve):
            links = [0]

            def link(ins):
                links[0] += 1
                ins.then_inc(S("dve_link"), 1)
                dve.wait_ge(S("dve_link"), links[0])

            def mark(ins, name):
                ins.then_inc(*now(name))
                after(dve, name)

            V = nc.vector
            V.memset(fill, -1).then_inc(S("fill_set"), 1)
            dve.wait_ge(S("const"), 4)
            link(V.tensor_copy(iotab[:], iota[:]))
            dve.wait_ge(S("ids"), 48)
            link(V.tensor_single_scalar(posA[:, 0], dst_c, 7, op=ALU.arith_shift_right))
            link(V.tensor_single_scalar(posA[:, 1], src_c, 7, op=ALU.arith_shift_right))
            link(V.tensor_copy(dbf, posA[:, 0]))
            link(V.tensor_copy(sbf, posA[:, 1]))
            mark(V.scalar_tensor_tensor(out=key, in0=dbf, scalar=32.0, in1=sbf, op0=ALU.mult, op1=ALU.add), "key")
            for n, (st, dt) in enumerate(((keyst, f16), (dbst, bf16))):
                for c in range(8):
                    dve.wait_ge(S("row_tr"), n * 8 + c + 1)
                    V.tensor_copy(st[:, c, :], ps[0:rows8, c % 2, 0:ET]).then_inc(S("rows_t"), 1)
            def onehots(b, g):
                gs = bass.ds(g * GT, GT)
                V.tensor_tensor(ohD[:, b], dbf[:, gs].unsqueeze(2).to_broadcast([ET, GT, NB]),
                                iota[0:ET, 0:NB].unsqueeze(1).to_broadcast([ET, GT, NB]), ALU.is_equal)
                return V.tensor_tensor(ohS[:, b], sbf[:, gs].unsqueeze(2).to_broadcast([ET, GT, NB]),
                                       iota[0:ET, 0:NB].unsqueeze(1).to_broadcast([ET, GT, NB]), ALU.is_equal)
            for b in range(2):
                onehots(b, b).then_inc(S("oh"), 1)
            with dve.Fori(1, IG // 2) as i:
                for b in range(2):
                    g = i * 2 + b
                    dve.wait_ge(S("counted"), g - 1)
                    onehots(b, g).then_inc(S("oh"), 1)
            dve.wait_ge(S("C_in"), IG)
            dve.wait_ge(S("filled"), 16)
            link(V.memset(C[:, 0, :], 0.0))
            zero = WK[0:NB, 2000:2000 + IT]
            link(V.memset(zero, 0.0))
            for s in range(NB):
                last = V.tensor_tensor_scan(C[:, 1:IT + 1, s], C[:, 1:IT + 1, s], zero, 0.0, ALU.add, ALU.add)
                link(last)
            link(V.tensor_scalar(toti, C[:, IT, :], float(P - 1), None, ALU.add))
            link(V.tensor_single_scalar(toti2, toti, 7, op=ALU.arith_shift_right))
            link(V.tensor_scalar(nt_f, toti2, 1.0, None, ALU.max))
            link(V.memset(one25, 0.0))
            mark(V.tensor_tensor_scan(incl, nt_f, one25, 0.0, ALU.add, ALU.add), "rowtot")
            after(dve, "roff")
            link(V.tensor_copy(roff, ps[0:NB, 4, 0:1]))
            link(V.tensor_tensor(incl, incl, nt_f, ALU.subtract))
            mark(V.tensor_scalar(incl, incl, roff, None, ALU.add), "bins")
            link(V.tensor_scalar(tot, incl, float(P), None, ALU.mult))
            mark(V.tensor_tensor(C[:, 0:IT, :], C[:, 0:IT, :], tot.unsqueeze(1).to_broadcast([NB, IT, NB]), ALU.add), "based")
            dve.wait_ge(S("tri"), 2)

            def lookup(b, g, first):
                gs = bass.ds(g * GT, GT)
                q = (g - b) // 2 if isinstance(g, int) else None
                n = g + 1
                dve.wait_ge(S(f"krow{b}"), (half(g, b) + 1) * 32)
                if not first:
                    dve.wait_ge(S("looked"), g - 1)
                V.tensor_scalar(ohT[:, b, :], drow[:, b, :], pcol[0:NB, :], None, ALU.is_equal).then_inc(S("ohT"), 1)
                V.tensor_tensor(ohS[:, b], sbf[:, gs].unsqueeze(2).to_broadcast([ET, GT, NB]),
                                iota[0:ET, 0:NB].unsqueeze(1).to_broadcast([ET, GT, NB]), ALU.is_equal)
                V.tensor_tensor(kk, key[:, gs], zk, ALU.add).then_inc(S("kk"), 1)
                dve.wait_ge(S("kk"), n)
                for k in range(GT):
                    last = V.scalar_tensor_tensor(out=junk2[:, k % 2, :], in0=krow[:, b, k * ET:(k + 1) * ET], scalar=kk[:, k:k + 1],
                                                  in1=tri[0:ET, 0:ET], op0=ALU.is_equal, op1=ALU.mult,
                                                  accum_out=rank[:, k:k + 1])
                    last.then_inc(S("ranked"), 1)
                    dve.wait_ge(S("ranked"), g * GT + k + 1)
                dve.wait_ge(S("looked"), n)
                V.tensor_tensor(sel3, ps[0:ET, 5 + b, 0:GT * NB].rearrange("p (t s) -> p t s", s=NB), ohS[:, b], ALU.mult).then_inc(S("selected"), 1)
                dve.wait_ge(S("selected"), n)
                V.tensor_reduce(base_e, sel3, AX.X, ALU.add).then_inc(S("reduced"), 1)
                dve.wait_ge(S("reduced"), n)
                steps = [0]

                def step(ins):
                    steps[0] += 1
                    ins.then_inc(S("pos_step"), 1)
                    dve.wait_ge(S("pos_step"), g * 5 + steps[0])
                step(V.tensor_tensor(posi[:, 0], base_e, rank, ALU.add))
                step(V.tensor_single_scalar(posi[:, 1], posi[:, 0], 7, op=ALU.arith_shift_right))
                step(V.tensor_single_scalar(posi[:, 2], posi[:, 0], P - 1, op=ALU.bitwise_and))
                step(V.tensor_copy(posf, posi[:, 1]))
                if not first:
                    dve.wait_ge(S(f"scattered{b}"), half(g, b) * (16 * GT))
                V.tensor_single_scalar(rec[:, b, :, 1], src_c[:, gs], P - 1, op=ALU.bitwise_and)
                V.tensor_single_scalar(rec[:, b, :, 2], dst_c[:, gs], P - 1, op=ALU.bitwise_and)
                V.tensor_scalar(rec[:, b, :, 3], typ_c[:, gs], 0.0, None, ALU.add)
                step(V.scalar_tensor_tensor(out=rec[:, b, :, 0], in0=src_c[:, gs], scalar=float(R), in1=typ_c[:, gs], op0=ALU.mult, op1=ALU.add))
                V.scalar_tensor_tensor(out=idx[:, b, :], in0=posi[:, 2], scalar=float(NT), in1=posf, op0=ALU.mult, op1=ALU.add).then_inc(S("idx_ready"), 1)
                dve.wait_ge(S("idx_ready"), n)

            def half(g, b):
                return hb[0]
            hb = [0]
            link(V.memset(zk, 0.0))
            for b in range(2):
                lookup(b, b, True)
            with dve.Fori(1, IG // 2) as i:
                for b in range(2):
                    hb[0] = i
                    lookup(b, i * 2 + b, False)
            for b in range(2):
                dve.wait_ge(S(f"scattered{b}"), IG // 2 * 16 * GT)
            mark(V.memset(binjunk[:, 0:1], 0.0), "scat_seen")
            link(V.tensor_scalar(tcol[:, TC:2 * TC], tcol[:, 0:TC], -1.0, None, ALU.add))
            link(V.tensor_scalar(tcol[:, 2 * TC:3 * TC], tcol[:, 0:TC], 1.0, None, ALU.add))
            dve.wait_ge(S("binrow"), 16)
            for c in range(3 * TC):
                link(V.tensor_scalar(binjunk, binrow, tcol[:, c:c + 1], 0.0, ALU.is_le, ALU.add, accum_out=kcol[:, c:c + 1]))
            link(V.tensor_scalar(kcol, kcol, -1.0, None, ALU.add))
            for c in range(TC):
                link(V.tensor_scalar(tmp24, edge25, kcol[:, c:c + 1], 0.0, ALU.is_le, ALU.add, accum_out=dbc[:, c:c + 1]))
            link(V.tensor_scalar(dbc, dbc, -1.0, None, ALU.add))
            link(V.scalar_tensor_tensor(out=sbc, in0=dbc, scalar=-float(NB), in1=kcol[:, 0:TC], op0=ALU.mult, op1=ALU.add))
            link(V.tensor_tensor(samec, kcol[:, 0:TC], kcol[:, TC:2 * TC], ALU.is_equal))
            link(V.tensor_scalar(tmp24[:, 0:TC], tcol[:, 0:TC], float(NT - 1), None, ALU.is_equal))
            link(V.tensor_tensor(kcol[:, 2 * TC:3 * TC], kcol[:, 2 * TC:3 * TC], tmp24[:, 0:TC], ALU.add))
            link(V.tensor_tensor(fin, kcol[:, 0:TC], kcol[:, 2 * TC:3 * TC], ALU.not_equal))
            link(V.tensor_copy(tri4, tcol[:, 0:TC]))
            link(V.tensor_single_scalar(tri4b, tri4, TRASH - 1, op=ALU.bitwise_and))
            link(V.tensor_scalar(tr4, tri4b, float(NB), None, ALU.add))
            link(V.tensor_copy(tabc[:, 0], dbc))
            link(V.tensor_copy(tabc[:, 1], sbc))
            for k, blk in ((2, sbc), (3, dbc)):
                link(V.tensor_tensor(tmp24[:, 0:TC], blk, tr4, ALU.subtract))
                link(V.tensor_tensor(tmp24[:, 0:TC], tmp24[:, 0:TC], fin, ALU.mult))
                ins = V.tensor_tensor(tabc[:, k], tmp24[:, 0:TC], tr4, ALU.add)
                link(ins) if k == 2 else mark(ins, "tab_c")
            dve.wait_ge(S("slots_in"), 16)
            link(V.tensor_copy(slf[:], slot_i[:, :, 1]))
            link(V.tensor_copy(tyf, slot_i[:, :, 3]))
            link(V.tensor_scalar(yidx, slot_i[:, :, 0], 0.0, None, ALU.max))
            mark(V.tensor_copy(dlf[:], slot_i[:, :, 2]), "fields")
            for n in range(2):
                for c in range(TC):
                    dve.wait_ge(S("slot_tr"), n * TC + c + 1)
                    ins = V.tensor_copy(rowst[:, n, c, :], ps[:, (n * TC + c) % 2, 0:P])
                    ins.then_inc(S("slot_cp"), 1)
            dve.wait_ge(S("slot_cp"), 2 * TC)
            V.memset(binjunk[:, 0:1], 0.0).then_inc(S("rows_s"), 1)
            dve.wait_ge(S("slrow_out"), 32)
            link(V.memset(xs[:, :, D:2 * D], 0.0))
            mark(V.memset(epsc[:], EPS), "consts2")
            mark(V.memset(zerob[:], 0.0), "zerob")
            after(dve, "rows_s")
            dve.wait_ge(S("tab_in"), 32)
            mark(V.memset(FT[0][:, PAD], 0.0), "xpad")
            after(dve, "W_ps")
            V.tensor_copy(Wsb[:, 0:4 * BANK], ps[0:R, 0:4, :].rearrange("p b n -> p (b n)")).then_inc(S("W_sb"), 1)
            for k in range(NB):
                dve.wait_ge(S("y_ps"), k + 1)
                if k >= 2:
                    dve.wait_ge(S(f"y_out{k % 2}"), 16 * (k // 2))
                V.tensor_copy(ystg[:, k % 2, 0:R * D // 2], ps[:, 2 * (k % 2), 0:R * D // 2]).then_inc(S("y_v"), 1)

            def onehot(o, column, n, width=P, tiles=H):
                return V.tensor_tensor(o.rearrange("p (k n) -> p k n", k=tiles), column[:, bass.ds(n * tiles, tiles)].unsqueeze(2).to_broadcast([P, tiles, width]),
                                       iota[:, 0:width].unsqueeze(1).to_broadcast([P, tiles, width]), ALU.is_equal)

            def counts(i, b, n):
                wait_count(dve, S("c_mm"), n - 1)
                onehot(c_oD[:, b, :], dlf, n, P, 2 * H)
                onehot(c_oT[:, b, :], tyf, n, R, 2 * H).then_inc(S("c_oh"), 1)
            counting_rounds(dve, counts)
            after(dve, "cnt")
            link(V.tensor_copy(cnt[:], ps[:, 7, 0:NB * 16]))
            link(V.tensor_scalar(inv[:], cnt[:], 1.0, None, ALU.max))
            mark(V.reciprocal(inv[:], inv[:]), "inv")

            def build(i, b):
                n, s4, _ = stage_of(i, b, 0)
                u, u4, _ = stage_of(i, b, 1)

                def running(k):
                    if u is None:
                        return
                    if k % 2 == 0:
                        dve.wait_ge(S("bl_mm"), u * 2 + k // 2 + 1)
                    wait_count(dve, S(f"bl_out{k}"), u * 32)
                    wait_count(dve, S("bl_acc"), u * H + k)
                    V.scalar_tensor_tensor(out=b_acc[:, k, :], in0=b_acc[:, (k - 1) % 4, :], scalar=b_same[:, u4 % 2, k:k + 1],
                                           in1=ps[:, 5 + k // 2, (k % 2) * 2 * P:(k % 2 + 1) * 2 * P],
                                           op0=ALU.mult, op1=ALU.add).then_inc(S("bl_acc"), 1)
                running(0)
                if n is not None:
                    wait_count(dve, S("bl_mm"), (n - 1) * 2 if not isinstance(n, int) or n > 1 else 0)
                    wait_count(dve, S("l0_sc"), n - 3)
                    onehot(b_oS[:, b % 2, :], slf, n)
                running(1)
                if n is not None:
                    onehot(b_oD[:, s4, :], dlf, n).then_inc(S("bl_oh"), 1)
                running(2)
                if n is not None:
                    wait_count(dve, S(f"l0_y{s4}"), i * 64)
                    V.tensor_scalar(l_idx[:, s4, :], yidx[:, bass.ds(n * H, H)], 0.0, None, ALU.add).then_inc(S("l0_idx"), 1)
                    dve.wait_ge(S(f"l0_row{b % 2}"), (2 * i + b // 2 + 1) * 16)
                    wait_count(dve, S("l0_g"), n - 1)
                    V.tensor_scalar(l_oDT[:, b % 2, :], l_row[:, b % 2, :], pcol[:], None, ALU.is_equal).then_inc(S("l0_tr"), 1)
                running(3)
                if u is not None:
                    dve.wait_ge(S("l0_g"), u + 1)
                    V.tensor_tensor(l_g, ps[:, (4, 7)[u4 % 2], 0:H * 16].rearrange("p (k r) -> p k r", r=16)[:, :, 0:R],
                                    l_oT[:, u4 % 2], ALU.mult).then_inc(S("l0_sel"), 1)
                    dve.wait_ge(S("l0_sel"), u + 1)
                    wait_count(dve, S("l0_ys"), u - 1)
                    V.tensor_reduce(l_w[:, u4 % 2, :], l_g, AX.X, ALU.add).then_inc(S("l0_w"), 1)
                    dve.wait_ge(S("l0_w"), u + 1)
                if n is not None:
                    V.tensor_scalar(b_same[:, b % 2, :], same[:, bass.ds(n * H, H)], 0.0, None, ALU.add)
                    onehot(l_oT[:, b % 2].rearrange("p k r -> p (k r)"), tyf, n, R).then_inc(S("l0_oT"), 1)
                    dve.wait_ge(S("l0_oT"), n + 1)
            link(V.memset(b_acc[:, 3, :], 0.0))
            half_rounds(dve, build, 1)
            link(V.memset(cols[:], 0.0))

            vl = slice(0, N)

            def col(k):
                return cols[:, k:k + 1]

            def ln(tag, o, t):
                def blocks(ap):
                    return ap.rearrange("p (b d) -> p b d", d=D)

                def spread(k):
                    return stat[:, k, :].unsqueeze(2).to_broadcast([P, NB, D])
                after(dve, tag + "_ps")
                link(V.tensor_reduce(stat[:, 0, :], blocks(psN), AX.X, ALU.add))
                link(V.tensor_scalar(stat[:, 0, :], stat[:, 0, :], 1.0 / D, None, ALU.mult))
                link(V.tensor_tensor(blocks(o), blocks(psN), spread(0), ALU.subtract))
                link(V.tensor_tensor(t, o, o, ALU.mult))
                link(V.tensor_reduce(stat[:, 1, :], blocks(t), AX.X, ALU.add))
                mark(V.tensor_scalar(stat[:, 1, :], stat[:, 1, :], 1.0 / D, None, ALU.mult), tag + "_var")
                after(dve, tag + "_std")
                link(V.reciprocal(stat[:, 1, :], stat[:, 1, :]))
                mark(V.tensor_tensor(blocks(o), blocks(o), spread(1), ALU.mult), tag)

            def ln_T(tag, o):
                after(dve, tag + "T_ps")
                link(V.tensor_copy(o, psF))
                mark(V.memset(o[:, PAD], 0.0), tag + "T")

            def affine(tag, m, var, g, be, s_, t_):
                mark(V.tensor_scalar(var, var, 1.0, None, ALU.mult), tag + "_var")
                after(dve, tag + "_std")
                link(V.reciprocal(s_, s_))
                if g is not None:
                    link(V.tensor_tensor(s_, s_, g, ALU.mult))
                link(V.tensor_tensor(t_, m, s_, ALU.mult))
                if be is not None:
                    link(V.tensor_tensor(t_, be, t_, ALU.subtract))
                else:
                    link(V.tensor_scalar(t_, t_, -1.0, None, ALU.mult))

            def bn(tag, X, o, g, be, relu):
                link(V.tensor_reduce(col(0), X[:, vl], AX.X, ALU.add))
                link(V.tensor_scalar(col(0), col(0), 1.0 / N, None, ALU.mult))
                link(V.tensor_scalar(X[:, vl], X[:, vl], col(0), None, ALU.subtract))
                link(V.scalar_tensor_tensor(out=o[:, vl], in0=X[:, vl], scalar=1.0, in1=X[:, vl], op0=ALU.mult, op1=ALU.mult,
                                            accum_out=col(1)))
                link(V.tensor_scalar(col(1), col(1), 1.0 / N, None, ALU.mult))
                link(V.memset(col(2), 0.0))
                affine(tag, col(2), col(1), g, be, col(3), col(4))
                link(V.tensor_scalar(o[:, vl], X[:, vl], col(3), col(4), ALU.mult, ALU.add))
                if relu:
                    link(V.tensor_scalar(o[:, vl], o[:, vl], 0.0, None, ALU.max))
                mark(V.memset(o[:, PAD], 0.0), tag)

            def dot(o, a, op, sc, b_, acc):
                link(V.scalar_tensor_tensor(out=o[:, vl], in0=a[:, vl], scalar=sc, in1=b_[:, vl], op0=op, op1=ALU.mult, accum_out=acc))

            def split(q, src):
                def rounds(i):
                    for j in range(PB):
                        x = src[:, bass.ds((i * PB + j) * D, D)]
                        parts = [xb[:, j, k * D:(k + 1) * D] for k in range(3)]
                        n = i * PB * 4 + (q - 1) * NB * 4 + j * 4
                        wait_count(dve, S("pr_mm"), i * 2 * PB + q * PH + 2 * (j - PB + 1))
                        V.tensor_copy(parts[0], x).then_inc(S("split"), 1)
                        dve.wait_ge(S("split"), n + 1)
                        V.tensor_tensor(rest[:, j, :], x, parts[0], ALU.subtract).then_inc(S("split"), 1)
                        dve.wait_ge(S("split"), n + 2)
                        V.tensor_copy(parts[1], rest[:, j, :]).then_inc(S("split"), 1)
                        dve.wait_ge(S("split"), n + 3)
                        V.tensor_tensor(parts[2], rest[:, j, :], parts[1], ALU.subtract).then_inc(S("split"), 1)
                        dve.wait_ge(S("split"), n + 4)
                        V.memset(rest[0:1, j, 0:1], 0.0).then_inc(S("pr_xb"), 1)
                rounds(0)
                with dve.Fori(1, NB // PB) as i:
                    rounds(i)

            def sums_of(q, o, upper):
                dve.wait_ge(S("pr_mm"), (q + 1) * PH)
                dve.wait_ge(S("upper"), q)
                link(V.tensor_tensor(o, psF, upper, ALU.add))

            dve.wait_ge(S("wts_in"), 80)
            link(V.tensor_reduce(sm25, cnt[:].rearrange("p (b r) -> p b r", r=16)[:, :, 0:R], AX.X, ALU.add))
            link(V.tensor_copy(NT_[0].rearrange("p (b d) -> p b d", d=D), sm25.unsqueeze(2).to_broadcast([P, NB, D])))
            after(dve, "acc0")
            mark(V.tensor_copy(NT_[1], psN), "acc0N")
            after(dve, "i0_ps")
            mark(V.tensor_copy(i0row, psF), "i0_sb")
            after(dve, "acc0_ps")
            mark(V.tensor_copy(FT[1], psF), "acc0T")
            after(dve, "root_ps")
            link(V.tensor_tensor(FT[2], psF, FT[1], ALU.add))
            link(V.tensor_scalar(FT[2], FT[2], pr["L0_gnn_bias"], 0.0, ALU.add, ALU.max))
            mark(V.tensor_tensor(FT[2], FT[2], FT[0], ALU.add), "ln0_in")
            ln("ln0", NT_[0], NT_[2])
            ln_T("ln0", FT[0])

            for k in range(PH):
                dve.wait_ge(S(f"arow{k % 5}"), 16 * (k // 5 + 1))
                V.tensor_reduce(oparts[:, k // 2, k % 2:k % 2 + 1], arow[:, k % 5, 0:HALF[k % 2][1]], AX.X, ALU.add).then_inc(S("odeg"), 1)
            dve.wait_ge(S("odeg"), PH)
            link(V.tensor_reduce(odeg[:], oparts[:], AX.X, ALU.add))
            link(V.tensor_reduce(large[:], odeg[:], AX.X, ALU.max))
            mark(V.tensor_scalar(large[:], large[:], 256.0, None, ALU.is_gt), "large")
            dve.wait_ge(S("pr_mm"), PH)
            after(dve, "large_ps")
            mark(V.tensor_copy(flag[:], ps[0:1, 7, 0:1]), "flag")
            mark(V.tensor_tensor(FT[1], psF, FT[0], ALU.add), "dsum")
            mark(V.tensor_copy(NT_[1].rearrange("p (b d) -> p b d", d=D), odeg[:].unsqueeze(2).to_broadcast([P, NB, D])), "odeg_rep")
            after(dve, "o0_ps")
            mark(V.tensor_copy(o0row, psF), "o0_sb")
            after(dve, "P_ps")
            mark(V.tensor_copy(FT[2], psF), "P_sb")
            after(dve, "Q_ps")
            mark(V.tensor_scalar(FT[3], psF, pr["L1_gnn_b_unite"], None, ALU.add), "Q_sb")
            after(dve, "DT_ps")
            mark(V.tensor_copy(FT[4], psF), "DT_sb")
            dot(FT[5], o0row, ALU.add, 1.0, FT[2], col(5))
            dot(FT[1], FT[5], ALU.mult, 1.0, FT[2], col(6))
            dot(FT[5], i0row, ALU.add, 1.0, FT[3], col(7))
            dot(FT[1], FT[5], ALU.mult, 1.0, FT[3], col(8))
            dot(FT[1], FT[4], ALU.mult, 2.0, FT[3], col(9))

            def row_stats(tag, sums, squares, g, be):
                link(V.tensor_tensor(col(0), sums[0], sums[1], ALU.add))
                link(V.tensor_scalar(col(0), col(0), 1.0 / ALL, None, ALU.mult))
                link(V.tensor_tensor(col(1), squares[0], squares[1], ALU.add))
                link(V.tensor_tensor(col(1), col(1), squares[2], ALU.add))
                link(V.tensor_tensor(col(2), col(0), col(0), ALU.mult))
                link(V.scalar_tensor_tensor(out=col(1), in0=col(1), scalar=1.0 / ALL, in1=col(2), op0=ALU.mult, op1=ALU.subtract))
                affine(tag, col(0), col(1), g, be, col(3), col(4))
            row_stats("bn1", (col(5), col(7)), (col(6), col(8), col(9)), pr["L1_gnn_g1"], pr["L1_gnn_be1"])
            link(V.tensor_scalar(FT[2], FT[2], col(3), None, ALU.mult))
            link(V.tensor_scalar(FT[3], FT[3], col(3), col(4), ALU.mult, ALU.add))
            link(V.memset(FT[2][:, PAD], 0.0))
            mark(V.memset(FT[3][:, PAD], 0.0), "PQ")
            link(V.tensor_tensor(FT[4], FT[2], FT[3], ALU.add))
            link(V.tensor_scalar(FT[4], FT[4], 0.0, None, ALU.max))
            after(dve, "PN")
            after(dve, "QN")
            link(V.tensor_tensor(NT_[2], NT_[0], NT_[1], ALU.add))
            mark(V.tensor_scalar(NT_[2], NT_[2], 0.0, None, ALU.max), "hsN")

            def onehot_round(p, which):
                def body(i, b):
                    n, s4, _ = stage_of(i, b, 0)
                    if n is not None:
                        dve.wait_ge(S(f"{p}_row{b % 2}"), (2 * i + b // 2 + 1) * (32 if p == "b" else 16))
                        wait_count(dve, S(p + "_sc"), n - 3)
                        if p == "b":
                            wait_count(dve, S("b_z"), n - 1)
                            V.tensor_scalar(e_oST[:, b % 2, :], e_srow[:, b % 2, :], pcol[:], None, ALU.is_equal)
                        V.tensor_scalar(e_oDT[:, s4, :], e_drow[:, b % 2, :], pcol[:], None, ALU.is_equal).then_inc(S(p + "_tr"), 1)
                        onehot(e_o[:, s4, :], (dlf, slf)[which], n).then_inc(S(p + "_o"), 1)
                return body
            dve.wait_ge(S("pr_mm"), PH)
            half_rounds(dve, onehot_round("b", 0), 0)
            after(dve, "accb")
            mark(V.tensor_tensor(NT_[2], NT_[2], psN, ALU.add), "s")
            after(dve, "s_ps")
            mark(V.tensor_copy(FT[5], psF), "sT")
            split(1, NT_[2])
            sums_of(1, FT[1], FT[3])
            mark(V.memset(cols[:, 21:22], 0.0), "msg")
            after(dve, "R_ps")
            mark(V.tensor_scalar(FT[2], psF, pr["L1_gnn_b_gconv"], None, ALU.add), "R_sb")
            after(dve, "sW_ps")
            mark(V.tensor_copy(FT[3], psF), "sW_sb")
            after(dve, "gram_up")
            mark(V.tensor_tensor(gram_sb, ps[0:D, 7, 0:D], diag2, ALU.add), "gram_sb")
            after(dve, "GW_ps")
            mark(V.tensor_tensor(gw_sb, ps[0:D, 7, 0:D], wt["gconv_h"], ALU.mult), "GW_sb")
            after(dve, "Mc_ps")
            link(V.tensor_copy(col(10), ps[0:D, 7, 0:1]))
            link(V.tensor_reduce(col(5), FT[3][:, vl], AX.X, ALU.add))
            dot(FT[1], i0row, ALU.add, 1.0, FT[2], col(7))
            dot(FT[1], FT[1], ALU.mult, 1.0, FT[2], col(8))
            dot(FT[1], FT[3], ALU.mult, 2.0, FT[2], col(9))
            row_stats("bn2", (col(5), col(7)), (col(10), col(8), col(9)), pr["L1_gnn_g2"], pr["L1_gnn_be2"])
            mark(V.tensor_scalar(diag2, ident[0:D, 0:D], col(3), None, ALU.mult), "diag2")
            link(V.tensor_scalar(FT[2], FT[2], col(3), col(4), ALU.mult, ALU.add))
            mark(V.memset(FT[2][:, PAD], 0.0), "RT")
            after(dve, "wc2_ps")
            link(V.memset(wc2s[:], 0.0))
            link(V.tensor_copy(wc2s[0:D, 0:D], ps[0:D, 7, 0:D]))
            link(V.tensor_copy(wc2s[D:P, D:2 * D], ps[0:D, 7, 0:D]))
            mark(V.tensor_copy(wc2, ps[0:D, 7, 0:D]), "wc2")
            after(dve, "h2_ps")
            link(V.tensor_tensor(FT[4], psF, FT[2], ALU.add))
            link(V.tensor_scalar(FT[4], FT[4], 0.0, None, ALU.max))
            mark(V.memset(cols[:, 20:21], 0.0), "h2")
            half_rounds(dve, onehot_round("d", 1), 0)
            after(dve, "accd")
            mark(V.tensor_copy(NT_[2], psN), "accdN")
            after(dve, "accd_ps")
            mark(V.tensor_tensor(FT[5], psF, FT[4], ALU.add), "agg")
            after(dve, "t_ps")
            link(V.tensor_scalar(FT[1], psF, pr["L1_gnn_b_transfer"], None, ALU.add))
            bn("bnt", FT[1], FT[2], pr["L1_gnn_g2"], pr["L1_gnn_be2"], True)
            after(dve, "lin_ps")
            link(V.tensor_scalar(FT[3], psF, pr["L1_gnn_b_lin"], 0.0, ALU.add, ALU.max))
            bn("bnl", FT[3], FT[4], pr["L1_gnn_g3"], pr["L1_gnn_be3"], True)
            mark(V.tensor_tensor(FT[5], FT[0], FT[4], ALU.add), "ln1_in")
            ln("ln1", NT_[0], NT_[2])
            ln_T("ln1", FT[0])

            link(V.tensor_scalar(sm25, sm25, 1.0, None, ALU.max))
            mark(V.memset(cols[:, 22:23], 0.0), "deg1")
            after(dve, "deg_sqrt")
            link(V.reciprocal(sm25, sm25))
            mark(V.tensor_copy(NT_[1].rearrange("p (b d) -> p b d", d=D), sm25.unsqueeze(2).to_broadcast([P, NB, D])), "norm_rep")
            after(dve, "norm_ps")
            link(V.tensor_copy(i0row, psF))
            dve.wait_ge(S("normt_in"), 16)
            link(V.memset(o0row[:, PAD], 0.0))
            link(V.tensor_scalar(FT[1], FT[0], 0.0, None, ALU.max))
            for k, (q, w) in enumerate(((2, "y1"), (4, "y2"))):
                bn(f"bnh{k}", FT[1], FT[2], None, None, False)
                after(dve, f"hN{k}")
                for j, (row, o) in enumerate(((i0row, FT[3]), (o0row, FT[4]))):
                    split(q + j, NT_[0])
                    sums_of(q + j, o, FT[5])
                    link(V.tensor_tensor(o, o, FT[2], ALU.add))
                    mark(V.tensor_tensor(o, o, row, ALU.mult), f"agg{q + j}")
                after(dve, w + "_ps")
                if k == 0:
                    link(V.tensor_scalar(FT[1], psF, 0.0, None, ALU.max))
            mark(V.scalar_tensor_tensor(out=FT[5], in0=FT[0], scalar=2.0, in1=psF, op0=ALU.mult, op1=ALU.add), "ln2_in")
            ln("ln2", NT_[0], NT_[2])
            ln_T("ln2", FT[0])

            split(6, NT_[0])
            sums_of(6, FT[1], FT[5])
            mark(V.memset(cols[:, 21:22], 0.0), "m3")
            after(dve, "h128_ps")
            mark(V.tensor_scalar(h128, psH, b1c[:], 0.0, ALU.add, ALU.max), "h128")
            after(dve, "up_ps")
            link(V.tensor_scalar(FT[3], psF, pr["L3_gnn_b2"], 0.0, ALU.add, ALU.max))
            mark(V.scalar_tensor_tensor(out=FT[5], in0=FT[0], scalar=2.0, in1=FT[3], op0=ALU.mult, op1=ALU.add), "ln3_in")
            ln("ln3", NT_[1], NT_[2])

        @block.scalar
        def _(act):
            act.wait_ge(S("filled"), 16)
            after(act, "key")
            with act.Fori(0, IG // 2) as i:
                for b in range(2):
                    g = i * 2 + b
                    act.wait_ge(S("counted"), g + 1)
                    nc.scalar.activation(C[:, bass.ds(g * GT + 1, GT), :], ps[0:NB, 2 + b, 0:GT * NB].rearrange("p (t s) -> p t s", s=NB),
                                         ACT.Copy).then_inc(S("C_in"), 1)
            after(act, "based")
            for b in range(2):
                nc.scalar.activation(cg[:, b, :].rearrange("p (t s) -> p t s", s=NB), C[:, b * GT:(b + 1) * GT, :], ACT.Copy).then_inc(S("cg"), 1)
            with act.Fori(1, IG // 2) as i:
                for b in range(2):
                    g = i * 2 + b
                    act.wait_ge(S("looked"), g - 1)
                    nc.scalar.activation(cg[:, b, :].rearrange("p (t s) -> p t s", s=NB), C[:, bass.ds(g * GT, GT), :], ACT.Copy).then_inc(S("cg"), 1)


            after(act, "W_ps")
            nc.scalar.activation(Wsb[:, 4 * BANK:8 * BANK], ps[0:R, 4:8, :].rearrange("p b n -> p (b n)"), ACT.Copy).then_inc(S("W_sb"), 1)
            for k in range(NB):
                act.wait_ge(S("y_ps"), k + 1)
                if k >= 2:
                    act.wait_ge(S(f"y_out{k % 2}"), 16 * (k // 2))
                nc.scalar.activation(ystg[:, k % 2, R * D // 2:R * D], ps[:, 2 * (k % 2) + 1, 0:R * D // 2], ACT.Copy).then_inc(S("y_a"), 1)

            act.wait_ge(S("tab_in"), 32)

            def put(i, b):
                n, s4, i4 = stage_of(i, b, 1)
                if n is None:
                    return
                rows, cols_ = blocks_of(act, n, 3, NB + TRASH - 1), blocks_of(act, n, 1)
                for k in range(H):
                    act.wait_ge(S("bl_acc"), n * H + k + 1)
                    act.dma_start(A_ds[bass.ds(rows[k] * P, P), bass.ds(cols_[k] * P, P)], b_acc[:, k, P:2 * P]).then_inc(S(f"bl_out{k}"), 16)
                act.wait_ge(S("l0_w"), n + 1)
                act.wait_ge(S(f"l0_y{s4}"), (i4 + 1) * 64)
                wait_count(act, S("l0_sc"), n - 1)
                for k in range(H):
                    last = nc.scalar.activation(l_ys[:, s4 % 2, k, :], l_y[:, s4, k, :], ACT.Copy, scale=l_w[:, s4 % 2, k:k + 1])
                last.then_inc(S("l0_ys"), 1)
            half_rounds(act, put, 1)

            def std(tag, o, in_, prior):
                after(act, prior)
                nc.scalar.activation(o, in_, ACT.Sqrt, bias=epsc[0:o.shape[0], :]).then_inc(S(tag), 1)

            def to_sb(name, o, in_):
                after(act, name + "_ps")
                nc.scalar.activation(o, in_, ACT.Copy).then_inc(*now(name))

            def stationary(q, src):
                def rounds(i):
                    for j in range(PB):
                        wait_count(act, S("pr_mm"), i * 2 * PB + q * PH + 2 * (j - PB + 1))
                        nc.scalar.activation(xs[:, j, 0:D], src[:, bass.ds((i * PB + j) * D, D)], ACT.Copy).then_inc(S("pr_xs"), 1)
                rounds(0)
                with act.Fori(1, NB // PB) as i:
                    rounds(i)

            def upper(q, o):
                act.wait_ge(S("pr_mm"), (q + 1) * PH)
                nc.scalar.activation(o, psU, ACT.Copy).then_inc(S("upper"), 1)

            def product_in(q, name, k=0):
                to_sb(name, NT_[k], psN)
                after(act, name)
                stationary(q, NT_[k])
            after(act, "consts2")
            std("ln0_std", stat[:, 1, :], stat[:, 1, :], "ln0_var")
            after(act, "ln0")
            stationary(0, NT_[0])
            std("bn1_std", cols[:, 3:4], cols[:, 1:2], "bn1_var")
            to_sb("PN", NT_[0], psN)
            to_sb("QN", NT_[1], psN)

            def relu_rounds(p):
                def body(i, b):
                    if p == "d":
                        n, s4, _ = stage_of(i, b, 1)
                        if n is not None:
                            act.wait_ge(S("d_u"), n + 1)
                            wait_count(act, S("d_sc"), n - 1)
                            nc.scalar.activation(e_h2[:, s4 % 2, :], ps[:, (4, 7)[s4 % 2], 0:H * D], ACT.Relu).then_inc(S("d_h2"), 1)
                        n, s4, _ = stage_of(i, b, 0)
                        if n is not None:
                            act.wait_ge(S("d_T"), n + 1)
                            wait_count(act, S("d_u"), n - 1)
                            nc.scalar.activation(e_hT[:, s4 % 2, :], ps[:, 5 + s4 % 2, 0:HE // 2], ACT.Copy).then_inc(S("d_hT"), 1)
                    else:
                        n, _, _ = stage_of(i, b, 0)
                        if n is not None:
                            act.wait_ge(S("b_z"), n + 1)
                            wait_count(act, S("b_sc"), n - 3)
                            wait_count(act, S(f"b_out{b}"), i * 16)
                            nc.scalar.activation(e_h[:, b, :], ps[:, 4 + b % 2, 0:H * D], ACT.Relu).then_inc(S("b_h"), 1)
                        n, s4, _ = stage_of(i, b, 1)
                        if n is not None:
                            act.wait_ge(S("b_h"), n + 1)
                            act.dma_start(h_d[bass.ds(n * P, P), :], e_h[:, s4, :]).then_inc(S(f"b_out{s4}"), 16)
                half_rounds(act, body, 1)
            relu_rounds("b")
            after(act, "accb")
            nc.scalar.activation(diag2, ps[D:P, 7, D:2 * D], ACT.Copy).then_inc(*now("gram_up"))
            after(act, "s")
            stationary(1, NT_[2])
            upper(1, FT[3])
            std("bn2_std", cols[:, 3:4], cols[:, 1:2], "bn2_var")
            act.wait_ge(S("pr_mm"), 2 * PH)
            to_sb("RN", NT_[2], psN)
            after(act, "RN")
            relu_rounds("d")
            std("bnt_std", cols[:, 3:4], cols[:, 1:2], "bnt_var")
            std("bnl_std", cols[:, 3:4], cols[:, 1:2], "bnl_var")
            std("ln1_std", stat[:, 1, :], stat[:, 1, :], "ln1_var")
            act.dma_start(o0row[:, 0:N], A["normt"].to_broadcast([D, N])).then_inc(S("normt_in"), 16)
            after(act, "deg1")
            nc.scalar.activation(sm25, sm25, ACT.Sqrt).then_inc(*now("deg_sqrt"))
            for k, q in enumerate((2, 4)):
                std(f"bnh{k}_std", cols[:, 3:4], cols[:, 1:2], f"bnh{k}_var")
                product_in(q, f"hN{k}")
                upper(q, FT[5])
                stationary(q + 1, NT_[0])
                upper(q + 1, FT[5])
            std("ln2_std", stat[:, 1, :], stat[:, 1, :], "ln2_var")
            after(act, "ln2")
            stationary(6, NT_[0])
            upper(6, FT[5])
            std("ln3_std", stat[:, 1, :], stat[:, 1, :], "ln3_var")

        @block.tensor
        def _(pe):
            after(pe, "ident")
            after(pe, "key")
            for n, col in enumerate((key, dbf)):
                for c in range(8):
                    m = n * 8 + c
                    if m >= 2:
                        pe.wait_ge(S("rows_t"), m - 1)
                    nc.tensor.transpose(ps[0:rows8, c % 2, 0:ET], col[:, c * rows8:(c + 1) * rows8],
                                        ident[0:ET, 0:ET]).then_inc(S("row_tr"), 1)
            def count(b, g, first):
                pe.wait_ge(S("oh"), g + 1)
                if not first:
                    pe.wait_ge(S("C_in"), g - 1)
                for k in range(GT):
                    last = nc.tensor.matmul(ps[0:NB, 2 + b, k * NB:(k + 1) * NB], ohD[:, b, k, :], ohS[:, b, k, :], start=True, stop=True)
                last.then_inc(S("counted"), 1)
            for b in range(2):
                count(b, b, True)
            with pe.Fori(1, IG // 2) as i:
                for b in range(2):
                    count(b, i * 2 + b, False)
            after(pe, "rowtot")
            pe.wait_ge(S("tri"), 2)
            nc.tensor.matmul(ps[0:NB, 4, 0:1], triT[0:NB, 0:NB], incl[:, NB - 1:NB], start=True, stop=True).then_inc(S("roff"), 1)

            def look(b, g, first):
                pe.wait_ge(S("ohT"), g + 1)
                pe.wait_ge(S("cg"), g + 1)
                if not first:
                    pe.wait_ge(S("selected"), g - 1)
                for k in range(GT):
                    last = nc.tensor.matmul(ps[0:ET, 5 + b, k * NB:(k + 1) * NB], ohT[:, b, k * ET:(k + 1) * ET],
                                            cg[:, b, k * NB:(k + 1) * NB], start=True, stop=True)
                last.then_inc(S("looked"), 1)
            for b in range(2):
                look(b, b, True)
            with pe.Fori(1, IG // 2) as i:
                for b in range(2):
                    look(b, i * 2 + b, False)
            after(pe, "fields")
            for n, col in enumerate((slf, dlf)):
                for c in range(TC):
                    m = n * TC + c
                    if m >= 2:
                        pe.wait_ge(S("slot_cp"), m - 1)
                    nc.tensor.transpose(ps[:, m % 2, 0:P], col[:, c * P:(c + 1) * P], ident[:]).then_inc(S("slot_tr"), 1)

            pe.wait_ge(S("basis_in"), 32)
            pe.wait_ge(S("slot_cp"), 2 * TC)
            for c in range(8):
                last = nc.tensor.matmul(ps[0:R, c, :], compT, basis[:, c * BANK:(c + 1) * BANK], start=True, stop=True)
            last.then_inc(S("W_ps"), 1)
            pe.wait_ge(S("W_in"), 16)
            pe.wait_ge(S("W_sb"), 2)
            pe.wait_ge(S("xT_in"), 16)
            after(pe, "xpad")
            wall = Wall.rearrange("p r o -> p (r o)")
            for k in range(NB):
                if k >= 2:
                    pe.wait_ge(S("y_v"), k - 1)
                    pe.wait_ge(S("y_a"), k - 1)
                for j in range(2):
                    last = nc.tensor.matmul(ps[:, 2 * (k % 2) + j, 0:R * D // 2], FT[0][:, k * P:(k + 1) * P],
                                            wall[:, j * R * D // 2:(j + 1) * R * D // 2], start=True, stop=True)
                last.then_inc(S("y_ps"), 1)
            pe.wait_ge(S("y_v"), NB)
            pe.wait_ge(S("y_a"), NB)
            after(pe, "zerob")

            def clear(bank, stop=False):
                return nc.tensor.matmul(ps[:, bank, :], zerob[:, 0:P], zerob[:], start=not stop, stop=stop)

            def warm_up(times, bank=7):
                for _ in range(times):
                    nc.tensor.matmul(ps[:, bank, :], zerob[:, 0:P], zerob[:], start=True, stop=True)

            clear(7)

            def counts(i, b, n):
                dbs = blocks_of(pe, n * 2, 0) + blocks_of(pe, n * 2 + 1, 0)
                pe.wait_ge(S("c_oh"), n + 1)
                for k in range(2 * H):
                    last = nc.tensor.matmul(ps[:, 7, bass.ds(dbs[k] * 16, R)], c_oD[:, b, k * P:(k + 1) * P],
                                            c_oT[:, b, k * R:(k + 1) * R], start=False, stop=False)
                last.then_inc(S("c_mm"), 1)
            counting_rounds(pe, counts)
            clear(7, True).then_inc(*now("cnt"))

            for k in range(4):
                clear(k)
            after(pe, "inv")

            def build(i, b):
                n, s4, _ = stage_of(i, b, 0)
                if n is not None:
                    dbs = blocks_of(pe, n, 0)
                    pe.wait_ge(S("bl_oh"), n + 1)
                    for j in range(2):
                        wait_count(pe, S("bl_acc"), n * H + 2 * j - 2 if not isinstance(n, int) or n else 0)
                        for k in (2 * j, 2 * j + 1):
                            e, at = slice(k * P, (k + 1) * P), (k % 2) * 2 * P
                            nc.tensor.matmul(ps[:, 5 + j, at:at + P], b_oS[:, b % 2, e], b_oD[:, s4, e], start=True, stop=True)
                            last = nc.tensor.matmul(ps[:, 5 + j, at + P:at + 2 * P], b_oD[:, s4, e], b_oS[:, b % 2, e], start=True, stop=True)
                        last.then_inc(S("bl_mm"), 1)
                    pe.wait_ge(S("l0_tr"), n + 1)
                    wait_count(pe, S("l0_w"), n - 1)
                    warm_up(1, (4, 7)[b % 2])
                    for k in range(H):
                        last = nc.tensor.matmul(ps[:, (4, 7)[b % 2], k * 16:k * 16 + R], l_oDT[:, b % 2, k * P:(k + 1) * P],
                                                inv[:, bass.ds(dbs[k] * 16, R)], start=True, stop=True)
                    last.then_inc(S("l0_g"), 1)
                n, s4, _ = stage_of(i, b, 2)
                if n is not None:
                    dbs = blocks_of(pe, n, 0)
                    pe.wait_ge(S("l0_ys"), n + 1)
                    for k in range(H):
                        last = nc.tensor.matmul(psN[:, bass.ds(dbs[k] * D, D)], b_oD[:, s4, k * P:(k + 1) * P],
                                                l_ys[:, s4 % 2, k, :], start=False, stop=False)
                    last.then_inc(S("l0_sc"), 1)
            half_rounds(pe, build, 2)

            def end_sums(name):
                for k in range(4):
                    last = clear(k, True)
                last.then_inc(*now(name))
            end_sums("acc0")

            def mm(name, terms, rows=D):
                for c, (at, w) in enumerate(CH):
                    for k, (lhs, rhs) in enumerate(terms):
                        last = nc.tensor.matmul(ps[0:rows, c, 0:w], lhs, rhs[:, at:at + w], start=k == 0, stop=k == len(terms) - 1)
                last.then_inc(*now(name))

            def to_T(name, src):
                for k in range(NB):
                    last = nc.tensor.transpose(psT(k), src[:, k * D:(k + 1) * D], ident[:])
                last.then_inc(*now(name))

            def psT(k):
                return ps[0:D, k // 4, (k % 4) * P:(k % 4 + 1) * P]

            def to_N(name, src):
                for k in range(NB):
                    last = nc.tensor.transpose(ps[:, k // 8, (k % 8) * D:(k % 8 + 1) * D], src[:, k * P:(k + 1) * P], ident[0:D, 0:D])
                last.then_inc(*now(name + "_ps"))

            def product(q):
                def rounds(i, first, final, exact):
                    for j in range(2 * PB):
                        pe.wait_ge(S(f"arow{j % 5}"), (i * 2 + q * 2 * PB + j // 5 + 1) * 16)
                        if j % 2 == 0:
                            pe.wait_ge(S("pr_xs"), i * PB + q * NB + j // 2 + 1)
                            if q:
                                pe.wait_ge(S("pr_xb"), i * PB + (q - 1) * NB + j // 2 + 1)
                        at, w = HALF[j % 2]
                        start, stop = first and j < 2, final and j >= 2 * PB - 2
                        if exact:
                            passes = [(2 * D, xb[:, j // 2, 0:2 * D], start, stop), (D, xb[:, j // 2, 2 * D:3 * D], False, False)]
                            passes = passes if start else passes[::-1]
                        else:
                            rows = D if q == 0 else 2 * D
                            passes = [(rows, xs[:, j // 2, 0:rows], start, stop)]
                        rows_in = arow_top if exact else arow
                        for rows, lhs, begin, end in passes:
                            for c, (c_at, c_w) in enumerate(CH):
                                if at <= c_at < at + w:
                                    last = nc.tensor.matmul(ps[0:rows, c, 0:c_w], lhs, rows_in[:, j % 5, c_at - at:c_at - at + c_w],
                                                            start=begin, stop=end)
                        last.then_inc(S("pr_mm"), 1)

                def all_rounds(exact):
                    rounds(0, True, False, exact)
                    with pe.Fori(1, NB // PB - 1) as i:
                        rounds(i, False, False, exact)
                    rounds(NB // PB - 1, False, True, exact)
                if q == 0:
                    all_rounds(0)
                    return
                many = pe.value_load(flag[0:1, 0:1], min_val=0, max_val=P)
                with pe.If(many == 0):
                    all_rounds(1)
                with pe.Else():
                    all_rounds(0)

            def ln(tag, X, o):
                after(pe, tag + "_in")
                to_N(tag, X)
                if o is not None:
                    after(pe, tag)
                    to_T(tag + "T_ps", o)

            after(pe, "acc0N")
            to_T("i0_ps", NT_[0])
            after(pe, "i0_sb")
            to_T("acc0_ps", NT_[1])
            after(pe, "acc0T")
            pe.wait_ge(S("wts_in"), 80)
            mm("root_ps", [(wt["root"], FT[0])])
            ln("ln0", FT[2], NT_[0])
            after(pe, "ln0T")
            product(0)
            after(pe, "large")
            nc.tensor.matmul(ps[0:D, 7, 0:1], ones[:, 0:D], large[:], start=True, stop=True).then_inc(*now("large_ps"))
            after(pe, "odeg_rep")
            to_T("o0_ps", NT_[1])
            after(pe, "o0_sb")
            mm("P_ps", [(wt["unite_x"], FT[0])])
            after(pe, "P_sb")
            mm("Q_ps", [(wt["unite_d"], FT[1])])
            after(pe, "Q_sb")
            mm("DT_ps", [(wt["unite_x"], FT[1])])
            after(pe, "DT_sb")
            after(pe, "PQ")
            to_N("PN", FT[2])
            after(pe, "PN")
            to_N("QN", FT[3])
            after(pe, "hsN")
            for k in range(4):
                clear(k)
            clear(7)
            for k in range(NB):
                nc.tensor.matmul(ps[0:D, 7, 0:D], NT_[2][:, k * D:(k + 1) * D], NT_[2][:, k * D:(k + 1) * D],
                                 start=False, stop=False)

            def gather_rows(n, s4):
                sls, dls = blocks_of(pe, n, 1), blocks_of(pe, n, 0)
                pe.wait_ge(S("b_tr"), n + 1)
                wait_count(pe, S("b_h"), n - 1)
                for k in range(H):
                    e = slice(k * P, (k + 1) * P)
                    o = ps[:, 4 + s4 % 2, k * D:(k + 1) * D]
                    nc.tensor.matmul(o, e_oST[:, s4 % 2, e], NT_[0][:, bass.ds(sls[k] * D, D)], start=True, stop=False)
                    last = nc.tensor.matmul(o, e_oDT[:, s4, e], NT_[1][:, bass.ds(dls[k] * D, D)], start=False, stop=True)
                last.then_inc(S("b_z"), 1)

            def sums(p, n, s4, h, ready, which):
                blks = blocks_of(pe, n, which)
                pe.wait_ge(S(ready), n + 1)
                pe.wait_ge(S(p + "_o"), n + 1)
                for k in range(H):
                    hk = h[:, s4 % h.shape[1], k * D:(k + 1) * D]
                    last = nc.tensor.matmul(psN[:, bass.ds(blks[k] * D, D)], e_o[:, s4, k * P:(k + 1) * P], hk, start=False, stop=False)
                    if p == "b" and k % 2:
                        two = h[:, s4, (k - 1) * D:(k + 1) * D]
                        last = nc.tensor.matmul(ps[:, 7, 0:2 * D], two, two, start=False, stop=False)
                last.then_inc(S(p + "_sc"), 1)

            def round_b(i, b):
                n, s4, _ = stage_of(i, b, 2)
                if n is not None:
                    sums("b", n, s4, e_h, "b_h", 0)
                n, s4, _ = stage_of(i, b, 0)
                if n is not None:
                    gather_rows(n, s4)
            half_rounds(pe, round_b, 2)
            clear(7, True)
            end_sums("accb")
            after(pe, "s")
            to_T("s_ps", NT_[2])
            after(pe, "sT")
            product(1)
            after(pe, "msg")
            mm("R_ps", [(wt["gconv_m"], FT[1])])
            after(pe, "R_sb")
            mm("sW_ps", [(wt["gconv_h"], FT[5])])
            after(pe, "gram_sb")
            nc.tensor.matmul(ps[0:D, 7, 0:D], gram_sb, wt["gconv_h"], start=True, stop=True).then_inc(*now("GW_ps"))
            after(pe, "GW_sb")
            nc.tensor.matmul(ps[0:D, 7, 0:1], gw_sb, ones[0:D, 0:1], start=True, stop=True).then_inc(*now("Mc_ps"))
            after(pe, "diag2")
            nc.tensor.matmul(ps[0:D, 7, 0:D], wt["gconv_hT"], diag2, start=True, stop=True).then_inc(*now("wc2_ps"))
            after(pe, "RT")
            to_N("RN", FT[2])
            after(pe, "RN")
            after(pe, "wc2")
            mm("h2_ps", [(wc2, FT[4])])
            after(pe, "h2")
            warm_up(16)
            for k in range(4):
                clear(k)

            def round_d(i, b):
                n, s4, _ = stage_of(i, b, 2)
                if n is not None:
                    sums("d", n, s4, e_h2, "d_h2", 1)
                n, s4, _ = stage_of(i, b, 1)
                m, m4, mi = stage_of(i, b, 0)
                dls = None if n is None else blocks_of(pe, n, 0)
                if m is not None:
                    pe.wait_ge(S(f"d_in{m4}"), (mi + 1) * 16)
                    wait_count(pe, S("d_hT"), m - 1)
                if n is not None:
                    pe.wait_ge(S("d_tr"), n + 1)
                    pe.wait_ge(S("d_hT"), n + 1)
                    wait_count(pe, S("d_h2"), n - 1)
                    warm_up(10 if isinstance(n, int) else 2, (4, 7)[s4 % 2])
                    for k in range(H):
                        e = slice(k * P, (k + 1) * P)
                        o = ps[:, (4, 7)[s4 % 2], k * D:(k + 1) * D]
                        if k % 2 == 0:
                            nc.tensor.matmul(ps[:, (4, 7)[s4 % 2], k * D:(k + 2) * D], e_hT[:, s4 % 2, k // 2 * P:(k // 2 + 1) * P], wc2s[:],
                                             start=True, stop=False)
                        last = nc.tensor.matmul(o, e_oDT[:, s4, e], NT_[2][:, bass.ds(dls[k] * D, D)], start=False, stop=k % 2 == 1)
                    last.then_inc(S("d_u"), 1)
                if m is not None:
                    for k in range(H // 2):
                        last = nc.tensor.transpose(ps[:, 5 + m4 % 2, k * P:(k + 1) * P], e_h[:, m4, 2 * k * D:2 * (k + 1) * D], ident[:])
                    last.then_inc(S("d_T"), 1)
            half_rounds(pe, round_d, 2)
            end_sums("accd")
            after(pe, "accdN")
            to_T("accd_ps", NT_[2])
            after(pe, "agg")
            mm("t_ps", [(wt["transfer_h"], FT[4]), (wt["transfer_a"], FT[5])])
            after(pe, "bnt")
            mm("lin_ps", [(wt["lin"], FT[2])])
            ln("ln1", FT[5], NT_[0])
            after(pe, "norm_rep")
            to_T("norm_ps", NT_[1])
            for k, (q, w) in enumerate(((2, "1"), (4, "2"))):
                after(pe, f"bnh{k}")
                to_N(f"hN{k}", FT[2])
                after(pe, f"hN{k}")
                product(q)
                after(pe, f"agg{q}")
                product(q + 1)
                after(pe, f"agg{q + 1}")
                mm(f"y{k + 1}_ps", [(wt[f"W{w}_out"], FT[3]), (wt[f"W{w}_back"], FT[4])])
            ln("ln2", FT[5], NT_[0])
            after(pe, "ln2T")
            product(6)
            after(pe, "m3")
            mm("h128_ps", [(w1T[:], FT[1])], 2 * D)
            after(pe, "h128")
            mm("up_ps", [(w2T[:], h128)])
            ln("ln3", FT[5], None)


def kernel(**inputs):
    import numpy as np
    import concourse.bacc as bacc
    from concourse.bass_utils import run_bass_kernel_spmd

    a = {k: np.asarray(v) for k, v in inputs.items()}
    arrays = {
        "xT": np.ascontiguousarray(a["x"].T),
        "src_c": np.ascontiguousarray(a["src"].reshape(IT, ET).T),
        "dst_c": np.ascontiguousarray(a["dst"].reshape(IT, ET).T),
        "typ_c": np.ascontiguousarray(a["edge_type_12"].reshape(IT, ET).T),
    }
    g = a["L1_gnn_W_gconv"]
    weights = [a["L0_gnn_root"], a["L1_gnn_W_unite"][:D], a["L1_gnn_W_unite"][D:], g[:D], g[D:],
               a["L1_gnn_W_transfer"][:D], a["L1_gnn_W_transfer"][D:], a["L1_gnn_W_lin"], a["L2_gnn_W1_out"],
               a["L2_gnn_W1_back"], a["L2_gnn_W2_out"], a["L2_gnn_W2_back"], g[:D].T]
    arrays.update({
        "weights": np.ascontiguousarray(np.stack(weights, 1)),
        "params": np.ascontiguousarray(np.stack([a[n] for n in PARAMS], 1)),
        "w1T": np.ascontiguousarray(a["L3_gnn_w1"].T), "w2T": np.ascontiguousarray(a["L3_gnn_w2"].T),
        "b1": a["L3_gnn_b1"].reshape(2 * D, 1), "compT": np.ascontiguousarray(a["L0_gnn_comp"].T),
        "basis": a["L0_gnn_basis"].reshape(BASES, D * D), "normt": a["node_vec1"].reshape(1, N),
    })
    nc = bacc.Bacc("TRN2", target_bir_lowering=False, num_devices=1)
    handles = {n: nc.dram_tensor("in_" + n, v.shape, mybir.dt.from_np(v.dtype), kind="ExternalInput").ap()
               for n, v in arrays.items()}
    out = nc.dram_tensor("out", (N, D), f32, kind="ExternalOutput").ap()
    build(nc, handles, out)
    r = run_bass_kernel_spmd(nc, [{"in_" + n: v for n, v in arrays.items()}], core_ids=[0])
    return r.results[0]["out"]
```
